# Optimizing a Trainium2 kernel written in Bass

```python
import numpy as np
import jax
import jax.numpy as jnp

def _softmax(x, axis=-1):
    return jax.nn.softmax(x, axis=axis)

def _gelu(x):
    return jax.nn.gelu(x, approximate=True)

def _silu(x):
    return jax.nn.silu(x)

def _sigmoid(x):
    return jax.nn.sigmoid(x)

def _layernorm(x, axis=-1, eps=1e-05):
    m = jnp.mean(x, axis=axis, keepdims=True)
    v = jnp.var(x, axis=axis, keepdims=True)
    return (x - m) / jnp.sqrt(v + eps)

def _scatter_add(tgt, idx, src, axis=0):
    return tgt.at[idx].add(src)

def _segment_sum(src, seg, n):
    return jax.ops.segment_sum(src, seg, n)
kernel_name = 'mk_xattn_ffn_d2_seqx_r4_843b65'

def setup_inputs(seed: int=0):
    np.random.seed(seed)
    _w = jnp.asarray

    def _rec_inputs():
        import jax
        import jax.numpy as jnp
        _rk = jax.random.key(seed)
        x = 7.22e-05 + 1 * jax.random.normal(jax.random.fold_in(_rk, 1), (2, 512, 256), jnp.float32)
        _lenS = 512 - jax.random.randint(jax.random.fold_in(_rk, 7), (2,), 0, max(1, 512 // 4) + 1, jnp.int32)
        _lenS2 = 1024 - jax.random.randint(jax.random.fold_in(_rk, 8), (2,), 0, max(1, 1024 // 4) + 1, jnp.int32)
        _ctx_1024P = jax.random.normal(jax.random.fold_in(_rk, 11), (2, 16, 256), jnp.float32)
        _ctx_1024c = jax.random.dirichlet(jax.random.fold_in(_rk, 511), 0.3 * jnp.ones((16,), jnp.float32), (2, 1024))
        _ctx_1024t = jnp.einsum('bsk,bkd->bsd', _ctx_1024c, _ctx_1024P)
        _ctx_1024t = _ctx_1024t * jax.lax.rsqrt(jnp.mean(jnp.square(_ctx_1024t)) + 1e-12) * 0.953939
        ctx_1024 = 4.13588e-05 + 0.999923 * (_ctx_1024t + 0.3 * jax.random.normal(jax.random.fold_in(_rk, 611), (2, 1024, 256), jnp.float32))
        fside_Bx16xSxS2_0 = 9.80324e-06 + 0.100009 * jax.random.normal(jax.random.fold_in(_rk, 13), (2, 16, 512, 1024), jnp.float32)
        fside_SxS2_0 = -2.64403e-05 + 0.100002 * jax.random.normal(jax.random.fold_in(_rk, 15), (512, 1024), jnp.float32)
        _validS = jnp.arange(512)[None, :] < _lenS[:, None]
        _validS2 = jnp.arange(1024)[None, :] < _lenS2[:, None]
        _causal = jnp.tril(jnp.ones((512, 512), dtype=bool))
        mask_1x1xSxS2_bk1 = jnp.broadcast_to(_validS2[0:1, None, None, :], (1, 1, 512, 1024))
        mask_BxS2_bf0 = jnp.logical_not(jnp.ones((2, 1024), dtype=bool))
        return (x, ctx_1024, fside_Bx16xSxS2_0, fside_SxS2_0, mask_1x1xSxS2_bk1, mask_BxS2_bf0)
    x, ctx_1024, fside_Bx16xSxS2_0, fside_SxS2_0, mask_1x1xSxS2_bk1, mask_BxS2_bf0 = _rec_inputs()

    def _L0_xattn_setup():
        import jax, jax.numpy as jnp
        import numpy as np
        D_MODEL = 256
        NUM_HEADS = 16
        D_K = D_MODEL // NUM_HEADS
        B, S = (4, 512)
        key = jax.random.key(seed)
        ks = jax.random.split(key, 12)
        sd = 1.0 / np.sqrt(D_MODEL)
        inp = {'query': jax.random.normal(ks[0], (B, S, D_MODEL), jnp.float32), 'key': jax.random.normal(ks[1], (B, S, D_MODEL), jnp.float32), 'value': jax.random.normal(ks[2], (B, S, D_MODEL), jnp.float32), 'mask': jnp.triu(jnp.ones((S, S), jnp.bool_), k=1)[None, None], 'Wq': jax.random.normal(ks[3], (D_MODEL, D_MODEL), jnp.float32) * sd, 'bq': jnp.zeros((D_MODEL,), jnp.float32), 'Wk': jax.random.normal(ks[4], (D_MODEL, D_MODEL), jnp.float32) * sd, 'bk': jnp.zeros((D_MODEL,), jnp.float32), 'Wv': jax.random.normal(ks[5], (D_MODEL, D_MODEL), jnp.float32) * sd, 'bv': jnp.zeros((D_MODEL,), jnp.float32), 'Wo': jax.random.normal(ks[6], (D_MODEL, D_MODEL), jnp.float32) * sd, 'bo': jnp.zeros((D_MODEL,), jnp.float32)}
        return inp
    _L0_xattn_all = _L0_xattn_setup()
    _L0_xattn_in = {k: v for k, v in _L0_xattn_all.items() if k in ('Wq', 'bq', 'Wk', 'bk', 'Wv', 'bv', 'Wo', 'bo')}
    del _L0_xattn_all

    def _L0_ffn_setup():
        import jax, jax.numpy as jnp
        import numpy as np
        B, L, M = (4, 512, 256)
        G, E = (8, 8)
        CAP_FACTOR = 2.0

        def _ffn_size(m, widening=8.0):
            f = int(widening * m) * 2 // 3
            return f + (8 - f) % 8
        H = _ffn_size(M)

        def _gating_top2(logits, C):
            Gd, Sd, Ed = logits.shape
            raw = jax.nn.softmax(logits, axis=-1)
            idx1 = jnp.argmax(raw, axis=-1)
            m1 = jax.nn.one_hot(idx1, Ed, dtype=logits.dtype)
            gate1 = jnp.sum(raw * m1, axis=-1)
            rest = raw * (1.0 - m1)
            idx2 = jnp.argmax(rest, axis=-1)
            m2 = jax.nn.one_hot(idx2, Ed, dtype=logits.dtype)
            gate2 = jnp.sum(rest * m2, axis=-1)
            p1 = jnp.cumsum(m1, axis=-2) - m1
            m1 = m1 * (p1 < C).astype(m1.dtype)
            p1 = jnp.sum(p1 * m1, axis=-1)
            m1_flat = jnp.sum(m1, axis=-1)
            m1_count = jnp.sum(m1, axis=-2)
            p2 = jnp.cumsum(m2, axis=-2) - m2 + m1_count[:, None, :]
            m2 = m2 * (p2 < C).astype(m2.dtype)
            p2 = jnp.sum(p2 * m2, axis=-1)
            m2_flat = jnp.sum(m2, axis=-1)
            gate1 = gate1 * m1_flat
            gate2 = gate2 * m2_flat
            c1 = (gate1[..., None] * jax.nn.one_hot(idx1, Ed, dtype=jnp.float32))[..., None] * jax.nn.one_hot(p1.astype(jnp.int32), C, dtype=jnp.float32)[:, :, None, :]
            c2 = (gate2[..., None] * jax.nn.one_hot(idx2, Ed, dtype=jnp.float32))[..., None] * jax.nn.one_hot(p2.astype(jnp.int32), C, dtype=jnp.float32)[:, :, None, :]
            combine = (c1 + c2).astype(logits.dtype)
            dispatch = (combine != 0).astype(logits.dtype)
            return (dispatch, combine)
        key = jax.random.key(seed)
        k0, k1, k2, k3, k4 = jax.random.split(key, 5)
        return {'inputs': jax.random.normal(k0, (B, L, M), jnp.float32), 'router_w': jax.random.normal(k1, (M, E), jnp.float32) * 0.02, 'w0_kernel': jax.random.normal(k2, (E, M, H), jnp.float32) * 0.02, 'w1_kernel': jax.random.normal(k3, (E, M, H), jnp.float32) * 0.02, 'wo_kernel': jax.random.normal(k4, (E, H, M), jnp.float32) * 0.02}
    _L0_ffn_all = _L0_ffn_setup()
    _L0_ffn_in = {k: v for k, v in _L0_ffn_all.items() if k in ('router_w', 'w0_kernel', 'w1_kernel', 'wo_kernel')}
    del _L0_ffn_all

    def _L1_xattn_setup():
        import jax, jax.numpy as jnp
        import numpy as np
        E = 256
        H = 16
        D = E // H
        key = jax.random.key(seed)
        ks = jax.random.split(key, 12)
        B, T, S = (2, 512, 512)
        inp = {'query': jax.random.normal(ks[0], (B, T, E), jnp.float32), 'key': jax.random.normal(ks[1], (B, S, E), jnp.float32), 'value': jax.random.normal(ks[2], (B, S, E), jnp.float32), 'spatial_bias': jax.random.normal(ks[3], (B, H, T, S), jnp.float32) * 0.1, 'directional_bias': jax.random.normal(ks[4], (B, H, T, S), jnp.float32) * 0.1, 'key_padding_mask': jnp.zeros((B, S), dtype=bool), 'attn_mask': jax.random.normal(ks[5], (T, S), jnp.float32) * 0.1, 'Wq': jax.random.normal(ks[6], (E, E), jnp.float32) / np.sqrt(E), 'bq': jnp.zeros((E,), jnp.float32), 'Wk': jax.random.normal(ks[7], (E, E), jnp.float32) / np.sqrt(E), 'bk': jnp.zeros((E,), jnp.float32), 'Wv': jax.random.normal(ks[8], (E, E), jnp.float32) / np.sqrt(E), 'bv': jnp.zeros((E,), jnp.float32), 'Wo': jax.random.normal(ks[9], (E, E), jnp.float32) / np.sqrt(E), 'bo': jnp.zeros((E,), jnp.float32)}
        return inp
    _L1_xattn_all = _L1_xattn_setup()
    _L1_xattn_in = {k: v for k, v in _L1_xattn_all.items() if k in ('Wq', 'bq', 'Wk', 'bk', 'Wv', 'bv', 'Wo', 'bo')}
    del _L1_xattn_all

    def _L1_ffn_setup():
        import jax, jax.numpy as jnp
        import numpy as np
        E, K = (8, 2)
        key = jax.random.key(seed)
        ks = jax.random.split(key, 5)
        B, S, H, I = (2, 256, 256, 1024)
        scale_h = 1.0 / np.sqrt(H)
        scale_i = 1.0 / np.sqrt(I)
        return {'hidden_states': jax.random.normal(ks[0], (B, S, H), jnp.float32), 'conf_w': jax.random.normal(ks[1], (E, H), jnp.float32) * 0.1 * scale_h, 'conf_b': jnp.zeros((E,), jnp.float32), 'gate_w': jax.random.normal(ks[2], (E, I, H), jnp.float32) * scale_h, 'up_w': jax.random.normal(ks[3], (E, I, H), jnp.float32) * scale_h, 'down_w': jax.random.normal(ks[4], (E, H, I), jnp.float32) * scale_i, 'wealth': jnp.ones((E,), jnp.float32)}
    _L1_ffn_all = _L1_ffn_setup()
    _L1_ffn_in = {k: v for k, v in _L1_ffn_all.items() if k in ('conf_w', 'conf_b', 'gate_w', 'up_w', 'down_w', 'wealth')}
    del _L1_ffn_all
    return {'x': x, 'ctx_1024': ctx_1024, 'fside_Bx16xSxS2_0': fside_Bx16xSxS2_0, 'fside_SxS2_0': fside_SxS2_0, 'mask_1x1xSxS2_bk1': mask_1x1xSxS2_bk1, 'mask_BxS2_bf0': mask_BxS2_bf0, 'L0_xattn_Wq': _L0_xattn_in['Wq'], 'L0_xattn_bq': _L0_xattn_in['bq'], 'L0_xattn_Wk': _L0_xattn_in['Wk'], 'L0_xattn_bk': _L0_xattn_in['bk'], 'L0_xattn_Wv': _L0_xattn_in['Wv'], 'L0_xattn_bv': _L0_xattn_in['bv'], 'L0_xattn_Wo': _L0_xattn_in['Wo'], 'L0_xattn_bo': _L0_xattn_in['bo'], 'L0_ffn_router_w': _L0_ffn_in['router_w'], 'L0_ffn_w0_kernel': _L0_ffn_in['w0_kernel'], 'L0_ffn_w1_kernel': _L0_ffn_in['w1_kernel'], 'L0_ffn_wo_kernel': _L0_ffn_in['wo_kernel'], 'L1_xattn_Wq': _L1_xattn_in['Wq'], 'L1_xattn_bq': _L1_xattn_in['bq'], 'L1_xattn_Wk': _L1_xattn_in['Wk'], 'L1_xattn_bk': _L1_xattn_in['bk'], 'L1_xattn_Wv': _L1_xattn_in['Wv'], 'L1_xattn_bv': _L1_xattn_in['bv'], 'L1_xattn_Wo': _L1_xattn_in['Wo'], 'L1_xattn_bo': _L1_xattn_in['bo'], 'L1_ffn_conf_w': _L1_ffn_in['conf_w'], 'L1_ffn_conf_b': _L1_ffn_in['conf_b'], 'L1_ffn_gate_w': _L1_ffn_in['gate_w'], 'L1_ffn_up_w': _L1_ffn_in['up_w'], 'L1_ffn_down_w': _L1_ffn_in['down_w'], 'L1_ffn_wealth': _L1_ffn_in['wealth']}

def reference(x, ctx_1024, fside_Bx16xSxS2_0, fside_SxS2_0, mask_1x1xSxS2_bk1, mask_BxS2_bf0, L0_xattn_Wq, L0_xattn_bq, L0_xattn_Wk, L0_xattn_bk, L0_xattn_Wv, L0_xattn_bv, L0_xattn_Wo, L0_xattn_bo, L0_ffn_router_w, L0_ffn_w0_kernel, L0_ffn_w1_kernel, L0_ffn_wo_kernel, L1_xattn_Wq, L1_xattn_bq, L1_xattn_Wk, L1_xattn_bk, L1_xattn_Wv, L1_xattn_bv, L1_xattn_Wo, L1_xattn_bo, L1_ffn_conf_w, L1_ffn_conf_b, L1_ffn_gate_w, L1_ffn_up_w, L1_ffn_down_w, L1_ffn_wealth):
    import jax
    import jax.numpy as jnp

    def _L0_xattn_ref(query, key, value, mask, Wq, bq, Wk, bk, Wv, bv, Wo, bo):
        import jax, jax.numpy as jnp
        import numpy as np
        D_MODEL = 256
        NUM_HEADS = 16
        D_K = D_MODEL // NUM_HEADS
        B, S = (4, 512)
        b = query.shape[0]
        Q = query @ Wq.T + bq
        K = key @ Wk.T + bk
        V = value @ Wv.T + bv

        def split(x):
            return x.reshape(b, -1, NUM_HEADS, D_K).transpose(0, 2, 1, 3)
        Q, K, V = (split(Q), split(K), split(V))
        scores = jnp.einsum('bhqd,bhkd->bhqk', Q, K) / jnp.sqrt(jnp.float32(D_K))
        scores = jnp.where(mask, -jnp.inf, scores)
        attn_w = jax.nn.softmax(scores, axis=-1)
        attn_w = jnp.where(jnp.isnan(attn_w), 0.0, attn_w)
        out = jnp.einsum('bhqk,bhkd->bhqd', attn_w, V)
        out = out.transpose(0, 2, 1, 3).reshape(b, -1, D_MODEL)
        return out @ Wo.T + bo

    def _L0_ffn_ref(inputs, router_w, w0_kernel, w1_kernel, wo_kernel):
        import jax, jax.numpy as jnp
        import numpy as np
        B, L, M = (4, 512, 256)
        G, E = (8, 8)
        CAP_FACTOR = 2.0

        def _ffn_size(m, widening=8.0):
            f = int(widening * m) * 2 // 3
            return f + (8 - f) % 8
        H = _ffn_size(M)

        def _gating_top2(logits, C):
            Gd, Sd, Ed = logits.shape
            raw = jax.nn.softmax(logits, axis=-1)
            idx1 = jnp.argmax(raw, axis=-1)
            m1 = jax.nn.one_hot(idx1, Ed, dtype=logits.dtype)
            gate1 = jnp.sum(raw * m1, axis=-1)
            rest = raw * (1.0 - m1)
            idx2 = jnp.argmax(rest, axis=-1)
            m2 = jax.nn.one_hot(idx2, Ed, dtype=logits.dtype)
            gate2 = jnp.sum(rest * m2, axis=-1)
            p1 = jnp.cumsum(m1, axis=-2) - m1
            m1 = m1 * (p1 < C).astype(m1.dtype)
            p1 = jnp.sum(p1 * m1, axis=-1)
            m1_flat = jnp.sum(m1, axis=-1)
            m1_count = jnp.sum(m1, axis=-2)
            p2 = jnp.cumsum(m2, axis=-2) - m2 + m1_count[:, None, :]
            m2 = m2 * (p2 < C).astype(m2.dtype)
            p2 = jnp.sum(p2 * m2, axis=-1)
            m2_flat = jnp.sum(m2, axis=-1)
            gate1 = gate1 * m1_flat
            gate2 = gate2 * m2_flat
            c1 = (gate1[..., None] * jax.nn.one_hot(idx1, Ed, dtype=jnp.float32))[..., None] * jax.nn.one_hot(p1.astype(jnp.int32), C, dtype=jnp.float32)[:, :, None, :]
            c2 = (gate2[..., None] * jax.nn.one_hot(idx2, Ed, dtype=jnp.float32))[..., None] * jax.nn.one_hot(p2.astype(jnp.int32), C, dtype=jnp.float32)[:, :, None, :]
            combine = (c1 + c2).astype(logits.dtype)
            dispatch = (combine != 0).astype(logits.dtype)
            return (dispatch, combine)
        Bb, Ll, Mm = inputs.shape
        S = Bb * Ll // G
        x = inputs.reshape(G, S, Mm)
        logits = jnp.einsum('GSM,ME->GSE', x, router_w)
        cap = int(CAP_FACTOR * S / E)
        C = (cap + 3) // 4 * 4
        dispatch, combine = _gating_top2(logits, C)
        expert_inputs = jnp.einsum('GSEC,GSM->EGCM', dispatch, x)
        layer_w0 = jnp.einsum('EGCM,EMH->EGCH', expert_inputs, w0_kernel)
        layer_w1 = jnp.einsum('EGCM,EMH->EGCH', expert_inputs, w1_kernel)
        hidden = jax.nn.gelu(layer_w0, approximate=True) * layer_w1
        expert_outputs = jnp.einsum('EGCH,EHM->EGCM', hidden, wo_kernel)
        out = jnp.einsum('EGCM,GSEC->GSM', expert_outputs, combine)
        return out.reshape(Bb, Ll, Mm)

    def _L1_xattn_ref(query, key, value, spatial_bias, directional_bias, key_padding_mask, attn_mask, Wq, bq, Wk, bk, Wv, bv, Wo, bo):
        import jax, jax.numpy as jnp
        import numpy as np
        E = 256
        H = 16
        D = E // H
        B, T, _ = query.shape
        S = key.shape[1]
        scale = D ** (-0.5)
        q = (query @ Wq.T + bq).reshape(B, T, H, D).transpose(0, 2, 1, 3)
        k = (key @ Wk.T + bk).reshape(B, S, H, D).transpose(0, 2, 1, 3)
        v = (value @ Wv.T + bv).reshape(B, S, H, D).transpose(0, 2, 1, 3)
        scores = jnp.einsum('bhtd,bhsd->bhts', q, k) * scale
        scores = scores + attn_mask[None, None, :, :]
        pad = key_padding_mask[:, None, None, :]
        scores = jnp.where(pad, -jnp.inf, scores)
        if T == S:
            scores = scores + spatial_bias + directional_bias
        probs = jax.nn.softmax(scores, axis=-1)
        out = jnp.einsum('bhts,bhsd->bhtd', probs, v)
        out = out.transpose(0, 2, 1, 3).reshape(B, T, E)
        return out @ Wo.T + bo

    def _L1_ffn_ref(hidden_states, conf_w, conf_b, gate_w, up_w, down_w, wealth):
        import jax, jax.numpy as jnp
        import numpy as np
        E, K = (8, 2)
        x = hidden_states
        confidences = jax.nn.sigmoid(jnp.einsum('bsh,eh->bse', x, conf_w) + conf_b)
        bids = confidences * wealth
        top_bids, selected_experts = jax.lax.top_k(bids, K)
        sorted_bids = -jnp.sort(-bids, axis=-1)
        payments = jnp.broadcast_to(sorted_bids[..., K:K + 1], top_bids.shape)
        routing_weights = jax.nn.softmax(top_bids, axis=-1)
        combine = jnp.sum(jax.nn.one_hot(selected_experts, E, dtype=x.dtype) * routing_weights[..., None], axis=2)

        def ffn(gw, uw, dw):
            g = jnp.einsum('bsh,ih->bsi', x, gw)
            u = jnp.einsum('bsh,ih->bsi', x, uw)
            return jnp.einsum('bsi,hi->bsh', jax.nn.silu(g) * u, dw)
        expert_out = jax.vmap(ffn)(gate_w, up_w, down_w)
        output = jnp.einsum('ebsh,bse->bsh', expert_out, combine)
        return output
    x = x + _L0_xattn_ref(_layernorm(x, axis=-1), ctx_1024, ctx_1024, mask_1x1xSxS2_bk1, L0_xattn_Wq, L0_xattn_bq, L0_xattn_Wk, L0_xattn_bk, L0_xattn_Wv, L0_xattn_bv, L0_xattn_Wo, L0_xattn_bo)
    x = x + _L0_ffn_ref(_layernorm(x, axis=-1), L0_ffn_router_w, L0_ffn_w0_kernel, L0_ffn_w1_kernel, L0_ffn_wo_kernel)
    x = x + _L1_xattn_ref(_layernorm(x, axis=-1), ctx_1024, ctx_1024, fside_Bx16xSxS2_0, fside_Bx16xSxS2_0, mask_BxS2_bf0, fside_SxS2_0, L1_xattn_Wq, L1_xattn_bq, L1_xattn_Wk, L1_xattn_bk, L1_xattn_Wv, L1_xattn_bv, L1_xattn_Wo, L1_xattn_bo)
    x = x + _L1_ffn_ref(_layernorm(x, axis=-1), L1_ffn_conf_w, L1_ffn_conf_b, L1_ffn_gate_w, L1_ffn_up_w, L1_ffn_down_w, L1_ffn_wealth)
    return x

_drawn_inputs = setup_inputs


def setup_inputs(seed=0):
    import zlib

    import numpy as np

    out = dict(_drawn_inputs(seed))
    spreads = {'L0_xattn_bq': (0.0, 0.276),
     'L0_xattn_bk': (0.0, 2.0),
     'L0_xattn_bv': (0.0, 0.1),
     'L0_xattn_bo': (0.0, 0.1),
     'L1_xattn_bq': (0.0, 0.327),
     'L1_xattn_bk': (0.0, 2.0),
     'L1_xattn_bv': (0.0, 0.1),
     'L1_xattn_bo': (0.0, 0.1),
     'L1_ffn_conf_b': (0.0, 0.1),
     'L1_ffn_wealth': (1.0, 0.2)}
    factors = {'fside_SxS2_0': 10.507,
     'L0_ffn_router_w': 2.909,
     'L0_ffn_w0_kernel': 3.822,
     'L0_ffn_w1_kernel': 4.722,
     'L0_ffn_wo_kernel': 2.828}
    for name, (base, spread) in spreads.items():
        noise = np.random.default_rng([zlib.crc32(name.encode()), seed]).standard_normal(out[name].shape)
        drawn = base * np.exp(spread * noise) if base else spread * noise
        out[name] = jnp.asarray(drawn.astype(out[name].dtype))
    for name, factor in factors.items():
        out[name] = (out[name] * factor).astype(out[name].dtype)
    return out
```

```python
from contextlib import ExitStack, contextmanager

import concourse.bass as bass
from concourse import mybir

F32 = mybir.dt.float32
BF16 = mybir.dt.bfloat16
U8 = mybir.dt.uint8
U32 = mybir.dt.uint32
I32 = mybir.dt.int32
ALU = mybir.AluOpType
ACT = mybir.ActivationFunctionType
AX = mybir.AxisListType

P = 128
B, SQ, SK, D = 2, 512, 1024, 256
NH, DH = 16, 16
TOK = B * SQ
NT = TOK // P
DT = D // P
QT = SQ // P
KT = SK // P
HG = 4
NG = NH // HG
E0, H0, CAP = 8, 1368, 32
E1, I1 = 8, 1024
TILES = 2 * TOK // P + E1 - 1
BIG = float(2.0 ** 100)
EPS = 1e-5
K_PARTS = (0, 1, 0, 2, 0, 1)
Q_PARTS = (0, 0, 1, 0, 2, 1)
STACK = 6 * DH
MROW = STACK
PADROW = STACK + 3
ROWS = STACK + 4
A_SPLIT = (5, 5, 5, 5, 5, 4, 3, 0)


class Prog:

    def __init__(self, nc, t):
        self.nc, self.t, self.sems = nc, t, []

    def sem(self, name):
        s = self.nc.alloc_semaphore(name=name)
        self.sems.append(s)
        return s

    @contextmanager
    def stage(self):
        outer, self.sems = self.sems, []
        with ExitStack() as inner:
            yield inner
        if self.sems:
            self.nc.clear_and_free_semaphores(self.sems)
            self.nc.all_engine_barrier()
        self.sems = outer

    def sb(self, ctx, name, shape, dt):
        return ctx.enter_context(self.nc.sbuf_tensor(name, shape, dt))

    def banks(self, ctx, name, n):
        return ctx.enter_context(self.nc.psum_tensor(name, [P, n, 512], F32))


def setup(pr):
    nc, t = pr.nc, pr.t
    with pr.stage() as c:
        ctxT = pr.sb(c, "ctxT", [P, DT, B * SK], F32)
        wk = pr.sb(c, "wk", [P, 2, DT, D], F32)
        wv = pr.sb(c, "wv", [P, 2, DT, D], F32)
        bk = pr.sb(c, "bk", [P, 2, DT], F32)
        bv = pr.sb(c, "bv", [P, 2, D], F32)
        full = pr.sb(c, "k_full", [P, 2, 512], F32)
        rest = pr.sb(c, "k_rest", [P, 2, 512], F32)
        parts = pr.sb(c, "k_parts", [P, 3, 2 * DT, B * SK], BF16)
        vals = pr.sb(c, "vals", [P, 2, B * KT, D], F32)
        kps = pr.banks(c, "k_ps", 4)
        vps = pr.banks(c, "v_ps", 4)
        x_in = pr.sem("x_in")
        w_in = [pr.sem(f"wkv_in{l}") for l in range(2)]
        ctx_in = [pr.sem(f"ctx_in{i}") for i in range(4)]
        id_zero, id_done, sel_zero, sel_done = pr.sem("id_zero"), pr.sem("id_done"), pr.sem("sel_zero"), pr.sem("sel_done")
        k_ready, k_full, k_hi = pr.sem("k_ready"), pr.sem("k_full_done"), pr.sem("k_hi_done")
        k_rest, k_mid, k_lo = pr.sem("k_rest_done"), pr.sem("k_mid_done"), pr.sem("k_lo_done")
        v_ready, v_done, k_out, v_out = pr.sem("v_ready"), pr.sem("v_done"), pr.sem("k_out"), pr.sem("v_out")
        CH = B * SK // 512
        NK = DT * CH
        NV = B * KT

        def tile_of(n):
            l, r = divmod(n, NK)
            return l, r // CH, r % CH

        with nc.Block() as block:

            @block.sync
            def _(sp):
                for l in range(2):
                    sp.dma_start(wk[:, l], t[f"wkT{l}"].rearrange("(t p) n -> p t n", p=P)).then_inc(w_in[l], 16)
                    sp.dma_start(bk[:, l], t[f"bk{l}"]).then_inc(w_in[l], 16)
                    if l == 0:
                        for i in range(4):
                            cols = slice(i * 512, (i + 1) * 512)
                            sp.dma_start(ctxT[:, :, cols],
                                         t["ctxT"][:, cols].rearrange("(t p) n -> p t n", p=P)).then_inc(ctx_in[i], 16)
                    sp.dma_start(wv[:, l], t[f"wvT{l}"].rearrange("(t p) n -> p t n", p=P)).then_inc(w_in[l], 16)
                    sp.dma_start(bv[:, l], t[f"bv{l}"].partition_broadcast(P)).then_inc(w_in[l], 16)
                sp.dma_start(pr.x[:], t["x"].rearrange("(t p) d -> p t d", p=P)).then_inc(x_in, 16)
                for l in range(2):
                    for dt in range(DT):
                        u = l * DT + dt
                        sp.wait_ge(k_hi, CH * (u + 1))
                        sp.wait_ge(k_mid, CH * (u + 1))
                        sp.wait_ge(k_lo, CH * (u + 1))
                        for part in range(3):
                            sp.dma_start(t["k_scr"][l, part, dt * P:(dt + 1) * P, :],
                                         parts[:, part, u]).then_inc(k_out, 16)
                    sp.wait_ge(v_done, NV * (l + 1))
                    sp.dma_start(t["v_scr"][l], vals[:, l]).then_inc(v_out, 16)
                sp.wait_ge(k_out, 16 * 3 * 2 * DT)
                sp.wait_ge(v_out, 32)
                sp.wait_ge(x_in, 16)

            @block.gpsimd
            def _(pool):
                nc.gpsimd.memset(pr.ident[:], 0.0).then_inc(id_zero, 1)
                nc.gpsimd.memset(pr.lower[:], 1.0).then_inc(id_zero, 1)
                nc.gpsimd.memset(pr.ones[:], 1.0).then_inc(id_zero, 1)
                nc.gpsimd.memset(pr.sel[:], 0.0).then_inc(sel_zero, 1)
                pool.wait_ge(id_zero, 3)
                nc.gpsimd.affine_select(out=pr.ident[:], in_=pr.ident[:], compare_op=ALU.not_equal, fill=1.0,
                                        base=0, pattern=[[-1, P]], channel_multiplier=1).then_inc(id_done, 1)
                nc.gpsimd.affine_select(out=pr.lower[:], in_=pr.lower[:], compare_op=ALU.is_gt, fill=0.0,
                                        base=0, pattern=[[1, P]], channel_multiplier=-1).then_inc(id_done, 1)
                pool.wait_ge(id_done, 2)
                nc.gpsimd.tensor_copy(pr.ident_bf[:], pr.ident[:]).then_inc(id_done, 1)
                pool.wait_ge(sel_zero, 1)
                nc.gpsimd.affine_select(out=pr.sel[:].rearrange("p (h r) -> p h r", h=HG),
                                        in_=pr.sel[:].rearrange("p (h r) -> p h r", h=HG),
                                        compare_op=ALU.not_equal, fill=1.0, base=-DH,
                                        pattern=[[-32, HG], [0, 32]], channel_multiplier=1).then_inc(sel_done, 1)
                nc.gpsimd.iota(pr.desc[:], pattern=[[-1, 8]], base=8, channel_multiplier=0,
                               allow_small_or_imprecise_dtypes=True).then_inc(sel_done, 1)
                nc.gpsimd.iota(pr.place[:], pattern=[[1, CAP]], base=0, channel_multiplier=0,
                               allow_small_or_imprecise_dtypes=True).then_inc(sel_done, 1)
                pool.wait_ge(sel_done, 3)
                pool.wait_ge(id_done, 3)

            @block.tensor
            def _(pe):
                for l in range(2):
                    pe.wait_ge(w_in[l], 64)
                    for r in range(NK):
                        n = l * NK + r
                        _, dt, ch = tile_of(n)
                        if n < CH:
                            pe.wait_ge(ctx_in[ch], 16)
                        if n >= 4:
                            pe.wait_ge(k_hi, n - 3)
                        for k in range(DT):
                            mm = pe.matmul(kps[:, n % 4], wk[:, l, k, dt * P:(dt + 1) * P],
                                           ctxT[:, k, ch * 512:(ch + 1) * 512], start=(k == 0), stop=(k == DT - 1))
                        mm.then_inc(k_ready, 1)
                    for r in range(NV):
                        n = l * NV + r
                        if n >= 4:
                            pe.wait_ge(v_done, n - 3)
                        for k in range(DT):
                            mm = pe.matmul(vps[:, n % 4, 0:D], ctxT[:, k, r * P:(r + 1) * P],
                                           wv[:, l, k], start=(k == 0), stop=(k == DT - 1))
                        mm.then_inc(v_ready, 1)

            @block.scalar
            def _(act):
                def middle(n):
                    l, dt, ch = tile_of(n)
                    act.wait_ge(k_rest, n + 1)
                    nc.scalar.activation(parts[:, 1, l * DT + dt, ch * 512:(ch + 1) * 512], rest[:, n % 2],
                                         ACT.Copy).then_inc(k_mid, 1)

                act.wait_ge(w_in[0], 64)
                act.wait_ge(w_in[1], 64)
                for n in range(2 * NK):
                    l, dt, ch = tile_of(n)
                    act.wait_ge(k_ready, n + 1)
                    if n >= 2:
                        act.wait_ge(k_rest, n - 1)
                    nc.scalar.activation(full[:, n % 2], kps[:, n % 4], ACT.Identity,
                                         bias=bk[:, l, dt:dt + 1]).then_inc(k_full, 1)
                    nc.scalar.activation(parts[:, 0, l * DT + dt, ch * 512:(ch + 1) * 512], kps[:, n % 4],
                                         ACT.Identity, bias=bk[:, l, dt:dt + 1]).then_inc(k_hi, 1)
                    if n % NK:
                        middle(n - 1)
                    if n % NK == NK - 1:
                        middle(n)

            @block.vector
            def _(dve):
                def low(n):
                    l, dt, ch = tile_of(n)
                    dve.wait_ge(k_mid, n + 1)
                    nc.vector.tensor_tensor(parts[:, 2, l * DT + dt, ch * 512:(ch + 1) * 512], rest[:, n % 2],
                                            parts[:, 1, l * DT + dt, ch * 512:(ch + 1) * 512],
                                            ALU.subtract).then_inc(k_lo, 1)

                for l in range(2):
                    for r in range(NK):
                        n = l * NK + r
                        _, dt, ch = tile_of(n)
                        dve.wait_ge(k_full, n + 1)
                        dve.wait_ge(k_hi, n + 1)
                        if n >= 2:
                            dve.wait_ge(k_lo, n - 1)
                        nc.vector.tensor_tensor(rest[:, n % 2], full[:, n % 2],
                                                parts[:, 0, l * DT + dt, ch * 512:(ch + 1) * 512],
                                                ALU.subtract).then_inc(k_rest, 1)
                        if r >= 1:
                            low(n - 1)
                    low(l * NK + NK - 1)
                    dve.wait_ge(w_in[l], 64)
                    for r in range(NV):
                        n = l * NV + r
                        dve.wait_ge(v_ready, n + 1)
                        nc.vector.tensor_tensor(vals[:, l, r], vps[:, n % 4, 0:D], bv[:, l],
                                                ALU.add).then_inc(v_done, 1)


class NormSteps:

    def __init__(self, pr, c, tag):
        self.pr, self.tag = pr, tag
        self.stats = pr.sb(c, f"{tag}_stats", [P, NT, 6], F32)
        self.mv = pr.sb(c, f"{tag}_mv", [P, NT, 2], F32)
        self.rstd = pr.sb(c, f"{tag}_rstd", [P, NT], F32)
        self.var = pr.sb(c, f"{tag}_var", [P, NT], F32)
        self.root = pr.sb(c, f"{tag}_root", [P, NT], F32)
        self.s_var, self.s_root = pr.sem(f"{tag}_var_done"), pr.sem(f"{tag}_root_done")
        self.s_stats, self.s_mv, self.s_rstd = (pr.sem(f"{tag}_{x}") for x in ("stats", "mv", "rstd"))
        self.s_y, self.s_tr, self.s_yT = (pr.sem(f"{tag}_{x}") for x in ("y", "tr", "yT"))

    def vector(self, dve):
        nc, pr = self.pr.nc, self.pr
        for i in range(NT):
            nc.vector.bn_stats(self.stats[:, i], pr.x[:, i]).then_inc(self.s_stats, 1)
        for i in range(NT):
            dve.wait_ge(self.s_stats, i + 1)
            nc.vector.bn_aggr(self.mv[:, i], self.stats[:, i]).then_inc(self.s_mv, 1)
        dve.wait_ge(self.s_root, 1)
        nc.vector.reciprocal(self.rstd[:], self.root[:]).then_inc(self.s_rstd, 1)
        dve.wait_ge(self.s_rstd, 1)
        nc.vector.tensor_tensor(self.root[:], self.rstd[:], self.rstd[:], ALU.mult).then_inc(self.s_rstd, 1)
        dve.wait_ge(self.s_rstd, 2)
        nc.vector.tensor_tensor(self.root[:], self.root[:], self.var[:], ALU.mult).then_inc(self.s_rstd, 1)
        dve.wait_ge(self.s_rstd, 3)
        nc.vector.tensor_scalar(self.root[:], self.root[:], -0.5, 1.5, ALU.mult, ALU.add).then_inc(self.s_rstd, 1)
        dve.wait_ge(self.s_rstd, 4)
        nc.vector.tensor_tensor(self.rstd[:], self.rstd[:], self.root[:], ALU.mult).then_inc(self.s_rstd, 1)
        dve.wait_ge(self.s_rstd, 5)
        for i in range(NT):
            nc.vector.tensor_scalar(pr.y[:, i], pr.x[:, i], self.mv[:, i, 0:1], self.rstd[:, i:i + 1],
                                    ALU.subtract, ALU.mult).then_inc(self.s_y, 1)

    def pool(self, pool):
        pool.wait_ge(self.s_mv, NT)
        self.pr.nc.gpsimd.tensor_scalar(self.var[:], self.mv[:, :, 1], EPS, None, ALU.add).then_inc(self.s_var, 1)

    def tensor(self, pe, ps):
        for j in range(NT // 2):
            pe.wait_ge(self.s_y, 2 * j + 2)
            if j >= 2:
                pe.wait_ge(self.s_yT, j - 1)
            for i in range(2):
                for k in range(DT):
                    mm = pe.transpose(ps[:, j % 2, (k * 2 + i) * P:(k * 2 + i + 1) * P],
                                      self.pr.y[:, 2 * j + i, k * P:(k + 1) * P], self.pr.ident[:])
            mm.then_inc(self.s_tr, 1)

    def scalar(self, act, ps):
        act.wait_ge(self.s_var, 1)
        self.pr.nc.scalar.activation(self.root[:], self.var[:], ACT.Sqrt).then_inc(self.s_root, 1)
        for j in range(NT // 2):
            act.wait_ge(self.s_tr, j + 1)
            self.pr.nc.scalar.activation(self.pr.yT[:, :, 2 * j * P:2 * (j + 1) * P],
                                         ps[:, j % 2].rearrange("p (k n) -> p k n", k=DT),
                                         ACT.Copy).then_inc(self.s_yT, 1)


def prepare_attention(pr, c, l, m):
    nc, t = pr.nc, pr.t
    with pr.stage() as c:
        norm = NormSteps(pr, c, f"an{l}")
        wq = pr.sb(c, f"wq{l}", [P, DT, D], F32)
        bq = pr.sb(c, f"bq{l}", [P, DT], F32)
        bq4 = pr.sb(c, f"bq4{l}", [P, DT], F32)
        full = pr.sb(c, f"q_full{l}", [P, 2, 512], F32)
        rest = pr.sb(c, f"q_rest{l}", [P, 2, 512], F32)
        parts = pr.sb(c, f"q_parts{l}", [P, 3, DT, TOK], BF16)
        tps = pr.banks(c, f"tr_ps{l}", 2)
        qps = pr.banks(c, f"q_ps{l}", 4)
        if l == 0:
            mrow = pr.sb(c, "mask_rows", [P, QT, SK // 4], U32)
            mcol = pr.sb(c, "mask_cols", [P, KT, SQ // 4], U32)
        else:
            add = pr.sb(c, "amask_rows", [P, QT, SK], F32)
            pad = pr.sb(c, "pad_rows", [P, B, SK // 4], U32)
            padin = pr.sb(c, "pad_in", [1, B * SK // 4], U32)
            brest = pr.sb(c, "bias_rest", [P, KT, SQ], F32)
        padbf = pr.sb(c, f"pad_bf{l}", [1, B, SK], BF16)
        w_in, m_in, v_in = pr.sem(f"wq_in{l}"), pr.sem(f"m_in{l}"), pr.sem(f"v_in{l}")
        b4, q_ready, q_full, q_hi = (pr.sem(f"{x}{l}") for x in ("bq4_", "q_ready", "q_full_", "q_hi"))
        q_rest, q_mid, q_lo, q_out = (pr.sem(f"{x}{l}") for x in ("q_rest_", "q_mid", "q_lo", "q_out"))
        s_pad, pad_out, s_mask, s_rows = (pr.sem(f"{x}{l}") for x in ("s_pad", "pad_out", "s_mask", "s_rows"))
        b_hi, b_rest, b_mid, b_lo = (pr.sem(f"{x}{l}") for x in ("b_hi", "b_rest", "b_mid", "b_lo"))
        CH = TOK // 512
        NQ = DT * CH

        with nc.Block() as block:

            @block.sync
            def _(sp):
                sp.dma_start(wq[:], t[f"wqT{l}"].rearrange("(t p) n -> p t n", p=P)).then_inc(w_in, 16)
                sp.dma_start(bq[:], t[f"bq{l}"]).then_inc(w_in, 16)
                if l == 0:
                    sp.dma_start(mrow[:], t["mask"].rearrange("(t p) k -> p t k", p=P)).then_inc(m_in, 16)
                    sp.dma_start(mcol[:], t["maskT"].rearrange("(t p) k -> p t k", p=P)).then_inc(m_in, 16)
                else:
                    sp.dma_start(add[:], t["amask"].rearrange("(t p) k -> p t k", p=P)).then_inc(m_in, 16)
                    sp.dma_start(m.bias_cols[:], t["amaskT"].rearrange("(t p) k -> p t k", p=P)).then_inc(m_in, 16)
                    sp.dma_start(padin[:], t["pad"].rearrange("b k -> (b k)").unsqueeze(0)).then_inc(m_in, 16)
                    sp.dma_start(pad[:].rearrange("p b k -> p (b k)"),
                                 t["pad"].rearrange("b k -> (b k)").partition_broadcast(P)).then_inc(m_in, 16)
                sp.dma_start(m.vals[:], t["v_scr"][l]).then_inc(v_in, 16)
                sp.wait_ge(s_pad, 1)
                for h in range(HG):
                    sp.dma_start(t["pad_scr"][l, :, h].unsqueeze(0), padbf[:]).then_inc(pad_out, 16)
                for dt in range(DT):
                    sp.wait_ge(q_hi, CH * (dt + 1))
                    sp.wait_ge(q_mid, CH * (dt + 1))
                    sp.wait_ge(q_lo, CH * (dt + 1))
                    for part in range(3):
                        sp.dma_start(t["q_scr"][l, part, dt * P:(dt + 1) * P, :], parts[:, part, dt]).then_inc(q_out, 16)
                sp.wait_ge(pad_out, 16 * HG)
                sp.wait_ge(q_out, 16 * 3 * DT)
                sp.wait_ge(v_in, 16)

            @block.gpsimd
            def _(pool):
                norm.pool(pool)
                pool.wait_ge(m_in, 32 if l == 0 else 64)
                if l == 0:
                    nc.gpsimd.memset(padbf[:], 0.0).then_inc(s_pad, 1)
                    nc.gpsimd.tensor_scalar(m.bias_hi[:], mcol[:].bitcast(U8), -BIG, None, ALU.mult).then_inc(s_mask, 1)
                    nc.gpsimd.tensor_scalar(m.bias_rows[0][:], mrow[:].bitcast(U8), -BIG, None, ALU.mult).then_inc(s_rows, 1)
                else:
                    nc.gpsimd.tensor_scalar(padbf[:].rearrange("p b k -> p (b k)"), padin[:].bitcast(U8), -BIG, None,
                                            ALU.mult).then_inc(s_pad, 1)
                    nc.gpsimd.tensor_scalar(m.bias_cols[:], m.bias_cols[:], -BIG, None, ALU.max).then_inc(s_mask, 1)
                    nc.gpsimd.tensor_scalar(add[:], add[:], -BIG, None, ALU.max).then_inc(s_rows, 1)
                pool.wait_ge(s_mask, 1)
                pool.wait_ge(s_rows, 1)

            @block.tensor
            def _(pe):
                norm.tensor(pe, tps)
                pe.wait_ge(w_in, 32)
                pe.wait_ge(norm.s_yT, NT // 2)
                for n in range(NQ):
                    dt, ch = divmod(n, CH)
                    for k in range(DT):
                        mm = pe.matmul(qps[:, n % 4], wq[:, k, dt * P:(dt + 1) * P],
                                       pr.yT[:, k, ch * 512:(ch + 1) * 512], start=(k == 0), stop=(k == DT - 1))
                    mm.then_inc(q_ready, 1)

            @block.scalar
            def _(act):
                def middle(n):
                    dt, ch = divmod(n, CH)
                    act.wait_ge(q_rest, n + 1)
                    nc.scalar.activation(parts[:, 1, dt, ch * 512:(ch + 1) * 512], rest[:, n % 2],
                                         ACT.Copy).then_inc(q_mid, 1)

                if l == 1:
                    act.wait_ge(s_mask, 1)
                    nc.scalar.activation(m.bias_hi[:], m.bias_cols[:], ACT.Copy).then_inc(b_hi, 1)
                norm.scalar(act, tps)
                act.wait_ge(w_in, 32)
                nc.scalar.activation(bq4[:], bq[:], ACT.Copy, scale=0.25).then_inc(b4, 1)
                act.wait_ge(b4, 1)
                for n in range(NQ):
                    dt, ch = divmod(n, CH)
                    act.wait_ge(q_ready, n + 1)
                    if n >= 2:
                        act.wait_ge(q_rest, n - 1)
                    nc.scalar.activation(full[:, n % 2], qps[:, n % 4], ACT.Identity, bias=bq4[:, dt:dt + 1],
                                         scale=0.25).then_inc(q_full, 1)
                    nc.scalar.activation(parts[:, 0, dt, ch * 512:(ch + 1) * 512], qps[:, n % 4], ACT.Identity,
                                         bias=bq4[:, dt:dt + 1], scale=0.25).then_inc(q_hi, 1)
                    if n >= 1:
                        middle(n - 1)
                middle(NQ - 1)
                if l == 1:
                    act.wait_ge(b_rest, 1)
                    nc.scalar.activation(m.bias_mid[:], brest[:], ACT.Copy).then_inc(b_mid, 1)

            @block.vector
            def _(dve):
                def low(n):
                    dt, ch = divmod(n, CH)
                    dve.wait_ge(q_mid, n + 1)
                    nc.vector.tensor_tensor(parts[:, 2, dt, ch * 512:(ch + 1) * 512], rest[:, n % 2],
                                            parts[:, 1, dt, ch * 512:(ch + 1) * 512], ALU.subtract).then_inc(q_lo, 1)

                norm.vector(dve)
                for n in range(NQ):
                    dt, ch = divmod(n, CH)
                    dve.wait_ge(q_full, n + 1)
                    dve.wait_ge(q_hi, n + 1)
                    if n >= 2:
                        dve.wait_ge(q_lo, n - 1)
                    nc.vector.tensor_tensor(rest[:, n % 2], full[:, n % 2],
                                            parts[:, 0, dt, ch * 512:(ch + 1) * 512], ALU.subtract).then_inc(q_rest, 1)
                    if n >= 1:
                        low(n - 1)
                low(NQ - 1)
                if l == 1:
                    dve.wait_ge(b_hi, 1)
                    nc.vector.tensor_tensor(brest[:], m.bias_cols[:], m.bias_hi[:], ALU.subtract).then_inc(b_rest, 1)
                    dve.wait_ge(s_rows, 1)
                    for b in range(B):
                        for qt in range(QT):
                            nc.vector.scalar_tensor_tensor(out=m.bias_rows[b][:, qt], in0=pad[:, b].bitcast(U8), scalar=-BIG,
                                                           in1=add[:, qt], op0=ALU.mult, op1=ALU.add).then_inc(b_lo, 1)
                    dve.wait_ge(b_mid, 1)
                    nc.vector.tensor_tensor(m.bias_lo[:], brest[:], m.bias_mid[:], ALU.subtract).then_inc(b_lo, 1)
                    dve.wait_ge(b_lo, 1 + B * QT)


class Mem:
    pass


def attend(pr, l, m):
    nc, t = pr.nc, pr.t
    with pr.stage() as c:
        K = [pr.sb(c, f"k_stack{l}{b}", [P, HG, SK], BF16) for b in range(B)]
        Q = [pr.sb(c, f"q_stack{l}{b}", [P, HG, SQ], BF16) for b in range(B)]
        V = [pr.sb(c, f"v_unit{l}{b}", [P, KT, HG, 32], F32) for b in range(B)]
        prob = pr.sb(c, f"prob{l}", [P, 2, HG, SQ], F32)
        junk = pr.sb(c, f"junk{l}", [P, 2, 512], F32)
        mx = pr.sb(c, f"mx{l}", [P, 2, HG, QT, 2], F32)
        mneg = pr.sb(c, f"mneg{l}", [P, 2, 2 * QT], F32)
        mrest = pr.sb(c, f"mrest{l}", [P, 2, 2 * QT], F32)
        mpart = pr.sb(c, f"mpart{l}", [P, 2, 2 * QT, 3], BF16)
        s_ps = pr.banks(c, f"s_ps{l}", 2)
        st_ps = pr.banks(c, f"st_ps{l}", 4)
        o_ps = pr.banks(c, f"o_ps{l}", 1)
        m_ps = c.enter_context(nc.psum_tensor(f"m_ps{l}", [P, 1024], BF16))
        init, load = pr.sem(f"init{l}"), [pr.sem(f"kq_in{l}{b}") for b in range(B)]
        s_ready, mx_done = pr.sem(f"s_ready{l}"), pr.sem(f"mx_done{l}")
        chain, mp_done, mt_done, mrow_done = (pr.sem(f"{x}{l}") for x in ("chain", "mp_done", "mt_done", "mrow_done"))
        st_ready, add_done, exp_done, pv_done = (pr.sem(f"{x}{l}") for x in ("st_ready", "add_done", "exp_done", "pv_done"))
        pool_step, dve_step = pr.sem(f"pool_step{l}"), pr.sem(f"dve_step{l}")
        evac_done, v_copied = (pr.sem(f"{x}{l}") for x in ("evac_done", "v_copied"))
        N_DMA = 13

        def on_pe(hp):
            return l == 0 or hp == 0

        def units(eng, unit):
            with eng.Fori(0, NG - 1) as i:
                for b in range(B):
                    unit(i, b, True)
            for b in range(B):
                unit(NG - 1, b, b == 0)

        def nxt(i, b):
            return i * 2 + b + 1, 1 - b

        def a_jobs(kt):
            first = sum(A_SPLIT[:kt])
            return range(first, first + A_SPLIT[kt])

        def passed(eng, step):
            eng.sem_inc(step, 1)

        with nc.Block() as block:

            @block.sync
            def _(sp):
                def stacks(i, b):
                        rows = bass.ds(i * (HG * DH), HG * DH)
                        for r in range(6):
                            sp.dma_start(K[b][r * DH:(r + 1) * DH],
                                         t["k_scr"][l, K_PARTS[r], rows, b * SK:(b + 1) * SK]
                                         .rearrange("(h d) k -> d h k", h=HG)).then_inc(load[b], 16)
                            sp.dma_start(Q[b][r * DH:(r + 1) * DH],
                                         t["q_scr"][l, Q_PARTS[r], rows, b * SQ:(b + 1) * SQ]
                                         .rearrange("(h d) k -> d h k", h=HG)).then_inc(load[b], 16)
                        sp.dma_start(K[b][PADROW:PADROW + 1], t["pad_scr"][l, b].unsqueeze(0)).then_inc(load[b], 16)

                sp.wait_ge(init, 6)
                for b in range(B):
                    stacks(0, b)
                with sp.Fori(1, NG) as i:
                    for b in range(B):
                        sp.wait_ge(st_ready, (i * 2 + b - 1) * 16)
                        stacks(i, b)

            @block.gpsimd
            def _(pool):
                pool.wait_ge(init, 6)

                def values(u, i, b):
                    pool.wait_ge(evac_done, u + 1)
                    passed(pool, pool_step)
                    nc.gpsimd.tensor_copy(V[b][:, :, :, 0:DH],
                                          m.vals[:, b * KT:(b + 1) * KT, bass.ds(i * (HG * DH), HG * DH)]
                                          .rearrange("p k (h d) -> p k h d", h=HG)).then_inc(v_copied, 1)

                def half(u, b, c2):
                    hs = slice(2 * c2, 2 * c2 + 2)
                    n = (u * 2 + c2) * 4
                    pool.wait_ge(mx_done, u * 32 + 2 + 16 * (c2 + 1))
                    pool.wait_ge(mrow_done, u * 2 + c2 + 1)
                    passed(pool, pool_step)
                    nc.gpsimd.tensor_scalar(mneg[:, c2].rearrange("p (h q) -> p h q", h=2), mx[:, b, hs, :, 1], -BIG / 2, -1.0, ALU.max, ALU.mult).then_inc(chain, 1)
                    pool.wait_ge(chain, n + 1)
                    passed(pool, pool_step)
                    nc.gpsimd.tensor_copy(mpart[:, c2, :, 0], mneg[:, c2]).then_inc(chain, 1)
                    pool.wait_ge(chain, n + 2)
                    passed(pool, pool_step)
                    nc.gpsimd.tensor_tensor(mrest[:, c2], mneg[:, c2], mpart[:, c2, :, 0], ALU.subtract).then_inc(chain, 1)
                    pool.wait_ge(chain, n + 3)
                    passed(pool, pool_step)
                    nc.gpsimd.tensor_copy(mpart[:, c2, :, 1], mrest[:, c2]).then_inc(chain, 1)
                    pool.wait_ge(chain, n + 4)
                    passed(pool, pool_step)
                    nc.gpsimd.tensor_tensor(mpart[:, c2, :, 2], mrest[:, c2], mpart[:, c2, :, 1],
                                            ALU.subtract).then_inc(mp_done, 1)

                values(0, 0, 0)
                half(0, 0, 0)
                half(0, 0, 1)

                def unit(i, b, has_next):
                    if has_next:
                        u, nb = nxt(i, b)
                        values(u, i + b, nb)
                        half(u, nb, 0)
                        half(u, nb, 1)

                units(pool, unit)

            @block.tensor
            def _(pe):
                pe.sem_inc(pv_done, 2)

                def row_scores(u, b, jobs):
                    for j in jobs:
                        h, half, qt = j // 8, j % 8 // 4, j % 4
                        pe.wait_ge(mx_done, u * 32 + j + 1)
                        pe.matmul(s_ps[:, j % 2], Q[b][0:STACK, h, qt * P:(qt + 1) * P],
                                  K[b][0:STACK, h, half * 512:(half + 1) * 512], start=True, stop=True).then_inc(s_ready, 1)

                def turn_max(u, b, c2):
                    pe.wait_ge(mp_done, u * 2 + c2 + 1)
                    pe.wait_ge(mrow_done, u * 2 + c2 + 2)
                    for k in range(2 * QT):
                        mm = pe.transpose(m_ps[MROW:MROW + 3, k * P:(k + 1) * P], mpart[:, c2, k], pr.ident_bf[:])
                    mm.then_inc(mt_done, 1)

                def col_scores(u, b, kt, hp):
                    n = u * 16 + kt * 2 + hp
                    slot = hp
                    pe.wait_ge(exp_done, n + 1)
                    for e in range(2):
                        h = 2 * hp + e
                        mm = pe.matmul(st_ps[:, 2 * slot + e], K[b][0:ROWS, h, kt * P:(kt + 1) * P], Q[b][0:ROWS, h],
                                       start=True, stop=not on_pe(hp))
                        if on_pe(hp):
                            layers = [m.bias_hi] if l == 0 else [m.bias_hi, m.bias_mid, m.bias_lo]
                            for x in layers:
                                mm = pe.matmul(st_ps[:, 2 * slot + e], pr.ident_bf[:], x[:, kt], start=False,
                                               stop=(x is layers[-1]))
                    mm.then_inc(st_ready, 1)

                def weigh(u, b, kt):
                    pe.wait_ge(exp_done, u * 16 + 2 * kt + 4)
                    if kt == 0:
                        pe.wait_ge(evac_done, u + 2)
                        pe.wait_ge(v_copied, u + 1)
                    for h in range(HG):
                        mm = pe.matmul(o_ps[32 * h:32 * h + 32, 0], V[b][:, kt, h], prob[:, kt % 2, h],
                                       start=(kt == 0), stop=(kt == KT - 1))
                    mm.then_inc(pv_done, 1)

                pe.wait_ge(init, 6)
                pe.wait_ge(load[0], 16 * N_DMA)
                row_scores(0, 0, range(16))
                row_scores(0, 0, range(16, 32))
                turn_max(0, 0, 0)
                turn_max(0, 0, 1)

                def unit(i, b, has_next):
                    u = i * 2 + b
                    un, nb = nxt(i, b)
                    if has_next:
                        pe.wait_ge(load[nb], (i + b) * (16 * N_DMA) + 16 * N_DMA)
                    for kt in range(KT):
                        jobs = list(a_jobs(kt)) if has_next else []
                        if kt == 0:
                            pe.wait_ge(mrow_done, u * 2 + 3)
                        row_scores(un, nb, jobs[:len(jobs) // 2])
                        col_scores(u, b, kt, 0)
                        row_scores(un, nb, jobs[len(jobs) // 2:])
                        if kt == 0:
                            pe.wait_ge(mrow_done, u * 2 + 4)
                        col_scores(u, b, kt, 1)
                        if kt >= 1:
                            weigh(u, b, kt - 1)
                        if kt == 5 and has_next:
                            turn_max(un, nb, 0)
                    if has_next:
                        turn_max(un, nb, 1)
                    weigh(u, b, KT - 1)

                units(pe, unit)

            @block.scalar
            def _(act):
                nc.scalar.activation(prob[:, 0, 0, 0:8], pr.ones[:, 0:8], ACT.Copy).then_inc(exp_done, 2)
                nc.scalar.activation(prob[:, 0, 0, 8:16], pr.ones[:, 0:8], ACT.Copy).then_inc(evac_done, 2)
                nc.scalar.activation(prob[:, 0, 0, 16:24], pr.ones[:, 0:8], ACT.Copy).then_inc(mrow_done, 2)

                def max_row(u, b, c2):
                    act.wait_ge(mt_done, u * 2 + c2 + 1)
                    nc.scalar.activation(Q[b][MROW:MROW + 3, 2 * c2:2 * c2 + 2].rearrange("p h q -> p (h q)"),
                                         m_ps[MROW:MROW + 3, :], ACT.Copy).then_inc(mrow_done, 1)

                act.wait_ge(init, 6)
                max_row(0, 0, 0)
                max_row(0, 0, 1)

                def unit(i, b, has_next):
                    u = i * 2 + b
                    un, nb = nxt(i, b)
                    for kt in range(KT):
                        for hp in range(2):
                            if hp == 0:
                                act.wait_ge(pv_done, u * 8 + kt + 1)
                            if on_pe(hp):
                                act.wait_ge(st_ready, u * 16 + kt * 2 + hp + 1)
                            else:
                                act.wait_ge(add_done, u * 8 + kt + 1)
                            nc.scalar.activation(prob[:, kt % 2, 2 * hp:2 * hp + 2], st_ps[:, 2 * hp:2 * hp + 2],
                                                 ACT.Exp).then_inc(exp_done, 1)
                        if kt == 5 and has_next:
                            max_row(un, nb, 0)
                    if has_next:
                        max_row(un, nb, 1)
                    act.wait_ge(pv_done, u * 8 + KT + 2)
                    nc.scalar.activation(m.out[:, bass.ds(i, 1), b], o_ps[:, 0], ACT.Copy).then_inc(evac_done, 1)

                units(act, unit)

            @block.vector
            def _(dve):
                for b in range(B):
                    nc.vector.memset(K[b][MROW:ROWS], 1.0).then_inc(init, 1)
                    nc.vector.memset(Q[b][MROW:ROWS], 1.0).then_inc(init, 1)
                    nc.vector.memset(V[b][:], 1.0).then_inc(init, 1)
                nc.vector.memset(mx[:], 0.0).then_inc(mx_done, 2)

                def row_max(u, b, jobs):
                    for j in jobs:
                        h, half, qt = j // 8, j % 8 // 4, j % 4
                        dve.wait_ge(s_ready, u * 32 + j + 1)
                        rows = m.bias_rows[b if l == 1 else 0]
                        first = -4 * BIG
                        if half:
                            dve.wait_ge(mx_done, u * 32 + j + 1 - 4 + 2)
                            first = mx[:, b, h, qt, 0:1]
                        passed(dve, dve_step)
                        nc.vector.tensor_tensor_reduce(out=junk[:, j % 2], in0=s_ps[:, j % 2],
                                                       in1=rows[:, qt, half * 512:(half + 1) * 512],
                                                       scale=1.0, scalar=first, op0=ALU.add, op1=ALU.max,
                                                       accum_out=mx[:, b, h, qt, half:half + 1]).then_inc(mx_done, 1)

                row_max(0, 0, range(32))

                def unit(i, b, has_next):
                    u = i * 2 + b
                    un, nb = nxt(i, b)
                    for kt in range(KT):
                        if has_next:
                            row_max(un, nb, a_jobs(kt))
                        if not on_pe(1):
                            dve.wait_ge(st_ready, u * 16 + kt * 2 + 2)
                            nc.vector.tensor_tensor(st_ps[:, 2:4], st_ps[:, 2:4],
                                                    m.bias_cols[:, kt].unsqueeze(1).broadcast_to([P, 2, SQ]),
                                                    ALU.add).then_inc(add_done, 1)

                units(dve, unit)


def project(pr, l, m):
    nc, t = pr.nc, pr.t
    with pr.stage() as c:
        wo = pr.sb(c, f"wo{l}", [P, NG, D], F32)
        bo = pr.sb(c, f"bo{l}", [P, D], F32)
        sums = pr.sb(c, f"sums{l}", [P, 2, SQ], F32)
        rec = pr.sb(c, f"rec{l}", [P, 2, SQ], F32)
        b_ps = pr.banks(c, f"b_ps{l}", 2)
        y_ps = pr.banks(c, f"y_ps{l}", 4)
        w_zero, w_in, b_in, x_bias = (pr.sem(f"{x}{l}") for x in ("wo_zero", "wo_in", "bo_in", "x_bias"))
        sum_ready, sum_used, rec_done, out_done = (pr.sem(f"{x}{l}") for x in ("sum_ready", "sum_used", "rec_done", "out_done"))
        rec_clamp = pr.sem(f"rec_clamp{l}")
        y_ready, x_done = (pr.sem(f"{x}{l}") for x in ("y_ready", "x_done"))
        order = [(b, g) for b in range(B) for g in range(NG)]

        with nc.Block() as block:

            @block.sync
            def _(sp):
                sp.dma_start(bo[:], t[f"bo{l}"].partition_broadcast(P)).then_inc(b_in, 16)
                sp.wait_ge(w_zero, 1)
                for h in range(HG):
                    sp.dma_start(wo[32 * h:32 * h + DH], t[f"woT{l}"].rearrange("(g h d) n -> h d g n", g=NG, h=HG)[h]
                                 ).then_inc(w_in, 16)

            @block.gpsimd
            def _(pool):
                nc.gpsimd.memset(wo[:], 0.0).then_inc(w_zero, 1)
                pool.wait_ge(b_in, 16)
                nc.gpsimd.tensor_tensor(pr.x[:], pr.x[:], bo[:].unsqueeze(1).broadcast_to([P, NT, D]),
                                        ALU.add).then_inc(x_bias, 1)

            @block.tensor
            def _(pe):
                def token_tile(i):
                    b, q = divmod(i, QT)
                    if i >= 4:
                        pe.wait_ge(x_done, i - 3)
                    for g in range(NG):
                        mm = pe.matmul(y_ps[:, i % 4, 0:D], m.out[:, g, b, q * P:(q + 1) * P], wo[:, g],
                                       start=(g == 0), stop=(g == NG - 1))
                    mm.then_inc(y_ready, 1)

                for k, (b, g) in enumerate(order):
                    if k >= 2:
                        pe.wait_ge(sum_used, k - 1)
                    pe.matmul(b_ps[:, k % 2], pr.sel[:], m.out[:, g, b], start=True, stop=True).then_inc(sum_ready, 1)
                pe.wait_ge(w_in, 64)
                for i in range(NT):
                    if i % QT == 0:
                        pe.wait_ge(out_done, NG * (i // QT + 1))
                    token_tile(i)

            @block.scalar
            def _(act):
                for k in range(len(order)):
                    act.wait_ge(sum_ready, k + 1)
                    if k >= 2:
                        act.wait_ge(rec_done, k - 1)
                    nc.scalar.activation(sums[:, k % 2], b_ps[:, k % 2], ACT.Copy).then_inc(sum_used, 1)

            @block.vector
            def _(dve):
                for k, (b, g) in enumerate(order):
                    dve.wait_ge(sum_used, k + 1)
                    if l == 0:
                        nc.vector.tensor_scalar(sums[:, k % 2], sums[:, k % 2], 1e-30, None, ALU.max).then_inc(rec_clamp, 1)
                        dve.wait_ge(rec_clamp, k + 1)
                    if k >= 2:
                        dve.wait_ge(out_done, k - 1)
                    nc.vector.reciprocal(rec[:, k % 2], sums[:, k % 2]).then_inc(rec_done, 1)
                    dve.wait_ge(rec_done, k + 1)
                    nc.vector.tensor_tensor(m.out[:, g, b], m.out[:, g, b], rec[:, k % 2], ALU.mult).then_inc(out_done, 1)
                dve.wait_ge(x_bias, 1)
                for i in range(NT):
                    dve.wait_ge(y_ready, i + 1)
                    nc.vector.tensor_tensor(pr.x[:, i], pr.x[:, i], y_ps[:, i % 4, 0:D], ALU.add).then_inc(x_done, 1)
                dve.wait_ge(x_done, NT)


def attention_layer(pr, l):
    with pr.stage() as c:
        m = Mem()
        m.vals = pr.sb(c, f"vals_all{l}", [P, B * KT, D], F32)
        m.out = pr.sb(c, f"o_all{l}", [P, NG, B, SQ], F32)
        m.bias_rows = [pr.sb(c, f"bias_rows{l}{b}", [P, QT, SK], F32) for b in range(1 + l)]
        m.bias_hi = pr.sb(c, f"bias_hi{l}", [P, KT, SQ], BF16)
        if l == 1:
            m.bias_mid = pr.sb(c, "bias_mid", [P, KT, SQ], BF16)
            m.bias_lo = pr.sb(c, "bias_lo", [P, KT, SQ], BF16)
            m.bias_cols = pr.sb(c, "bias_cols", [P, KT, SQ], F32)
        prepare_attention(pr, c, l, m)
        attend(pr, l, m)
        project(pr, l, m)


def moe_capacity(pr):
    nc, t = pr.nc, pr.t
    HJ = [(j * P, min(P, H0 - j * P)) for j in range((H0 + P - 1) // P)]
    NJ = len(HJ)
    with pr.stage() as c:
        w0 = [pr.sb(c, f"w0_{s}", [P, DT, H0], F32) for s in range(2)]
        w1 = [pr.sb(c, f"w1_{s}", [P, DT, H0], F32) for s in range(2)]
        w2 = [pr.sb(c, f"w2_{s}", [P, NJ, D], F32) for s in range(2)]
        ein = pr.sb(c, "expert_in", [P, DT, E0, NT * CAP], F32)
        combT = pr.sb(c, "comb_T", [P, 2, TOK], F32)
        w_in = [pr.sem(f"w_in{s}") for s in range(2)]

        def load_weights(sp, e, s):
            sp.dma_start(w0[s][:], t["w0"][e].rearrange("(t p) h -> p t h", p=P)).then_inc(w_in[s], 16)
            sp.dma_start(w1[s][:], t["w1"][e].rearrange("(t p) h -> p t h", p=P)).then_inc(w_in[s], 16)
            full = (NJ - 1) * P
            sp.dma_start(w2[s][:, 0:NJ - 1], t["w2"][e, 0:full].rearrange("(j p) m -> p j m", p=P)).then_inc(w_in[s], 16)
            sp.dma_start(w2[s][0:H0 - full, NJ - 1], t["w2"][e, full:H0]).then_inc(w_in[s], 16)

        with pr.stage() as c1:
            norm = NormSteps(pr, c1, "fn0")
            rw = pr.sb(c1, "router", [P, DT, E0], F32)
            g3 = lambda name: pr.sb(c1, name, [P, NT, E0], F32)
            g2 = lambda name: pr.sb(c1, name, [P, NT], F32)
            raw, tmp, only, rest = g3("raw"), g3("gate_tmp"), g3("gate_only"), g3("gate_rest")
            first, second, amount = g3("first"), g3("second"), [g3("amount0"), g3("amount1")]
            top, low, gate, where = g2("top"), g2("low"), [g2("gate0"), g2("gate1")], g2("where")
            spot = [pr.sb(c1, f"spot{k}", [P, NT, CAP], F32) for k in range(2)]
            comb = pr.sb(c1, "comb", [P, NT, E0, CAP], F32)
            disp = pr.sb(c1, "disp", [P, NT, E0, CAP], F32)
            tps = pr.banks(c1, "ftr_ps", 2)
            rps = pr.banks(c1, "router_ps", 3)
            dps = pr.banks(c1, "disp_ps", 2)
            r_in, l_ready, x_sub, x_exp = pr.sem("r_in"), pr.sem("l_ready"), pr.sem("x_sub"), pr.sem("x_exp")
            g_step, m1_done, p1_ready, m1k_done, p2_ready = (
                pr.sem(x) for x in ("g_step", "m1_done", "p1_ready", "m1k_done", "p2_ready"))
            disp_done, ct_ready, ct_done, d_ready, d_done = (
                pr.sem(x) for x in ("disp_done", "ct_ready", "ct_done", "d_ready", "d_done"))

            with nc.Block() as block:

                @block.sync
                def _(sp):
                    sp.dma_start(rw[:], t["router"].rearrange("(t p) e -> p t e", p=P)).then_inc(r_in, 16)
                    load_weights(sp, 0, 0)
                    load_weights(sp, 1, 1)

                @block.gpsimd
                def _(pool):
                    norm.pool(pool)

                @block.tensor
                def _(pe):
                    norm.tensor(pe, tps)
                    pe.wait_ge(r_in, 16)
                    pe.wait_ge(norm.s_yT, NT // 2)
                    for g in range(NT):
                        for k in range(DT):
                            mm = pe.matmul(rps[:, 0, g * E0:(g + 1) * E0], pr.yT[:, k, g * P:(g + 1) * P], rw[:, k],
                                           start=(k == 0), stop=(k == DT - 1))
                    mm.then_inc(l_ready, 1)
                    pe.wait_ge(m1_done, 1)
                    pe.matmul(rps[:, 1, 0:NT * E0], pr.lower[:], first[:].rearrange("p g e -> p (g e)"),
                              start=True, stop=True).then_inc(p1_ready, 1)
                    pe.wait_ge(m1k_done, 1)
                    pe.matmul(rps[:, 2, 0:NT * E0], pr.lower[:], second[:].rearrange("p g e -> p (g e)"),
                              start=True, stop=False)
                    pe.matmul(rps[:, 2, 0:NT * E0], pr.ones[:], first[:].rearrange("p g e -> p (g e)"),
                              start=False, stop=True).then_inc(p2_ready, 1)
                    pe.wait_ge(disp_done, 2)
                    for g in range(NT):
                        if g >= 2:
                            pe.wait_ge(d_done, g - 1)
                        for k in range(DT):
                            mm = pe.matmul(dps[:, g % 2, k * 256:(k + 1) * 256], pr.y[:, g, k * P:(k + 1) * P],
                                           disp[:, g].rearrange("p e c -> p (e c)"), start=True, stop=True)
                        mm.then_inc(d_ready, 1)
                    for j in range(NT // 2):
                        if j >= 2:
                            pe.wait_ge(ct_done, j - 1)
                        for i in range(2):
                            for h in range(2):
                                mm = pe.transpose(tps[:, j % 2, (h * 2 + i) * P:(h * 2 + i + 1) * P],
                                                  comb[:, 2 * j + i, 4 * h:4 * h + 4].rearrange("p e c -> p (e c)"),
                                                  pr.ident[:])
                        mm.then_inc(ct_ready, 1)

                @block.scalar
                def _(act):
                    norm.scalar(act, tps)
                    act.wait_ge(x_sub, 1)
                    nc.scalar.activation(raw[:], raw[:], ACT.Exp).then_inc(x_exp, 1)
                    for g in range(NT):
                        act.wait_ge(d_ready, g + 1)
                        nc.scalar.activation(ein[:, :, :, g * CAP:(g + 1) * CAP],
                                             dps[:, g % 2].rearrange("p (k e c) -> p k e c", k=DT, e=E0),
                                             ACT.Copy).then_inc(d_done, 1)
                    act.wait_ge(d_done, NT)

                @block.vector
                def _(dve):
                    v = nc.vector
                    count = [0]

                    def link(ins):
                        count[0] += 1
                        ins.then_inc(g_step, 1)
                        dve.wait_ge(g_step, count[0])

                    over_e = lambda a: a.unsqueeze(2).broadcast_to([P, NT, E0])
                    order = pr.desc[:].unsqueeze(1).broadcast_to([P, NT, E0])

                    def best(src, one_hot):
                        link(v.tensor_reduce(top[:], src[:], AX.X, ALU.max))
                        link(v.tensor_tensor(tmp[:], src[:], over_e(top[:]), ALU.is_equal))
                        link(v.tensor_tensor(tmp[:], tmp[:], order, ALU.mult))
                        link(v.tensor_reduce(low[:], tmp[:], AX.X, ALU.max))
                        link(v.tensor_tensor(one_hot[:], order, over_e(low[:]), ALU.is_equal))

                    def keep(k, one_hot, counted):
                        link(v.tensor_scalar(tmp[:], counted, float(CAP), None, ALU.is_lt))
                        link(v.tensor_tensor(one_hot[:], one_hot[:], tmp[:], ALU.mult))
                        if k == 0:
                            v.tensor_copy(where[:], top[:]).then_inc(m1k_done, 1)
                        link(v.tensor_tensor(tmp[:], one_hot[:], counted, ALU.mult))
                        link(v.tensor_reduce(where[:], tmp[:], AX.X, ALU.add))
                        link(v.tensor_tensor(amount[k][:], one_hot[:], over_e(gate[k][:]), ALU.mult))
                        link(v.tensor_tensor(spot[k][:], pr.place[:].unsqueeze(1).broadcast_to([P, NT, CAP]),
                                             where[:].unsqueeze(2).broadcast_to([P, NT, CAP]), ALU.is_equal))

                    norm.vector(dve)
                    dve.wait_ge(l_ready, 1)
                    logits = rps[:, 0, 0:NT * E0].rearrange("p (g e) -> p g e", g=NT)
                    link(v.tensor_reduce(top[:], logits, AX.X, ALU.max))
                    v.tensor_tensor(raw[:], logits, over_e(top[:]), ALU.subtract).then_inc(x_sub, 1)
                    dve.wait_ge(x_exp, 1)
                    link(v.tensor_reduce(low[:], raw[:], AX.X, ALU.add))
                    link(v.reciprocal(low[:], low[:]))
                    link(v.tensor_tensor(raw[:], raw[:], over_e(low[:]), ALU.mult))
                    best(raw, first)
                    link(v.tensor_copy(gate[0][:], top[:]))
                    v.tensor_scalar(only[:], first[:], -1.0, 1.0, ALU.mult, ALU.add).then_inc(m1_done, 1)
                    dve.wait_ge(m1_done, 1)
                    link(v.tensor_tensor(rest[:], raw[:], only[:], ALU.mult))
                    best(rest, second)
                    link(v.tensor_copy(gate[1][:], top[:]))
                    dve.wait_ge(p1_ready, 1)
                    keep(0, first, rps[:, 1, 0:NT * E0].rearrange("p (g e) -> p g e", g=NT))
                    dve.wait_ge(p2_ready, 1)
                    keep(1, second, rps[:, 2, 0:NT * E0].rearrange("p (g e) -> p g e", g=NT))
                    for k, dst in enumerate((comb, disp)):
                        for g in range(NT):
                            ins = v.tensor_tensor(dst[:, g], amount[k][:, g].unsqueeze(2).broadcast_to([P, E0, CAP]),
                                                  spot[k][:, g].unsqueeze(1).broadcast_to([P, E0, CAP]), ALU.mult)
                    link(ins)
                    v.tensor_tensor(comb[:], comb[:], disp[:], ALU.add).then_inc(disp_done, 1)
                    dve.wait_ge(disp_done, 1)
                    v.tensor_scalar(disp[:], comb[:], 0.0, None, ALU.not_equal).then_inc(disp_done, 1)
                    for j in range(NT // 2):
                        dve.wait_ge(ct_ready, j + 1)
                        v.tensor_copy(combT[:, :, 2 * j * P:2 * (j + 1) * P],
                                      tps[:, j % 2].rearrange("p (h n) -> p h n", h=2)).then_inc(ct_done, 1)
                    dve.wait_ge(ct_done, NT // 2)

        hid = pr.sb(c, "hid", [P, NJ, NT * CAP], F32)
        act_out = pr.sb(c, "gelu_out", [P, 4, NT * CAP], F32)
        eout = pr.sb(c, "expert_out", [P, E0, 2, D], F32)
        ec = pr.sb(c, "expert_places", [P, NT, 2, D], F32)
        h_ps = pr.banks(c, "h_ps", 4)
        e_ps = pr.banks(c, "e_ps", 2)
        y_ps = pr.banks(c, "moe_y_ps", 2)
        h_ready, gelu_done, hid_done, e_ready = (pr.sem(x) for x in ("h_ready", "gelu_done", "hid_done", "e_ready"))
        e_copied, e_out, ec_in, y_ready, y_done = (pr.sem(x) for x in ("e_copied", "e_out", "ec_in", "my_ready", "my_done"))

        with nc.Block() as block:

            @block.sync
            def _(sp):
                def results_out(e):
                    sp.wait_ge(e_copied, e + 3)
                    sp.dma_start(t["e_scr"][e].rearrange("(r p) m -> p r m", p=P), eout[:, e]).then_inc(e_out, 16)

                with sp.Fori(1, E0 // 2) as i:
                    for s in range(2):
                        sp.wait_ge(e_ready, i * 2 + s - 1)
                        load_weights(sp, i * 2 + s, s)
                for e in range(E0):
                    results_out(e)
                sp.wait_ge(e_out, 16 * E0)
                for e in range(E0):
                    sp.dma_start(ec[CAP * (e % 4):CAP * (e % 4 + 1), :, e // 4],
                                 t["e_scr"][e].rearrange("(g c) m -> c g m", c=CAP)).then_inc(ec_in, 16)

            @block.tensor
            def _(pe):
                with pe.Fori(0, E0 // 2) as i:
                    for s in range(2):
                        e = i * 2 + s
                        pe.wait_ge(w_in[s], i * 64 + 64)
                        for j, (h0, hn) in enumerate(HJ):
                            if j >= 4:
                                pe.wait_ge(hid_done, e * NJ + j - 3)
                            for w, off in ((w0[s], 0), (w1[s], 256)):
                                for k in range(DT):
                                    mm = pe.matmul(h_ps[0:hn, j % 4, off:off + 256], w[:, k, h0:h0 + hn],
                                                   ein[:, k, bass.ds(e, 1)],
                                                   start=(k == 0), stop=(k == DT - 1))
                            mm.then_inc(h_ready, 1)
                        pe.wait_ge(e_copied, e + 1)
                        for r in range(2):
                            for j, (h0, hn) in enumerate(HJ):
                                if r == 0:
                                    pe.wait_ge(hid_done, e * NJ + j + 1)
                                mm = pe.matmul(e_ps[:, s, r * 256:(r + 1) * 256], hid[0:hn, j, r * P:(r + 1) * P],
                                               w2[s][0:hn, j], start=(j == 0), stop=(j == NJ - 1))
                        mm.then_inc(e_ready, 1)
                pe.wait_ge(ec_in, 16 * E0)
                for g in range(NT):
                    if g >= 2:
                        pe.wait_ge(y_done, g - 1)
                    for h in range(2):
                        mm = pe.matmul(y_ps[:, g % 2, 0:D], combT[:, h, g * P:(g + 1) * P], ec[:, g, h],
                                       start=(h == 0), stop=(h == 1))
                    mm.then_inc(y_ready, 1)

            @block.scalar
            def _(act):
                with act.Fori(0, E0 // 2) as i:
                    for s in range(2):
                        e = i * 2 + s
                        for j, (h0, hn) in enumerate(HJ):
                            act.wait_ge(h_ready, e * NJ + j + 1)
                            if j >= 4:
                                act.wait_ge(hid_done, e * NJ + j - 3)
                            nc.scalar.activation(act_out[0:hn, j % 4], h_ps[0:hn, j % 4, 0:256],
                                                 ACT.Gelu_apprx_tanh).then_inc(gelu_done, 1)

            @block.vector
            def _(dve):
                nc.vector.memset(eout[:, :, :, 0:1], 0.0).then_inc(e_copied, 2)
                with dve.Fori(0, E0 // 2) as i:
                    for s in range(2):
                        e = i * 2 + s
                        for j, (h0, hn) in enumerate(HJ):
                            dve.wait_ge(gelu_done, e * NJ + j + 1)
                            nc.vector.tensor_tensor(hid[0:hn, j], act_out[0:hn, j % 4], h_ps[0:hn, j % 4, 256:512],
                                                    ALU.mult).then_inc(hid_done, 1)
                        dve.wait_ge(e_ready, e + 1)
                        nc.vector.tensor_copy(eout[:, bass.ds(e, 1)].rearrange("p o r m -> p (o r m)"),
                                              e_ps[:, s]).then_inc(e_copied, 1)
                for g in range(NT):
                    dve.wait_ge(y_ready, g + 1)
                    nc.vector.tensor_tensor(pr.x[:, g], pr.x[:, g], y_ps[:, g % 2, 0:D], ALU.add).then_inc(y_done, 1)
                dve.wait_ge(y_done, NT)


def moe_top2(pr):
    nc, t = pr.nc, pr.t
    with pr.stage() as c:
        wg = pr.sb(c, "wg", [P, 2, DT, I1], F32)
        wu = pr.sb(c, "wu", [P, 2, DT, I1], F32)
        wd = pr.sb(c, "wd", [P, 2, I1 // P, D], F32)
        rows = pr.sb(c, "row_token", [P, TILES], U32)
        slots = pr.sb(c, "token_row", [P, 2, NT], U32)
        share = [pr.sb(c, f"share{k}", [P, NT], F32) for k in range(2)]
        table = pr.sb(c, "tile_table", [P, 2 * TILES + E1], I32)
        w_in = [pr.sem(f"w1_in{s}") for s in range(2)]

        def load_weights(sp, e, s):
            sp.dma_start(wg[:, s], t["gateT"][e].rearrange("(t p) i -> p t i", p=P)).then_inc(w_in[s], 16)
            sp.dma_start(wu[:, s], t["upT"][e].rearrange("(t p) i -> p t i", p=P)).then_inc(w_in[s], 16)
            sp.dma_start(wd[:, s], t["downT"][e].rearrange("(t p) d -> p t d", p=P)).then_inc(w_in[s], 16)

        with pr.stage() as c1:
            norm = NormSteps(pr, c1, "fn1")
            cw = pr.sb(c1, "conf_w", [P, DT, E1], F32)
            cb = pr.sb(c1, "conf_b", [P, E1], F32)
            wealth = pr.sb(c1, "wealth", [P, E1], F32)
            g3 = lambda name: pr.sb(c1, name, [P, NT, E1], F32)
            g2 = lambda name: pr.sb(c1, name, [P, NT], F32)
            g1 = lambda name: pr.sb(c1, name, [P, E1], F32)
            bids, tmp, chosen, rank, rest = g3("bids"), g3("bid_tmp"), g3("chosen"), g3("rank"), g3("bid_rest")
            one = [g3("one_hot0"), g3("one_hot1")]
            top, low = [g2("bid0"), g2("bid1")], g2("bid_low")
            place, full, tile_no, slot_f = g2("place_in"), g2("full_tiles"), g2("tile_no"), g2("slot_f")
            place_k = [g2("place0"), g2("place1")]
            count, tiles, end, start = g1("count"), g1("tiles"), g1("end"), g1("start")
            steps = pr.sb(c1, "steps", [P, 8], F32)
            big = pr.sb(c1, "compare", [P, TILES, 8], F32)
            line = pr.sb(c1, "line", [P, P], F32)
            token = pr.sb(c1, "token_no", [P, NT], F32)
            expert = pr.sb(c1, "expert_of", [P, TILES], F32)
            odd = pr.sb(c1, "odd", [P, TILES], F32)
            hot_row = pr.sb(c1, "hot_row", [P, 2 * NT, P], F32)
            hot_tile = pr.sb(c1, "hot_tile", [P, 2 * NT, TILES], F32)
            tps = pr.banks(c1, "gtr_ps", 2)
            rps = pr.banks(c1, "bid_ps", 3)
            ips = pr.banks(c1, "row_ps", 1)
            c_in, y_out, iota_done, l_ready, z_done, sig_done = (
                pr.sem(x) for x in ("c_in", "y_out", "iota_done", "bl_ready", "z_done", "sig_done"))
            b_step, c_done, r_ready, diff_done, exp_done, hot_done, i_ready = (
                pr.sem(x) for x in ("b_step", "c_done", "r_ready", "diff_done", "bexp_done", "hot_done", "i_ready"))

            with nc.Block() as block:

                @block.sync
                def _(sp):
                    sp.dma_start(cw[:], t["confT"].rearrange("(t p) e -> p t e", p=P)).then_inc(c_in, 16)
                    sp.dma_start(cb[:], t["conf_b"].partition_broadcast(P)).then_inc(c_in, 16)
                    sp.dma_start(wealth[:], t["wealth"].partition_broadcast(P)).then_inc(c_in, 16)
                    load_weights(sp, 0, 0)
                    load_weights(sp, 1, 1)
                    sp.wait_ge(norm.s_y, NT)
                    sp.dma_start(t["y_scr"].rearrange("(t p) d -> p t d", p=P), pr.y[:]).then_inc(y_out, 16)
                    sp.wait_ge(y_out, 16)

                @block.gpsimd
                def _(pool):
                    g = nc.gpsimd
                    loose = dict(allow_small_or_imprecise_dtypes=True)
                    g.iota(steps[:], pattern=[[P, 8]], base=0, channel_multiplier=0, **loose).then_inc(iota_done, 1)
                    g.iota(line[:], pattern=[[1, P]], base=0, channel_multiplier=0, **loose).then_inc(iota_done, 1)
                    g.iota(token[:], pattern=[[P, NT]], base=0, channel_multiplier=1, **loose).then_inc(iota_done, 1)
                    norm.pool(pool)

                @block.tensor
                def _(pe):
                    norm.tensor(pe, tps)
                    pe.wait_ge(c_in, 48)
                    pe.wait_ge(norm.s_yT, NT // 2)
                    for g in range(NT):
                        for k in range(DT):
                            mm = pe.matmul(rps[:, 0, g * E1:(g + 1) * E1], pr.yT[:, k, g * P:(g + 1) * P], cw[:, k],
                                           start=(k == 0), stop=(k == DT - 1))
                    mm.then_inc(l_ready, 1)
                    pe.wait_ge(c_done, 1)
                    flat = chosen[:].rearrange("p g e -> p (g e)")
                    pe.matmul(rps[:, 1, 0:NT * E1], pr.lower[:], flat, start=True, stop=True)
                    pe.matmul(rps[:, 2, 0:NT * E1], pr.ones[:], flat, start=True, stop=True).then_inc(r_ready, 1)
                    pe.wait_ge(hot_done, 1)
                    for n in range(2 * NT):
                        mm = pe.matmul(ips[:, 0, 0:TILES], hot_row[:, n], hot_tile[:, n],
                                       start=(n == 0), stop=(n == 2 * NT - 1))
                    mm.then_inc(i_ready, 1)

                @block.scalar
                def _(act):
                    norm.scalar(act, tps)
                    act.wait_ge(z_done, 1)
                    nc.scalar.activation(bids[:], bids[:], ACT.Sigmoid).then_inc(sig_done, 1)
                    act.wait_ge(diff_done, 1)
                    nc.scalar.activation(low[:], low[:], ACT.Exp).then_inc(exp_done, 1)

                @block.vector
                def _(dve):
                    v = nc.vector
                    n_links = [0]

                    def link(ins):
                        n_links[0] += 1
                        ins.then_inc(b_step, 1)
                        dve.wait_ge(b_step, n_links[0])

                    wide = lambda a: a.unsqueeze(2).broadcast_to([P, NT, E1])
                    by_e = lambda a: a.unsqueeze(1).broadcast_to([P, NT, E1])

                    def best(src, value, one_hot):
                        link(v.tensor_reduce(value[:], src[:], AX.X, ALU.max))
                        link(v.tensor_tensor(tmp[:], src[:], wide(value[:]), ALU.is_equal))
                        link(v.tensor_tensor(tmp[:], tmp[:], by_e(pr.desc[:]), ALU.mult))
                        link(v.tensor_reduce(low[:], tmp[:], AX.X, ALU.max))
                        link(v.tensor_tensor(one_hot[:], by_e(pr.desc[:]), wide(low[:]), ALU.is_equal))

                    norm.vector(dve)
                    dve.wait_ge(l_ready, 1)
                    v.tensor_tensor(bids[:], rps[:, 0, 0:NT * E1].rearrange("p (g e) -> p g e", g=NT), by_e(cb[:]),
                                    ALU.add).then_inc(z_done, 1)
                    dve.wait_ge(sig_done, 1)
                    link(v.tensor_tensor(bids[:], bids[:], by_e(wealth[:]), ALU.mult))
                    best(bids, top[0], one[0])
                    link(v.tensor_scalar(tmp[:], one[0][:], -1.0, 1.0, ALU.mult, ALU.add))
                    link(v.tensor_tensor(rest[:], bids[:], tmp[:], ALU.mult))
                    link(v.scalar_tensor_tensor(out=rest[:], in0=one[0][:], scalar=-BIG, in1=rest[:],
                                                op0=ALU.mult, op1=ALU.add))
                    best(rest, top[1], one[1])
                    v.tensor_tensor(chosen[:], one[0][:], one[1][:], ALU.add).then_inc(c_done, 1)
                    v.tensor_tensor(low[:], top[1][:], top[0][:], ALU.subtract).then_inc(diff_done, 1)
                    dve.wait_ge(exp_done, 1)
                    link(v.tensor_scalar(slot_f[:], low[:], 1.0, None, ALU.add))
                    link(v.reciprocal(share[0][:], slot_f[:]))
                    link(v.tensor_tensor(share[1][:], low[:], share[0][:], ALU.mult))
                    dve.wait_ge(r_ready, 1)
                    link(v.memset(count[:], 0.0))
                    for g in range(NT):
                        link(v.tensor_tensor(rank[:, g], rps[:, 1, g * E1:(g + 1) * E1], count[:], ALU.add))
                        link(v.tensor_tensor(count[:], count[:], rps[:, 2, g * E1:(g + 1) * E1], ALU.add))
                    dve.wait_ge(iota_done, 3)
                    grid = big[:, 0:E1]
                    link(v.tensor_tensor(grid, count[:].unsqueeze(2).broadcast_to([P, E1, 8]),
                                         steps[:].unsqueeze(1).broadcast_to([P, E1, 8]), ALU.is_gt))
                    link(v.tensor_reduce(tiles[:], grid, AX.X, ALU.add))
                    link(v.tensor_copy(end[:, 0:1], tiles[:, 0:1]))
                    for e in range(1, E1):
                        link(v.tensor_tensor(end[:, e:e + 1], end[:, e - 1:e], tiles[:, e:e + 1], ALU.add))
                    link(v.tensor_tensor(start[:], end[:], tiles[:], ALU.subtract))
                    link(v.tensor_tensor(big[:, :, 0:7], end[:, 0:7].unsqueeze(1).broadcast_to([P, TILES, 7]),
                                         line[:, 0:TILES].unsqueeze(2).broadcast_to([P, TILES, 7]), ALU.is_le))
                    link(v.tensor_reduce(expert[:], big[:, :, 0:7], AX.X, ALU.add))
                    link(v.tensor_tensor(big[:, :, 0:4], expert[:].unsqueeze(2).broadcast_to([P, TILES, 4]),
                                         line[:, 1:8:2].unsqueeze(1).broadcast_to([P, TILES, 4]), ALU.is_equal))
                    link(v.tensor_reduce(odd[:], big[:, :, 0:4], AX.X, ALU.add))
                    link(v.tensor_copy(table[:, 0:TILES], odd[:]))
                    link(v.tensor_scalar(table[:, TILES:2 * TILES], expert[:], 1.0, None, ALU.add))
                    link(v.tensor_scalar(table[:, 2 * TILES:], end[:], 1.0, None, ALU.add))
                    for k in range(2):
                        link(v.tensor_tensor(tmp[:], one[k][:], rank[:], ALU.mult))
                        link(v.tensor_reduce(place[:], tmp[:], AX.X, ALU.add))
                        link(v.tensor_tensor(tmp[:, :, 0:7], place[:].unsqueeze(2).broadcast_to([P, NT, 7]),
                                             steps[:, 1:8].unsqueeze(1).broadcast_to([P, NT, 7]), ALU.is_ge))
                        link(v.tensor_reduce(full[:], tmp[:, :, 0:7], AX.X, ALU.add))
                        link(v.tensor_tensor(tmp[:], one[k][:], by_e(start[:]), ALU.mult))
                        link(v.tensor_reduce(tile_no[:], tmp[:], AX.X, ALU.add))
                        link(v.scalar_tensor_tensor(out=slot_f[:], in0=tile_no[:], scalar=float(P), in1=place[:],
                                                    op0=ALU.mult, op1=ALU.add))
                        link(v.tensor_copy(slots[:, k], slot_f[:]))
                        link(v.tensor_tensor(tile_no[:], tile_no[:], full[:], ALU.add))
                        link(v.scalar_tensor_tensor(out=place_k[k][:], in0=full[:], scalar=-float(P), in1=place[:],
                                                    op0=ALU.mult, op1=ALU.add))
                        link(v.tensor_tensor(hot_row[:, k * NT:(k + 1) * NT],
                                             place_k[k][:].unsqueeze(2).broadcast_to([P, NT, P]),
                                             line[:].unsqueeze(1).broadcast_to([P, NT, P]), ALU.is_equal))
                        mine = hot_tile[:, k * NT:(k + 1) * NT]
                        link(v.tensor_tensor(mine, tile_no[:].unsqueeze(2).broadcast_to([P, NT, TILES]),
                                             line[:, 0:TILES].unsqueeze(1).broadcast_to([P, NT, TILES]), ALU.is_equal))
                        ins = v.tensor_tensor(mine, mine, token[:].unsqueeze(2).broadcast_to([P, NT, TILES]), ALU.mult)
                        if k == 0:
                            link(ins)
                    ins.then_inc(hot_done, 1)
                    dve.wait_ge(i_ready, 1)
                    link(v.tensor_copy(rows[:], ips[:, 0, 0:TILES]))

        now = pr.sb(c, "rows_now", [P, 2], U32)
        xg = pr.sb(c, "xg", [P, 2, D], F32)
        xgT = pr.sb(c, "xg_T", [P, DT, P], F32)
        silu = pr.sb(c, "silu", [P, 2, 512], F32)
        prod = pr.sb(c, "silu_up", [P, 2, 512], F32)
        prodT = pr.sb(c, "silu_up_T", [P, 8, P], F32)
        y_all = pr.sb(c, "y_all", [P, TILES, D], F32)
        back = pr.sb(c, "y_back", [P, NT, 2, D], F32)
        gu_ps = pr.banks(c, "gu_ps", 4)
        tr_ps = pr.banks(c, "pt_ps", 2)
        xt_ps = pr.banks(c, "xt_ps", 1)
        y_ps = pr.banks(c, "y2_ps", 1)
        xg_in = [pr.sem(f"xg_in{s}") for s in range(2)]
        ready, pool_step, now_done, xt_ready, xT_done = (
            pr.sem(x) for x in ("weights_ready", "pool_step", "now_done", "xt_ready", "xT_done"))
        g_ready, u_ready, silu_done, prod_done, tr_ready = (
            pr.sem(x) for x in ("g_ready", "u_ready", "silu_done", "prod_done", "tr_ready"))
        pT_done = [pr.sem("pT_done0"), pr.sem("pT_done1")]
        y_ready, y_copied, y_sent, x_done = (pr.sem(x) for x in ("y2_ready", "y2_copied", "y2_sent", "x2_done"))
        back_in = [pr.sem(f"back_in{g}") for g in range(NT)]

        def tiles_of(eng, tile):
            with eng.Fori(0, TILES // 2) as i:
                for s in range(2):
                    tile(i * 2 + s, i, s, True)
            tile(TILES - 1, TILES // 2, 0, False)

        with nc.Block() as block:

            @block.sync
            def _(sp):
                def arrived(n, s):
                    sp.wait_ge(w_in[s], n * 48 + 48)
                    sp.sem_inc(ready, 1)

                arrived(0, 0)
                with sp.Fori(1, E1 // 2) as i:
                    for s in range(2):
                        last = sp.value_load(table[0:1, bass.ds(i * 2 + s - 2 + 2 * TILES, 1)], min_val=1, max_val=TILES + 1)
                        sp.wait_ge(y_ready, last)
                        load_weights(sp, i * 2 + s, s)
                        arrived(i - 1 + s, 1 - s)
                arrived(E1 // 2 - 1, 1)

            @block.gpsimd
            def _(pool):
                def fetch(T, s):
                    pool.wait_ge(xt_ready, T + 1)
                    pool.sem_inc(pool_step, 1)
                    nc.gpsimd.tensor_copy(now[:, s:s + 1], rows[:, bass.ds(T, 1)]).then_inc(now_done, 1)
                    pool.wait_ge(now_done, T + 1)
                    pool.sem_inc(pool_step, 1)
                    pool.indirect_dma_start(out=xg[:, s], out_offset=None, in_=t["y_scr"],
                                            in_offset=bass.IndirectOffsetOnAxis(ap=now[:, s:s + 1], axis=0),
                                            bounds_check=TOK - 1).then_inc(xg_in[s], 16)

                tiles_of(pool, lambda T, i, s, has_next: fetch(T, s))
                pool.wait_ge(y_sent, 16 * TILES)
                for g in range(NT):
                    for k in range(2):
                        pool.indirect_dma_start(out=back[:, g, k], out_offset=None, in_=t["row_scr"],
                                                in_offset=bass.IndirectOffsetOnAxis(ap=slots[:, k, g:g + 1], axis=0),
                                                bounds_check=TILES * P - 1).then_inc(back_in[g], 16)

            @block.tensor
            def _(pe):
                pe.sem_inc(xt_ready, 2)
                pe.sem_inc(y_ready, 1)

                def turn_x(T, i, s):
                    pe.wait_ge(xg_in[s], i * 16 + 16)
                    for k in range(DT):
                        mm = pe.transpose(xt_ps[:, 0, k * P:(k + 1) * P], xg[:, s, k * P:(k + 1) * P], pr.ident[:])
                    mm.then_inc(xt_ready, 1)

                def up(w, slot, bank, h, done):
                    for k in range(DT):
                        mm = pe.matmul(gu_ps[:, bank], xgT[:, k], w[:, bass.ds(slot, 1), k, h * 512:(h + 1) * 512],
                                       start=(k == 0), stop=(k == DT - 1))
                    mm.then_inc(done, 1)

                def turn_prod(T, h):
                    pe.wait_ge(prod_done, T * 2 + h + 3)
                    for j in range(4):
                        mm = pe.transpose(tr_ps[:, h, j * P:(j + 1) * P], prod[:, h, j * P:(j + 1) * P], pr.ident[:])
                    mm.then_inc(tr_ready, 1)

                def down(T, slot, h):
                    pe.wait_ge(pT_done[h], T + 1)
                    if h == 0:
                        pe.wait_ge(y_copied, T + 1)
                    for j in range(4 * h, 4 * h + 4):
                        mm = pe.matmul(y_ps[:, 0, 0:D], prodT[:, j], wd[:, bass.ds(slot, 1), j],
                                       start=(j == 0), stop=(j == 7))
                    if h == 1:
                        mm.then_inc(y_ready, 1)

                def tile(T, i, s, has_next):
                    slot = pe.value_load(table[0:1, bass.ds(T, 1)], min_val=0, max_val=1)
                    need = pe.value_load(table[0:1, bass.ds(T + TILES, 1)], min_val=1, max_val=E1)
                    pe.wait_ge(ready, need)
                    pe.wait_ge(xT_done, T + 1)
                    pe.wait_ge(prod_done, T * 2 + 1)
                    up(wg, slot, 0, 0, g_ready)
                    up(wu, slot, 1, 0, u_ready)
                    pe.wait_ge(prod_done, T * 2 + 2)
                    up(wg, slot, 2, 1, g_ready)
                    turn_prod(T, 0)
                    up(wu, slot, 3, 1, u_ready)
                    down(T, slot, 0)
                    turn_prod(T, 1)
                    if has_next:
                        turn_x(T + 1, i + s, 1 - s)
                    down(T, slot, 1)

                turn_x(0, 0, 0)
                tiles_of(pe, tile)

            @block.scalar
            def _(act):
                def tile(T, i, s, has_next):
                    for h in range(2):
                        act.wait_ge(g_ready, T * 2 + h + 1)
                        nc.scalar.activation(silu[:, h], gu_ps[:, 2 * h], ACT.Silu).then_inc(silu_done, 1)
                    act.wait_ge(tr_ready, T * 2 + 2)
                    nc.scalar.activation(prodT[:, 4:8], tr_ps[:, 1].rearrange("p (j n) -> p j n", j=4),
                                         ACT.Copy).then_inc(pT_done[1], 1)
                    act.wait_ge(y_ready, T + 2)
                    nc.scalar.activation(y_all[:, bass.ds(T, 1)], y_ps[:, 0, 0:D], ACT.Copy).then_inc(y_copied, 1)
                    act.wait_ge(y_copied, T + 2)
                    act.dma_start(t["row_scr"][bass.ds(T * P, P)], y_all[:, bass.ds(T, 1)]
                                  .rearrange("p o d -> p (o d)")).then_inc(y_sent, 16)

                act.sem_inc(y_copied, 1)
                tiles_of(act, tile)

            @block.vector
            def _(dve):
                def turn_x_out(T):
                    dve.wait_ge(xt_ready, T + 3)
                    nc.vector.tensor_copy(xgT[:], xt_ps[:, 0, 0:D].rearrange("p (k n) -> p k n", k=DT)).then_inc(xT_done, 1)

                def multiply(T, h):
                    dve.wait_ge(silu_done, T * 2 + h + 1)
                    dve.wait_ge(u_ready, T * 2 + h + 1)
                    nc.vector.tensor_tensor(prod[:, h], silu[:, h], gu_ps[:, 2 * h + 1], ALU.mult).then_inc(prod_done, 1)

                def tile(T, i, s, has_next):
                    multiply(T, 0)
                    dve.wait_ge(tr_ready, T * 2 + 1)
                    nc.vector.tensor_copy(prodT[:, 0:4], tr_ps[:, 0].rearrange("p (j n) -> p j n", j=4)).then_inc(pT_done[0], 1)
                    multiply(T, 1)
                    if has_next:
                        turn_x_out(T + 1)

                nc.vector.memset(prod[:, :, 0:1], 0.0).then_inc(prod_done, 2)
                turn_x_out(0)
                tiles_of(dve, tile)
                for g in range(NT):
                    dve.wait_ge(back_in[g], 32)
                    for k in range(2):
                        nc.vector.scalar_tensor_tensor(out=pr.x[:, g], in0=back[:, g, k], scalar=share[k][:, g:g + 1],
                                                       in1=pr.x[:, g], op0=ALU.mult, op1=ALU.add).then_inc(x_done, 1)
                        dve.wait_ge(x_done, 2 * g + k + 1)


def main_program(nc, t, stages=99):
    with ExitStack() as ctx:
        pr = Prog(nc, t)
        pr.x = pr.sb(ctx, "x_tok", [P, NT, D], F32)
        pr.y = pr.sb(ctx, "y_tok", [P, NT, D], F32)
        pr.yT = pr.sb(ctx, "y_T", [P, DT, TOK], F32)
        pr.ident = pr.sb(ctx, "ident", [P, P], F32)
        pr.ident_bf = pr.sb(ctx, "ident_bf", [P, P], BF16)
        pr.lower = pr.sb(ctx, "lower", [P, P], F32)
        pr.ones = pr.sb(ctx, "ones", [P, P], F32)
        pr.sel = pr.sb(ctx, "sel", [P, P], F32)
        pr.desc = pr.sb(ctx, "desc", [P, 8], F32)
        pr.place = pr.sb(ctx, "place", [P, CAP], F32)
        setup(pr)
        attention_layer(pr, 0)
        if stages >= 2:
            moe_capacity(pr)
        if stages >= 3:
            attention_layer(pr, 1)
        if stages >= 4:
            moe_top2(pr)
        x_out = pr.sem("x_out")
        with nc.Block() as block:

            @block.sync
            def _(sp):
                sp.dma_start(t["out"].rearrange("(t p) d -> p t d", p=P), pr.x[:]).then_inc(x_out, 16)
                sp.wait_ge(x_out, 16)


def laid_out(v):
    import numpy as np

    a = {k: np.asarray(x) for k, x in v.items()}
    T = lambda x: np.ascontiguousarray(np.swapaxes(x, -1, -2))
    flag = lambda x: np.ascontiguousarray(x).view(np.uint32)
    t = {
        "x": a["x"].reshape(TOK, D),
        "ctxT": T(a["ctx_1024"].reshape(B * SK, D)),
        "mask": flag(a["mask_1x1xSxS2_bk1"].reshape(SQ, SK)),
        "maskT": flag(T(a["mask_1x1xSxS2_bk1"].reshape(SQ, SK))),
        "amask": a["fside_SxS2_0"],
        "amaskT": T(a["fside_SxS2_0"]),
        "pad": flag(a["mask_BxS2_bf0"]),
        "router": a["L0_ffn_router_w"],
        "w0": a["L0_ffn_w0_kernel"], "w1": a["L0_ffn_w1_kernel"], "w2": a["L0_ffn_wo_kernel"],
        "confT": T(a["L1_ffn_conf_w"]),
        "conf_b": a["L1_ffn_conf_b"], "wealth": a["L1_ffn_wealth"],
        "gateT": T(a["L1_ffn_gate_w"]), "upT": T(a["L1_ffn_up_w"]), "downT": T(a["L1_ffn_down_w"]),
    }
    for l in range(2):
        for n in "qkvo":
            t[f"w{n}T{l}"] = T(a[f"L{l}_xattn_W{n}"])
        for n in "qk":
            t[f"b{n}{l}"] = T(a[f"L{l}_xattn_b{n}"].reshape(DT, P))
        for n in "vo":
            t[f"b{n}{l}"] = a[f"L{l}_xattn_b{n}"]
    return {k: np.ascontiguousarray(x) for k, x in t.items()}


SCRATCH = {
    "k_scr": ([2, 3, D, B * SK], BF16),
    "q_scr": ([2, 3, D, TOK], BF16),
    "v_scr": ([2, P, B * KT, D], F32),
    "pad_scr": ([2, B, HG, SK], BF16),
    "y_scr": ([TOK, D], F32),
    "row_scr": ([TILES * P, D], F32),
    "e_scr": ([E0, NT * CAP, D], F32),
}


def kernel(**inputs):
    import concourse.bacc as bacc
    from concourse.bass_utils import run_bass_kernel_spmd

    nc = bacc.Bacc("TRN2", target_bir_lowering=False, num_devices=1)
    arrays = laid_out(inputs)
    t = {k: nc.dram_tensor(f"in_{k}", a.shape, mybir.dt.from_np(a.dtype), kind="ExternalInput").ap()
         for k, a in arrays.items()}
    t["out"] = nc.dram_tensor("out", [TOK, D], F32, kind="ExternalOutput").ap()
    for k, (shape, dt) in SCRATCH.items():
        t[k] = nc.dram_tensor(k, shape, dt, kind="Internal").ap()
    main_program(nc, t)
    r = run_bass_kernel_spmd(nc, [{f"in_{k}": a for k, a in arrays.items()}], core_ids=[0])
    return r.results[0]["out"].reshape(B, SQ, D)
```

```python
from contextlib import ExitStack, contextmanager

import concourse.bass as bass
from concourse import mybir

F32 = mybir.dt.float32
BF16 = mybir.dt.bfloat16
F32R = mybir.dt.float32r
U8 = mybir.dt.uint8
U32 = mybir.dt.uint32
I32 = mybir.dt.int32
ALU = mybir.AluOpType
ACT = mybir.ActivationFunctionType
AX = mybir.AxisListType

P = 128
B, SQ, SK, D = 2, 512, 1024, 256
NH, DH = 16, 16
TOK = B * SQ
NT = TOK // P
DT = D // P
QT = SQ // P
KT = SK // P
HG = 4
NG = NH // HG
E0, H0, CAP = 8, 1368, 32
E1, I1 = 8, 1024
TILES = 2 * TOK // P + E1 - 1
BIG = float(2.0 ** 100)
EPS = 1e-5
K_PARTS = (0, 1, 0, 2, 0, 1)
Q_PARTS = (0, 0, 1, 0, 2, 1)
STACK = 6 * DH
PADROW = STACK
MROW = STACK + 1
ROWS = STACK + 4
A_SPLIT = (0, 0, 7, 7, 6, 6, 6, 0)
FIRST_A = 2

class Prog:

    def __init__(self, nc, t):
        self.nc, self.t, self.sems = nc, t, []

    def sem(self, name):
        s = self.nc.alloc_semaphore(name=name)
        self.sems.append(s)
        return s

    @contextmanager
    def stage(self):
        outer, self.sems = self.sems, []
        with ExitStack() as inner:
            yield inner
        if self.sems:
            self.nc.clear_and_free_semaphores(self.sems)
            self.nc.all_engine_barrier()
        self.sems = outer

    def sb(self, ctx, name, shape, dt):
        return ctx.enter_context(self.nc.sbuf_tensor(name, shape, dt))

    def banks(self, ctx, name, n):
        return ctx.enter_context(self.nc.psum_tensor(name, [P, n, 512], F32))


def setup(pr, m):
    nc, t = pr.nc, pr.t
    with pr.stage() as c:
        ctxT = pr.sb(c, "ctxT", [P, DT, B * SK], F32)
        wk = pr.sb(c, "wk", [P, 2, DT, D], F32)
        wv = pr.sb(c, "wv", [P, 2, DT, D], F32)
        bk = pr.sb(c, "bk", [P, 2, DT], F32)
        bv = pr.sb(c, "bv", [P, 2, D], F32)
        full = pr.sb(c, "k_full", [P, 2, 512], F32)
        rest = pr.sb(c, "k_rest", [P, 2, 512], F32)
        parts = pr.sb(c, "k_parts", [P, 3, DT, B * SK], BF16)
        vals1 = pr.sb(c, "vals1", [P, B * KT, D], F32)
        mrow = pr.sb(c, "mask_rows", [P, QT, SK // 4], U32)
        mcol = pr.sb(c, "mask_cols", [P, KT, SQ // 4], U32)
        vals = [m.vals, vals1]
        kps = pr.banks(c, "k_ps", 4)
        vps = pr.banks(c, "v_ps", 4)
        x_in, init = pr.sem("x_in"), pr.sem("stack_init")
        w_in = [pr.sem(f"wkv_in{l}") for l in range(2)]
        ctx_in = [pr.sem(f"ctx_in{i}") for i in range(4)]
        id_zero, id_done, const_done = pr.sem("id_zero"), pr.sem("id_done"), pr.sem("const_done")
        k_ready, k_full, k_hi = pr.sem("k_ready"), pr.sem("k_full_done"), pr.sem("k_hi_done")
        k_rest, k_mid, k_lo = pr.sem("k_rest_done"), pr.sem("k_mid_done"), pr.sem("k_lo_done")
        v_ready, v_done, v_out, m_in, s_mask = (pr.sem(x) for x in ("v_ready", "v_done", "v_out", "m_in", "s_mask"))
        k_out = [pr.sem(f"k_out{u}") for u in range(2 * DT)]
        CH = B * SK // 512
        NK = DT * CH
        NV = B * KT

        def tile_of(n):
            l, r = divmod(n, NK)
            return l, r // CH, r % CH

        with nc.Block() as block:

            @block.sync
            def _(sp):
                for l in range(2):
                    sp.dma_start(wk[:, l], t[f"wkT{l}"].rearrange("(t p) n -> p t n", p=P)).then_inc(w_in[l], 16)
                    sp.dma_start(bk[:, l], t[f"bk{l}"]).then_inc(w_in[l], 16)
                    if l == 0:
                        for i in range(4):
                            cols = slice(i * 512, (i + 1) * 512)
                            sp.dma_start(ctxT[:, :, cols],
                                         t["ctxT"][:, cols].rearrange("(t p) n -> p t n", p=P)).then_inc(ctx_in[i], 16)
                    sp.dma_start(wv[:, l], t[f"wvT{l}"].rearrange("(t p) n -> p t n", p=P)).then_inc(w_in[l], 16)
                    sp.dma_start(bv[:, l], t[f"bv{l}"].partition_broadcast(P)).then_inc(w_in[l], 16)
                    if l == 0:
                        sp.dma_start(mrow[:], t["mask"].rearrange("(t p) k -> p t k", p=P)).then_inc(m_in, 16)
                        sp.dma_start(mcol[:], t["maskT"].rearrange("(t p) k -> p t k", p=P)).then_inc(m_in, 16)
                sp.dma_start(pr.x[:], t["x"].rearrange("(t p) d -> p t d", p=P)).then_inc(x_in, 16)
                for l in range(2):
                    for dt in range(DT):
                        u = l * DT + dt
                        sp.wait_ge(k_hi, CH * (u + 1))
                        sp.wait_ge(k_mid, CH * (u + 1))
                        sp.wait_ge(k_lo, CH * (u + 1))
                        for part in range(3):
                            sp.dma_start(t["k_scr"][l, part, dt * P:(dt + 1) * P, :],
                                         parts[:, part, dt]).then_inc(k_out[u], 16)
                sp.wait_ge(v_done, NV * 2)
                sp.dma_start(t["v_scr"], vals1[:]).then_inc(v_out, 16)
                for u in range(2 * DT):
                    sp.wait_ge(k_out[u], 48)
                sp.wait_ge(v_out, 16)
                sp.wait_ge(x_in, 16)

            @block.gpsimd
            def _(pool):
                nc.gpsimd.memset(pr.ident[:], 0.0).then_inc(id_zero, 1)
                nc.gpsimd.memset(pr.lower[:], 1.0).then_inc(id_zero, 1)
                nc.gpsimd.memset(pr.ones[:], 1.0).then_inc(id_zero, 1)
                pool.wait_ge(id_zero, 3)
                nc.gpsimd.affine_select(out=pr.ident[:], in_=pr.ident[:], compare_op=ALU.not_equal, fill=1.0,
                                        base=0, pattern=[[-1, P]], channel_multiplier=1).then_inc(id_done, 1)
                nc.gpsimd.affine_select(out=pr.lower[:], in_=pr.lower[:], compare_op=ALU.is_gt, fill=0.0,
                                        base=0, pattern=[[1, P]], channel_multiplier=-1).then_inc(id_done, 1)
                pool.wait_ge(id_done, 2)
                nc.gpsimd.tensor_copy(pr.ident_bf[:], pr.ident[:]).then_inc(id_done, 1)
                nc.gpsimd.tensor_copy(pr.ident_r[:], pr.ident[:]).then_inc(id_done, 1)
                nc.gpsimd.iota(pr.desc[:], pattern=[[-1, 8]], base=8, channel_multiplier=0,
                               allow_small_or_imprecise_dtypes=True).then_inc(const_done, 1)
                nc.gpsimd.iota(pr.place[:], pattern=[[1, CAP]], base=0, channel_multiplier=0,
                               allow_small_or_imprecise_dtypes=True).then_inc(const_done, 1)
                nc.gpsimd.memset(m.V[0][:], 1.0).then_inc(const_done, 1)
                nc.gpsimd.memset(m.V[1][:], 1.0).then_inc(const_done, 1)
                pool.wait_ge(m_in, 32)
                nc.gpsimd.tensor_scalar(m.bias_hi[:], mcol[:].bitcast(U8), -BIG, None, ALU.mult).then_inc(s_mask, 1)
                nc.gpsimd.tensor_scalar(m.bias_rows[:], mrow[:].bitcast(U8), -BIG, None, ALU.mult).then_inc(s_mask, 1)
                pool.wait_ge(s_mask, 2)
                pool.wait_ge(const_done, 4)
                pool.wait_ge(id_done, 4)

            @block.tensor
            def _(pe):
                for l in range(2):
                    pe.wait_ge(w_in[l], 64)
                    for r in range(NK):
                        n = l * NK + r
                        _, dt, ch = tile_of(n)
                        if n < CH:
                            pe.wait_ge(ctx_in[ch], 16)
                        if n >= 4:
                            pe.wait_ge(k_hi, n - 3)
                        for k in range(DT):
                            mm = pe.matmul(kps[:, n % 4], wk[:, l, k, dt * P:(dt + 1) * P],
                                           ctxT[:, k, ch * 512:(ch + 1) * 512], start=(k == 0), stop=(k == DT - 1))
                        mm.then_inc(k_ready, 1)
                    for r in range(NV):
                        n = l * NV + r
                        if n >= 4:
                            pe.wait_ge(v_done, n - 3)
                        for k in range(DT):
                            mm = pe.matmul(vps[:, n % 4, 0:D], ctxT[:, k, r * P:(r + 1) * P],
                                           wv[:, l, k], start=(k == 0), stop=(k == DT - 1))
                        mm.then_inc(v_ready, 1)

            @block.scalar
            def _(act):
                def middle(n):
                    l, dt, ch = tile_of(n)
                    act.wait_ge(k_rest, n + 1)
                    nc.scalar.activation(parts[:, 1, dt, ch * 512:(ch + 1) * 512], rest[:, n % 2],
                                         ACT.Copy).then_inc(k_mid, 1)

                act.wait_ge(w_in[0], 64)
                act.wait_ge(w_in[1], 64)
                for n in range(2 * NK):
                    l, dt, ch = tile_of(n)
                    act.wait_ge(k_ready, n + 1)
                    if n >= 2:
                        act.wait_ge(k_rest, n - 1)
                    nc.scalar.activation(full[:, n % 2], kps[:, n % 4], ACT.Identity,
                                         bias=bk[:, l, dt:dt + 1]).then_inc(k_full, 1)
                    if l == 1 and ch == 0:
                        act.wait_ge(k_out[dt], 48)
                    nc.scalar.activation(parts[:, 0, dt, ch * 512:(ch + 1) * 512], kps[:, n % 4],
                                         ACT.Identity, bias=bk[:, l, dt:dt + 1]).then_inc(k_hi, 1)
                    if n % NK:
                        middle(n - 1)
                    if n % NK == NK - 1:
                        middle(n)

            @block.vector
            def _(dve):
                def low(n):
                    l, dt, ch = tile_of(n)
                    dve.wait_ge(k_mid, n + 1)
                    nc.vector.tensor_tensor(parts[:, 2, dt, ch * 512:(ch + 1) * 512], rest[:, n % 2],
                                            parts[:, 1, dt, ch * 512:(ch + 1) * 512],
                                            ALU.subtract).then_inc(k_lo, 1)

                stack_ones(pr, m, dve, 0, init)
                dve.wait_ge(init, 5)
                for l in range(2):
                    for r in range(NK):
                        n = l * NK + r
                        _, dt, ch = tile_of(n)
                        dve.wait_ge(k_full, n + 1)
                        dve.wait_ge(k_hi, n + 1)
                        if n >= 2:
                            dve.wait_ge(k_lo, n - 1)
                        nc.vector.tensor_tensor(rest[:, n % 2], full[:, n % 2],
                                                parts[:, 0, dt, ch * 512:(ch + 1) * 512],
                                                ALU.subtract).then_inc(k_rest, 1)
                        if r >= 1:
                            low(n - 1)
                    low(l * NK + NK - 1)
                    dve.wait_ge(w_in[l], 64)
                    for r in range(NV):
                        n = l * NV + r
                        dve.wait_ge(v_ready, n + 1)
                        nc.vector.tensor_tensor(vals[l][:, r], vps[:, n % 4, 0:D], bv[:, l],
                                                ALU.add).then_inc(v_done, 1)


class NormSteps:

    def __init__(self, pr, c, tag):
        self.pr, self.tag = pr, tag
        self.stats = pr.sb(c, f"{tag}_stats", [P, NT, 6], F32)
        self.mv = pr.sb(c, f"{tag}_mv", [P, NT, 2], F32)
        self.rstd = pr.sb(c, f"{tag}_rstd", [P, NT], F32)
        self.var = pr.sb(c, f"{tag}_var", [P, NT], F32)
        self.root = pr.sb(c, f"{tag}_root", [P, NT], F32)
        self.s_var, self.s_root = pr.sem(f"{tag}_var_done"), pr.sem(f"{tag}_root_done")
        self.s_stats, self.s_mv, self.s_rstd = (pr.sem(f"{tag}_{x}") for x in ("stats", "mv", "rstd"))
        self.s_y, self.s_tr, self.s_yT = (pr.sem(f"{tag}_{x}") for x in ("y", "tr", "yT"))

    def vector(self, dve):
        nc, pr = self.pr.nc, self.pr
        for i in range(NT):
            nc.vector.bn_stats(self.stats[:, i], pr.x[:, i]).then_inc(self.s_stats, 1)
        for i in range(NT):
            dve.wait_ge(self.s_stats, i + 1)
            nc.vector.bn_aggr(self.mv[:, i], self.stats[:, i]).then_inc(self.s_mv, 1)
        dve.wait_ge(self.s_root, 1)
        nc.vector.reciprocal(self.rstd[:], self.root[:]).then_inc(self.s_rstd, 1)
        dve.wait_ge(self.s_rstd, 1)
        nc.vector.tensor_tensor(self.root[:], self.rstd[:], self.rstd[:], ALU.mult).then_inc(self.s_rstd, 1)
        dve.wait_ge(self.s_rstd, 2)
        nc.vector.tensor_tensor(self.root[:], self.root[:], self.var[:], ALU.mult).then_inc(self.s_rstd, 1)
        dve.wait_ge(self.s_rstd, 3)
        nc.vector.tensor_scalar(self.root[:], self.root[:], -0.5, 1.5, ALU.mult, ALU.add).then_inc(self.s_rstd, 1)
        dve.wait_ge(self.s_rstd, 4)
        nc.vector.tensor_tensor(self.rstd[:], self.rstd[:], self.root[:], ALU.mult).then_inc(self.s_rstd, 1)
        dve.wait_ge(self.s_rstd, 5)
        for i in range(NT):
            nc.vector.tensor_scalar(pr.y[:, i], pr.x[:, i], self.mv[:, i, 0:1], self.rstd[:, i:i + 1],
                                    ALU.subtract, ALU.mult).then_inc(self.s_y, 1)

    def pool(self, pool):
        pool.wait_ge(self.s_mv, NT)
        self.pr.nc.gpsimd.tensor_scalar(self.var[:], self.mv[:, :, 1], EPS, None, ALU.add).then_inc(self.s_var, 1)

    def tensor(self, pe, ps):
        for j in range(NT // 2):
            pe.wait_ge(self.s_y, 2 * j + 2)
            if j >= 2:
                pe.wait_ge(self.s_yT, j - 1)
            for i in range(2):
                for k in range(DT):
                    mm = pe.transpose(ps[:, j % 2, (k * 2 + i) * P:(k * 2 + i + 1) * P],
                                      self.pr.y[:, 2 * j + i, k * P:(k + 1) * P], self.pr.ident[:])
            mm.then_inc(self.s_tr, 1)

    def scalar(self, act, ps):
        act.wait_ge(self.s_var, 1)
        self.pr.nc.scalar.activation(self.root[:], self.var[:], ACT.Sqrt).then_inc(self.s_root, 1)
        for j in range(NT // 2):
            act.wait_ge(self.s_tr, j + 1)
            self.pr.nc.scalar.activation(self.pr.yT[:, :, 2 * j * P:2 * (j + 1) * P],
                                         ps[:, j % 2].rearrange("p (k n) -> p k n", k=DT),
                                         ACT.Copy).then_inc(self.s_yT, 1)


def k_stack(pr, sp, l, m, i, b):
    for r in range(6):
        sp.dma_start(m.K[b][r * DH:(r + 1) * DH],
                     pr.t["k_scr"][l, K_PARTS[r], bass.ds(i * (HG * DH), HG * DH), b * SK:(b + 1) * SK]
                     .rearrange("(h d) k -> d h k", h=HG)).then_inc(m.load[b], 16)


def q_stack(pr, sp, l, m, i, b):
    for r in range(6):
        sp.dma_start(m.Q[b][r * DH:(r + 1) * DH],
                     pr.t["q_scr"][l, Q_PARTS[r], bass.ds(i * (HG * DH), HG * DH), b * SQ:(b + 1) * SQ]
                     .rearrange("(h d) k -> d h k", h=HG)).then_inc(m.load[b], 16)


def stack_ones(pr, m, dve, l, done):
    for b in range(B):
        pr.nc.vector.memset(m.K[b][STACK:ROWS], 1.0).then_inc(done, 1)
        pr.nc.vector.memset(m.Q[b][STACK:ROWS], 1.0).then_inc(done, 1)
    dve.wait_ge(done, 4)
    if l == 0:
        for b in range(B):
            ins = pr.nc.vector.memset(m.K[b][PADROW:PADROW + 1], 0.0)
        ins.then_inc(done, 1)
    else:
        dve.sem_inc(done, 1)


def prepare_attention(pr, c, l, m):
    nc, t = pr.nc, pr.t
    with pr.stage() as c:
        norm = NormSteps(pr, c, f"an{l}")
        wq = pr.sb(c, f"wq{l}", [P, DT, D], F32)
        bq = pr.sb(c, f"bq{l}", [P, DT], F32)
        bq4 = pr.sb(c, f"bq4{l}", [P, DT], F32)
        full = pr.sb(c, f"q_full{l}", [P, 2, 512], F32)
        rest = pr.sb(c, f"q_rest{l}", [P, 2, 512], F32)
        parts = pr.sb(c, f"q_parts{l}", [P, 3, DT, TOK], BF16)
        tps = pr.banks(c, f"tr_ps{l}", 2)
        qps = pr.banks(c, f"q_ps{l}", 4)
        if l == 1:
            padin = pr.sb(c, "pad_in", [1, B * SK // 4], U32)
            padbf = pr.sb(c, "pad_bf", [1, B, SK], BF16)
        w_in, m_in, v_in = pr.sem(f"wq_in{l}"), pr.sem(f"m_in{l}"), pr.sem(f"v_in{l}")
        b4, q_ready, q_full, q_hi = (pr.sem(f"{x}{l}") for x in ("bq4_", "q_ready", "q_full_", "q_hi"))
        q_rest, q_mid, q_lo, q_out = (pr.sem(f"{x}{l}") for x in ("q_rest_", "q_mid", "q_lo", "q_out"))
        s_pad, pad_out, s_mask, rows_in = (pr.sem(f"{x}{l}") for x in ("s_pad", "pad_out", "s_mask", "rows_in"))
        init, v_init = pr.sem(f"init{l}"), pr.sem(f"v_init{l}")
        b_hi, b_lo = pr.sem(f"b_hi{l}"), pr.sem(f"b_lo{l}")
        CH = TOK // 512
        NQ = DT * CH

        with nc.Block() as block:

            @block.sync
            def _(sp):
                sp.dma_start(wq[:], t[f"wqT{l}"].rearrange("(t p) n -> p t n", p=P)).then_inc(w_in, 16)
                sp.dma_start(bq[:], t[f"bq{l}"]).then_inc(w_in, 16)
                if l == 1:
                    sp.dma_start(m.bias_cols[:], t["amaskT"].rearrange("(t p) k -> p t k", p=P)).then_inc(m_in, 16)
                    sp.dma_start(padin[:], t["pad"].rearrange("b k -> (b k)").unsqueeze(0)).then_inc(m_in, 16)
                k_stack(pr, sp, l, m, 0, 0)
                k_stack(pr, sp, l, m, 0, 1)
                if l == 1:
                    sp.dma_start(m.vals[:], t["v_scr"]).then_inc(v_in, 16)
                    sp.dma_start(m.bias_rows[:], t["amask"].rearrange("(t p) k -> p t k", p=P)).then_inc(rows_in, 16)
                sp.dma_start(m.wo[:], t[f"woT{l}"].rearrange("(t p) n -> p t n", p=P)).then_inc(m.wo_in, 16)
                sp.dma_start(m.bo[:], t[f"bo{l}"].partition_broadcast(P)).then_inc(m.wo_in, 16)
                for dt in range(DT):
                    sp.wait_ge(q_hi, CH * (dt + 1))
                    sp.wait_ge(q_mid, CH * (dt + 1))
                    sp.wait_ge(q_lo, CH * (dt + 1))
                    for part in range(3):
                        sp.dma_start(t["q_scr"][l, part, dt * P:(dt + 1) * P, :], parts[:, part, dt]).then_inc(q_out, 16)
                sp.wait_ge(q_out, 16 * 3 * DT)
                q_stack(pr, sp, l, m, 0, 0)
                q_stack(pr, sp, l, m, 0, 1)
                if l == 1:
                    sp.wait_ge(s_pad, 1)
                    sp.wait_ge(init, 5)
                    for b in range(B):
                        for h in range(HG):
                            sp.dma_start(m.K[b][PADROW:PADROW + 1, h], padbf[:, b]).then_inc(pad_out, 16)
                    sp.wait_ge(pad_out, 16 * B * HG)
                    sp.wait_ge(v_in, 16)
                    sp.wait_ge(rows_in, 16)

            @block.gpsimd
            def _(pool):
                norm.pool(pool)
                if l == 1:
                    nc.gpsimd.memset(m.V[0][:], 1.0).then_inc(v_init, 1)
                    nc.gpsimd.memset(m.V[1][:], 1.0).then_inc(v_init, 1)
                    pool.wait_ge(m_in, 32)
                    nc.gpsimd.tensor_scalar(m.bias_cols[:], m.bias_cols[:], -BIG, None, ALU.max).then_inc(s_mask, 1)
                    nc.gpsimd.tensor_scalar(padbf[:].rearrange("p b k -> p (b k)"), padin[:].bitcast(U8), -BIG, None,
                                            ALU.mult).then_inc(s_pad, 1)
                    pool.wait_ge(v_init, 2)
                    pool.wait_ge(s_mask, 1)

            @block.tensor
            def _(pe):
                norm.tensor(pe, tps)
                pe.wait_ge(w_in, 32)
                pe.wait_ge(norm.s_yT, NT // 2)
                for n in range(NQ):
                    dt, ch = divmod(n, CH)
                    for k in range(DT):
                        mm = pe.matmul(qps[:, n % 4], wq[:, k, dt * P:(dt + 1) * P],
                                       pr.yT[:, k, ch * 512:(ch + 1) * 512], start=(k == 0), stop=(k == DT - 1))
                    mm.then_inc(q_ready, 1)

            @block.scalar
            def _(act):
                def middle(n):
                    dt, ch = divmod(n, CH)
                    act.wait_ge(q_rest, n + 1)
                    nc.scalar.activation(parts[:, 1, dt, ch * 512:(ch + 1) * 512], rest[:, n % 2],
                                         ACT.Copy).then_inc(q_mid, 1)

                norm.scalar(act, tps)
                act.wait_ge(w_in, 32)
                nc.scalar.activation(bq4[:], bq[:], ACT.Copy, scale=0.25).then_inc(b4, 1)
                act.wait_ge(b4, 1)
                for n in range(NQ):
                    dt, ch = divmod(n, CH)
                    act.wait_ge(q_ready, n + 1)
                    if n >= 2:
                        act.wait_ge(q_rest, n - 1)
                    nc.scalar.activation(full[:, n % 2], qps[:, n % 4], ACT.Identity, bias=bq4[:, dt:dt + 1],
                                         scale=0.25).then_inc(q_full, 1)
                    nc.scalar.activation(parts[:, 0, dt, ch * 512:(ch + 1) * 512], qps[:, n % 4], ACT.Identity,
                                         bias=bq4[:, dt:dt + 1], scale=0.25).then_inc(q_hi, 1)
                    if n >= 1:
                        middle(n - 1)
                middle(NQ - 1)
                if l == 1:
                    act.wait_ge(s_mask, 1)
                    nc.scalar.activation(m.bias_hi[:], m.bias_cols[:], ACT.Copy).then_inc(b_hi, 1)

            @block.vector
            def _(dve):
                def low(n):
                    dt, ch = divmod(n, CH)
                    dve.wait_ge(q_mid, n + 1)
                    nc.vector.tensor_tensor(parts[:, 2, dt, ch * 512:(ch + 1) * 512], rest[:, n % 2],
                                            parts[:, 1, dt, ch * 512:(ch + 1) * 512], ALU.subtract).then_inc(q_lo, 1)

                norm.vector(dve)
                if l == 1:
                    stack_ones(pr, m, dve, 1, init)
                for n in range(NQ):
                    dt, ch = divmod(n, CH)
                    dve.wait_ge(q_full, n + 1)
                    dve.wait_ge(q_hi, n + 1)
                    if n >= 2:
                        dve.wait_ge(q_lo, n - 1)
                    nc.vector.tensor_tensor(rest[:, n % 2], full[:, n % 2],
                                            parts[:, 0, dt, ch * 512:(ch + 1) * 512], ALU.subtract).then_inc(q_rest, 1)
                    if n >= 1:
                        low(n - 1)
                low(NQ - 1)
                if l == 1:
                    dve.wait_ge(b_hi, 1)
                    nc.vector.tensor_tensor(m.bias_lo[:], m.bias_cols[:], m.bias_hi[:].bitcast(F32),
                                            ALU.subtract).then_inc(b_lo, 1)
                    dve.wait_ge(b_lo, 1)


class Mem:
    pass


def attend(pr, l, m):
    nc, t = pr.nc, pr.t
    with pr.stage() as c:
        K, Q, V, load = m.K, m.Q, m.V, m.load
        prob = pr.sb(c, f"prob{l}", [P, 2, HG, SQ], F32)
        junk = pr.sb(c, f"junk{l}", [P, 2, 512], F32)
        mx = pr.sb(c, f"mx{l}", [P, 2, HG, QT, 2], F32)
        mneg = pr.sb(c, f"mneg{l}", [P, 2, 2 * QT], F32)
        mrest = pr.sb(c, f"mrest{l}", [P, 2, 2 * QT], F32)
        mpart = pr.sb(c, f"mpart{l}", [P, 2, 2 * QT, 4], BF16)
        s_ps = pr.banks(c, f"s_ps{l}", 2)
        st_ps = pr.banks(c, f"st_ps{l}", 4)
        o_ps = pr.banks(c, f"o_ps{l}", 1)
        m_ps = c.enter_context(nc.psum_tensor(f"m_ps{l}", [P, 1024], BF16))
        init, x_bias = pr.sem(f"mpart_init{l}"), pr.sem(f"x_bias{l}")
        s_ready, mx_done = pr.sem(f"s_ready{l}"), pr.sem(f"mx_done{l}")
        chain, mp_done, mt_done, mrow_done = (pr.sem(f"{x}{l}") for x in ("chain", "mp_done", "mt_done", "mrow_done"))
        st_ready, add_done, exp_done, pv_done = (pr.sem(f"{x}{l}") for x in ("st_ready", "add_done", "exp_done", "pv_done"))
        pool_step, dve_step = pr.sem(f"pool_step{l}"), pr.sem(f"dve_step{l}")
        evac_done, v_copied = (pr.sem(f"{x}{l}") for x in ("evac_done", "v_copied"))
        N_DMA = 12

        def on_pe(kt, hp):
            return l == 0 or hp == 0 or A_SPLIT[kt] > 0
        n_added = [sum(not on_pe(k, 1) for k in range(kt + 1)) for kt in range(KT)]

        def units(eng, unit):
            with eng.Fori(0, NG - 1) as i:
                for b in range(B):
                    unit(i, b, True)
            for b in range(B):
                unit(NG - 1, b, b == 0)

        def nxt(i, b):
            return i * 2 + b + 1, 1 - b

        def a_jobs(kt):
            first = sum(A_SPLIT[:kt])
            return range(first, first + A_SPLIT[kt])

        def passed(eng, step):
            eng.sem_inc(step, 1)

        with nc.Block() as block:

            @block.sync
            def _(sp):
                with sp.Fori(1, NG) as i:
                    for b in range(B):
                        sp.wait_ge(st_ready, (i * 2 + b - 1) * 16)
                        k_stack(pr, sp, l, m, i, b)
                        q_stack(pr, sp, l, m, i, b)

            @block.gpsimd
            def _(pool):
                nc.gpsimd.memset(mpart[:], 1.0).then_inc(init, 1)

                def values(u, i, b):
                    pool.wait_ge(evac_done, u + 1)
                    passed(pool, pool_step)
                    nc.gpsimd.tensor_copy(V[b][:, :, :, 0:DH],
                                          m.vals[:, b * KT:(b + 1) * KT, bass.ds(i * (HG * DH), HG * DH)]
                                          .rearrange("p k (h d) -> p k h d", h=HG)).then_inc(v_copied, 1)

                def half(u, b, c2):
                    hs = slice(2 * c2, 2 * c2 + 2)
                    n = (u * 2 + c2) * 4
                    pool.wait_ge(mx_done, u * 32 + 2 + 16 * (c2 + 1))
                    pool.wait_ge(mrow_done, u * 2 + c2 + 1)
                    passed(pool, pool_step)
                    nc.gpsimd.tensor_scalar(mneg[:, c2].rearrange("p (h q) -> p h q", h=2), mx[:, b, hs, :, 1], -BIG / 2, -1.0, ALU.max, ALU.mult).then_inc(chain, 1)
                    pool.wait_ge(chain, n + 1)
                    passed(pool, pool_step)
                    nc.gpsimd.tensor_copy(mpart[:, c2, :, 1], mneg[:, c2]).then_inc(chain, 1)
                    pool.wait_ge(chain, n + 2)
                    passed(pool, pool_step)
                    nc.gpsimd.tensor_tensor(mrest[:, c2], mneg[:, c2], mpart[:, c2, :, 1], ALU.subtract).then_inc(chain, 1)
                    pool.wait_ge(chain, n + 3)
                    passed(pool, pool_step)
                    nc.gpsimd.tensor_copy(mpart[:, c2, :, 2], mrest[:, c2]).then_inc(chain, 1)
                    pool.wait_ge(chain, n + 4)
                    passed(pool, pool_step)
                    nc.gpsimd.tensor_tensor(mpart[:, c2, :, 3], mrest[:, c2], mpart[:, c2, :, 2],
                                            ALU.subtract).then_inc(mp_done, 1)

                values(0, 0, 0)
                pool.wait_ge(init, 1)
                pool.wait_ge(m.wo_in, 32)
                nc.gpsimd.tensor_tensor(pr.x[:], pr.x[:], m.bo[:].unsqueeze(1).broadcast_to([P, NT, D]),
                                        ALU.add).then_inc(x_bias, 1)
                half(0, 0, 0)
                half(0, 0, 1)

                def unit(i, b, has_next):
                    if has_next:
                        u, nb = nxt(i, b)
                        values(u, i + b, nb)
                        half(u, nb, 0)
                        half(u, nb, 1)

                units(pool, unit)
                pool.wait_ge(x_bias, 1)

            @block.tensor
            def _(pe):
                pe.sem_inc(pv_done, 2)

                def row_scores(u, b, jobs):
                    for j in jobs:
                        h, half, qt = j // 8, j % 8 // 4, j % 4
                        pe.wait_ge(mx_done, u * 32 + j + 1)
                        pe.matmul(s_ps[:, j % 2], Q[b][0:MROW, h, qt * P:(qt + 1) * P],
                                  K[b][0:MROW, h, half * 512:(half + 1) * 512], start=True, stop=True).then_inc(s_ready, 1)

                def turn_max(u, b, c2):
                    pe.wait_ge(mp_done, u * 2 + c2 + 1)
                    pe.wait_ge(mrow_done, u * 2 + c2 + 2)
                    for k in range(2 * QT):
                        mm = pe.transpose(m_ps[STACK:ROWS, k * P:(k + 1) * P], mpart[:, c2, k], pr.ident_bf[:])
                    mm.then_inc(mt_done, 1)

                def col_scores(u, b, kt, hp):
                    n = u * 16 + kt * 2 + hp
                    slot = hp
                    pe.wait_ge(exp_done, n + 1)
                    for e in range(2):
                        h = 2 * hp + e
                        mm = pe.matmul(st_ps[:, 2 * slot + e], K[b][0:ROWS, h, kt * P:(kt + 1) * P], Q[b][0:ROWS, h],
                                       start=True, stop=not on_pe(kt, hp))
                        if on_pe(kt, hp):
                            layers = [m.bias_hi] if l == 0 else [m.bias_hi, m.bias_lo]
                            for x in layers:
                                mm = pe.matmul(st_ps[:, 2 * slot + e], (pr.ident_r if l else pr.ident_bf)[:], x[:, kt], start=False,
                                               stop=(x is layers[-1]))
                    mm.then_inc(st_ready, 1)

                def weigh(u, b, kt):
                    pe.wait_ge(exp_done, u * 16 + 2 * kt + 4)
                    if kt == 0:
                        pe.wait_ge(evac_done, u + 2)
                        pe.wait_ge(v_copied, u + 1)
                    for h in range(HG):
                        mm = pe.matmul(o_ps[32 * h:32 * h + 32, 0], V[b][:, kt, h], prob[:, kt % 2, h],
                                       start=(kt == 0), stop=(kt == KT - 1))
                    mm.then_inc(pv_done, 1)

                pe.wait_ge(load[0], 16 * N_DMA)
                row_scores(0, 0, range(16))
                row_scores(0, 0, range(16, 32))
                turn_max(0, 0, 0)
                turn_max(0, 0, 1)

                def unit(i, b, has_next):
                    u = i * 2 + b
                    un, nb = nxt(i, b)
                    for kt in range(KT):
                        jobs = list(a_jobs(kt)) if has_next else []
                        if kt == FIRST_A and has_next:
                            pe.wait_ge(load[nb], (i + b) * (16 * N_DMA) + 16 * N_DMA)
                        if kt == 0:
                            pe.wait_ge(mrow_done, u * 2 + 3)
                        col_scores(u, b, kt, 0)
                        row_scores(un, nb, jobs[:2])
                        if kt == 0:
                            pe.wait_ge(mrow_done, u * 2 + 4)
                        col_scores(u, b, kt, 1)
                        row_scores(un, nb, jobs[2:4])
                        if kt >= 1:
                            weigh(u, b, kt - 1)
                        row_scores(un, nb, jobs[4:])
                        if kt == 4 and has_next:
                            turn_max(un, nb, 0)
                    if has_next:
                        turn_max(un, nb, 1)
                    weigh(u, b, KT - 1)

                units(pe, unit)

            @block.scalar
            def _(act):
                nc.scalar.activation(prob[:, 0, 0, 0:8], pr.ones[:, 0:8], ACT.Copy).then_inc(exp_done, 2)
                nc.scalar.activation(prob[:, 0, 0, 8:16], pr.ones[:, 0:8], ACT.Copy).then_inc(evac_done, 2)
                nc.scalar.activation(prob[:, 0, 0, 16:24], pr.ones[:, 0:8], ACT.Copy).then_inc(mrow_done, 2)

                def max_row(u, b, c2):
                    act.wait_ge(mt_done, u * 2 + c2 + 1)
                    nc.scalar.activation(Q[b][STACK:ROWS, 2 * c2:2 * c2 + 2].rearrange("p h q -> p (h q)"),
                                         m_ps[STACK:ROWS, :], ACT.Copy).then_inc(mrow_done, 1)

                max_row(0, 0, 0)
                max_row(0, 0, 1)

                def unit(i, b, has_next):
                    u = i * 2 + b
                    un, nb = nxt(i, b)
                    for kt in range(KT):
                        for hp in range(2):
                            if hp == 0:
                                act.wait_ge(pv_done, u * 8 + kt + 1)
                            if on_pe(kt, hp):
                                act.wait_ge(st_ready, u * 16 + kt * 2 + hp + 1)
                            else:
                                act.wait_ge(add_done, u * n_added[-1] + n_added[kt])
                            nc.scalar.activation(prob[:, kt % 2, 2 * hp:2 * hp + 2], st_ps[:, 2 * hp:2 * hp + 2],
                                                 ACT.Exp).then_inc(exp_done, 1)
                        if kt == 4 and has_next:
                            max_row(un, nb, 0)
                    if has_next:
                        max_row(un, nb, 1)
                    act.wait_ge(pv_done, u * 8 + KT + 2)
                    nc.scalar.activation(m.out[:, bass.ds(i, 1), b], o_ps[:, 0], ACT.Copy).then_inc(evac_done, 1)

                units(act, unit)

            @block.vector
            def _(dve):
                nc.vector.memset(mx[:], 0.0).then_inc(mx_done, 2)

                def row_max(u, b, jobs):
                    for j in jobs:
                        h, half, qt = j // 8, j % 8 // 4, j % 4
                        dve.wait_ge(s_ready, u * 32 + j + 1)
                        rows = m.bias_rows
                        first = -4 * BIG
                        if half:
                            dve.wait_ge(mx_done, u * 32 + j + 1 - 4 + 2)
                            first = mx[:, b, h, qt, 0:1]
                        passed(dve, dve_step)
                        nc.vector.tensor_tensor_reduce(out=junk[:, j % 2], in0=s_ps[:, j % 2],
                                                       in1=rows[:, qt, half * 512:(half + 1) * 512],
                                                       scale=1.0, scalar=first, op0=ALU.add, op1=ALU.max,
                                                       accum_out=mx[:, b, h, qt, half:half + 1]).then_inc(mx_done, 1)

                row_max(0, 0, range(32))

                def unit(i, b, has_next):
                    u = i * 2 + b
                    un, nb = nxt(i, b)
                    for kt in range(KT):
                        jobs = list(a_jobs(kt)) if has_next else []
                        row_max(un, nb, jobs[:2])
                        if not on_pe(kt, 1):
                            dve.wait_ge(st_ready, u * 16 + kt * 2 + 2)
                            nc.vector.tensor_tensor(st_ps[:, 2:4], st_ps[:, 2:4],
                                                    m.bias_cols[:, kt].unsqueeze(1).broadcast_to([P, 2, SQ]),
                                                    ALU.add).then_inc(add_done, 1)
                        row_max(un, nb, jobs[2:])

                units(dve, unit)


def project(pr, l, m):
    nc = pr.nc
    with pr.stage() as c:
        sums = pr.sb(c, f"sums{l}", [P, 2, NH], F32)
        rec = pr.sb(c, f"rec{l}", [P, 2, NH], F32)
        o = pr.sb(c, f"o_tok{l}", [P, 2, D], F32)
        oT = pr.sb(c, f"o_T{l}", [P, 2, DT, P], F32)
        o_ps = pr.banks(c, f"o_tok_ps{l}", 3)
        t_ps = pr.banks(c, f"o_T_ps{l}", 2)
        y_ps = pr.banks(c, f"y_ps{l}", 2)
        o_ready, sum_done, rec_done, o_done = (pr.sem(f"{x}{l}") for x in ("o_ready", "sum_done", "rec_done", "o_done"))
        t_ready, t_done, y_ready, x_done = (pr.sem(f"{x}{l}") for x in ("t_ready", "t_done", "y_ready", "x_done"))

        with nc.Block() as block:

            @block.tensor
            def _(pe):
                def to_tokens(i):
                    b, q = divmod(i, QT)
                    if i >= 3:
                        pe.wait_ge(o_done, i - 2)
                    for g in range(NG):
                        mm = pe.transpose(o_ps[:, i % 3, g * P:(g + 1) * P], m.out[:, g, b, q * P:(q + 1) * P], pr.ident[:])
                    mm.then_inc(o_ready, 1)

                def back(i):
                    pe.wait_ge(o_done, i + 1)
                    if i >= 2:
                        pe.wait_ge(t_done, i - 1)
                    for k in range(DT):
                        mm = pe.transpose(t_ps[:, i % 2, k * P:(k + 1) * P], o[:, i % 2, k * P:(k + 1) * P], pr.ident[:])
                    mm.then_inc(t_ready, 1)

                def output(i):
                    pe.wait_ge(t_done, i + 1)
                    if i >= 2:
                        pe.wait_ge(x_done, i - 1)
                    for k in range(DT):
                        mm = pe.matmul(y_ps[:, i % 2, 0:D], oT[:, i % 2, k], m.wo[:, k], start=(k == 0), stop=(k == DT - 1))
                    mm.then_inc(y_ready, 1)

                to_tokens(0)
                to_tokens(1)
                pe.wait_ge(m.wo_in, 32)
                for i in range(NT):
                    if i + 2 < NT:
                        to_tokens(i + 2)
                    back(i)
                    if i >= 1:
                        output(i - 1)
                output(NT - 1)

            @block.scalar
            def _(act):
                for i in range(NT):
                    act.wait_ge(t_ready, i + 1)
                    if i >= 2:
                        act.wait_ge(y_ready, i - 1)
                    nc.scalar.activation(oT[:, i % 2], t_ps[:, i % 2, 0:D].rearrange("p (k n) -> p k n", k=DT),
                                         ACT.Copy).then_inc(t_done, 1)

            @block.vector
            def _(dve):
                def add(i):
                    dve.wait_ge(y_ready, i + 1)
                    nc.vector.tensor_tensor(pr.x[:, i], pr.x[:, i], y_ps[:, i % 2, 0:D], ALU.add).then_inc(x_done, 1)

                for i in range(NT):
                    heads = o_ps[:, i % 3].rearrange("p (h r) -> p h r", h=NH)
                    dve.wait_ge(o_ready, i + 1)
                    nc.vector.tensor_scalar(sums[:, i % 2], heads[:, :, DH], 1e-30 if l == 0 else 0.0, None,
                                            ALU.max).then_inc(sum_done, 1)
                    dve.wait_ge(sum_done, i + 1)
                    nc.vector.reciprocal(rec[:, i % 2], sums[:, i % 2]).then_inc(rec_done, 1)
                    dve.wait_ge(rec_done, i + 1)
                    if i >= 2:
                        dve.wait_ge(t_ready, i - 1)
                    nc.vector.tensor_tensor(o[:, i % 2].rearrange("p (h d) -> p h d", h=NH), heads[:, :, 0:DH],
                                            rec[:, i % 2].unsqueeze(2).broadcast_to([P, NH, DH]),
                                            ALU.mult).then_inc(o_done, 1)
                    if i >= 2:
                        add(i - 2)
                add(NT - 2)
                add(NT - 1)
                dve.wait_ge(x_done, NT)


def attention_memory(pr, c, l):
    m = Mem()
    m.vals = pr.sb(c, f"vals_all{l}", [P, B * KT, D], F32)
    m.bias_rows = pr.sb(c, f"bias_rows{l}", [P, QT, SK], F32)
    m.bias_hi = pr.sb(c, f"bias_hi{l}", [P, KT, SQ], F32R if l else BF16)
    if l == 1:
        m.bias_lo = pr.sb(c, "bias_lo", [P, KT, SQ], F32R)
        m.bias_cols = pr.sb(c, "bias_cols", [P, KT, SQ], F32)
    m.K = [pr.sb(c, f"k_stack{l}{b}", [P, HG, SK], BF16) for b in range(B)]
    m.Q = [pr.sb(c, f"q_stack{l}{b}", [P, HG, SQ], BF16) for b in range(B)]
    m.V = [pr.sb(c, f"v_unit{l}{b}", [P, KT, HG, 32], F32) for b in range(B)]
    m.wo = pr.sb(c, f"wo{l}", [P, DT, D], F32)
    m.bo = pr.sb(c, f"bo{l}", [P, D], F32)
    m.load, m.wo_in = [pr.sem(f"kq_in{l}{b}") for b in range(B)], pr.sem(f"wo_in{l}")
    return m


def attention_layer(pr, l):
    with pr.stage() as c:
        m = attention_memory(pr, c, l)
        if l == 0:
            setup(pr, m)
        prepare_attention(pr, c, l, m)
        m.out = pr.sb(c, f"o_all{l}", [P, NG, B, SQ], F32)
        attend(pr, l, m)
        project(pr, l, m)


def moe_capacity(pr):
    nc, t = pr.nc, pr.t
    HJ = [(j * P, min(P, H0 - j * P)) for j in range((H0 + P - 1) // P)]
    NJ = len(HJ)
    with pr.stage() as c:
        w0 = [pr.sb(c, f"w0_{s}", [P, DT, H0], F32) for s in range(2)]
        w1 = [pr.sb(c, f"w1_{s}", [P, DT, H0], F32) for s in range(2)]
        w2 = [pr.sb(c, f"w2_{s}", [P, NJ, D], F32) for s in range(2)]
        ein = pr.sb(c, "expert_in", [P, DT, E0, NT * CAP], F32)
        combT = pr.sb(c, "comb_T", [P, 2, TOK], F32)
        w_in = [pr.sem(f"w_in{s}") for s in range(2)]

        def load_weights(sp, e, s):
            sp.dma_start(w0[s][:], t["w0"][e].rearrange("(t p) h -> p t h", p=P)).then_inc(w_in[s], 16)
            sp.dma_start(w1[s][:], t["w1"][e].rearrange("(t p) h -> p t h", p=P)).then_inc(w_in[s], 16)
            full = (NJ - 1) * P
            sp.dma_start(w2[s][:, 0:NJ - 1], t["w2"][e, 0:full].rearrange("(j p) m -> p j m", p=P)).then_inc(w_in[s], 16)
            sp.dma_start(w2[s][0:H0 - full, NJ - 1], t["w2"][e, full:H0]).then_inc(w_in[s], 16)

        with pr.stage() as c1:
            norm = NormSteps(pr, c1, "fn0")
            rw = pr.sb(c1, "router", [P, DT, E0], F32)
            g3 = lambda name: pr.sb(c1, name, [P, NT, E0], F32)
            g2 = lambda name: pr.sb(c1, name, [P, NT], F32)
            raw, tmp, only, rest = g3("raw"), g3("gate_tmp"), g3("gate_only"), g3("gate_rest")
            first, second, amount = g3("first"), g3("second"), [g3("amount0"), g3("amount1")]
            top, low, gate, where = g2("top"), g2("low"), [g2("gate0"), g2("gate1")], g2("where")
            spot = [pr.sb(c1, f"spot{k}", [P, NT, CAP], F32) for k in range(2)]
            comb = pr.sb(c1, "comb", [P, NT, E0, CAP], F32)
            disp = pr.sb(c1, "disp", [P, NT, E0, CAP], F32)
            tps = pr.banks(c1, "ftr_ps", 2)
            rps = pr.banks(c1, "router_ps", 3)
            dps = pr.banks(c1, "disp_ps", 2)
            r_in, l_ready, x_sub, x_exp = pr.sem("r_in"), pr.sem("l_ready"), pr.sem("x_sub"), pr.sem("x_exp")
            g_step, m1_done, p1_ready, m1k_done, p2_ready = (
                pr.sem(x) for x in ("g_step", "m1_done", "p1_ready", "m1k_done", "p2_ready"))
            disp_done, ct_ready, ct_done, d_ready, d_done = (
                pr.sem(x) for x in ("disp_done", "ct_ready", "ct_done", "d_ready", "d_done"))

            with nc.Block() as block:

                @block.sync
                def _(sp):
                    sp.dma_start(rw[:], t["router"].rearrange("(t p) e -> p t e", p=P)).then_inc(r_in, 16)
                    load_weights(sp, 0, 0)
                    load_weights(sp, 1, 1)

                @block.gpsimd
                def _(pool):
                    norm.pool(pool)

                @block.tensor
                def _(pe):
                    norm.tensor(pe, tps)
                    pe.wait_ge(r_in, 16)
                    pe.wait_ge(norm.s_yT, NT // 2)
                    for g in range(NT):
                        for k in range(DT):
                            mm = pe.matmul(rps[:, 0, g * E0:(g + 1) * E0], pr.yT[:, k, g * P:(g + 1) * P], rw[:, k],
                                           start=(k == 0), stop=(k == DT - 1))
                    mm.then_inc(l_ready, 1)
                    pe.wait_ge(m1_done, 1)
                    pe.matmul(rps[:, 1, 0:NT * E0], pr.lower[:], first[:].rearrange("p g e -> p (g e)"),
                              start=True, stop=True).then_inc(p1_ready, 1)
                    pe.wait_ge(m1k_done, 1)
                    pe.matmul(rps[:, 2, 0:NT * E0], pr.lower[:], second[:].rearrange("p g e -> p (g e)"),
                              start=True, stop=False)
                    pe.matmul(rps[:, 2, 0:NT * E0], pr.ones[:], first[:].rearrange("p g e -> p (g e)"),
                              start=False, stop=True).then_inc(p2_ready, 1)
                    pe.wait_ge(disp_done, 2)
                    for g in range(NT):
                        if g >= 2:
                            pe.wait_ge(d_done, g - 1)
                        for k in range(DT):
                            mm = pe.matmul(dps[:, g % 2, k * 256:(k + 1) * 256], pr.y[:, g, k * P:(k + 1) * P],
                                           disp[:, g].rearrange("p e c -> p (e c)"), start=True, stop=True)
                        mm.then_inc(d_ready, 1)
                    for j in range(NT // 2):
                        if j >= 2:
                            pe.wait_ge(ct_done, j - 1)
                        for i in range(2):
                            for h in range(2):
                                mm = pe.transpose(tps[:, j % 2, (h * 2 + i) * P:(h * 2 + i + 1) * P],
                                                  comb[:, 2 * j + i, 4 * h:4 * h + 4].rearrange("p e c -> p (e c)"),
                                                  pr.ident[:])
                        mm.then_inc(ct_ready, 1)

                @block.scalar
                def _(act):
                    norm.scalar(act, tps)
                    act.wait_ge(x_sub, 1)
                    nc.scalar.activation(raw[:], raw[:], ACT.Exp).then_inc(x_exp, 1)
                    for g in range(NT):
                        act.wait_ge(d_ready, g + 1)
                        nc.scalar.activation(ein[:, :, :, g * CAP:(g + 1) * CAP],
                                             dps[:, g % 2].rearrange("p (k e c) -> p k e c", k=DT, e=E0),
                                             ACT.Copy).then_inc(d_done, 1)
                    act.wait_ge(d_done, NT)

                @block.vector
                def _(dve):
                    v = nc.vector
                    count = [0]

                    def link(ins):
                        count[0] += 1
                        ins.then_inc(g_step, 1)
                        dve.wait_ge(g_step, count[0])

                    over_e = lambda a: a.unsqueeze(2).broadcast_to([P, NT, E0])
                    order = pr.desc[:].unsqueeze(1).broadcast_to([P, NT, E0])

                    def best(src, one_hot):
                        link(v.tensor_reduce(top[:], src[:], AX.X, ALU.max))
                        link(v.tensor_tensor(tmp[:], src[:], over_e(top[:]), ALU.is_equal))
                        link(v.tensor_tensor(tmp[:], tmp[:], order, ALU.mult))
                        link(v.tensor_reduce(low[:], tmp[:], AX.X, ALU.max))
                        link(v.tensor_tensor(one_hot[:], order, over_e(low[:]), ALU.is_equal))

                    def keep(k, one_hot, counted):
                        link(v.tensor_scalar(tmp[:], counted, float(CAP), None, ALU.is_lt))
                        link(v.tensor_tensor(one_hot[:], one_hot[:], tmp[:], ALU.mult))
                        if k == 0:
                            v.tensor_copy(where[:], top[:]).then_inc(m1k_done, 1)
                        link(v.tensor_tensor(tmp[:], one_hot[:], counted, ALU.mult))
                        link(v.tensor_reduce(where[:], tmp[:], AX.X, ALU.add))
                        link(v.tensor_tensor(amount[k][:], one_hot[:], over_e(gate[k][:]), ALU.mult))
                        link(v.tensor_tensor(spot[k][:], pr.place[:].unsqueeze(1).broadcast_to([P, NT, CAP]),
                                             where[:].unsqueeze(2).broadcast_to([P, NT, CAP]), ALU.is_equal))

                    norm.vector(dve)
                    dve.wait_ge(l_ready, 1)
                    logits = rps[:, 0, 0:NT * E0].rearrange("p (g e) -> p g e", g=NT)
                    link(v.tensor_reduce(top[:], logits, AX.X, ALU.max))
                    v.tensor_tensor(raw[:], logits, over_e(top[:]), ALU.subtract).then_inc(x_sub, 1)
                    dve.wait_ge(x_exp, 1)
                    link(v.tensor_reduce(low[:], raw[:], AX.X, ALU.add))
                    link(v.reciprocal(low[:], low[:]))
                    link(v.tensor_tensor(raw[:], raw[:], over_e(low[:]), ALU.mult))
                    best(raw, first)
                    link(v.tensor_copy(gate[0][:], top[:]))
                    v.tensor_scalar(only[:], first[:], -1.0, 1.0, ALU.mult, ALU.add).then_inc(m1_done, 1)
                    dve.wait_ge(m1_done, 1)
                    link(v.tensor_tensor(rest[:], raw[:], only[:], ALU.mult))
                    best(rest, second)
                    link(v.tensor_copy(gate[1][:], top[:]))
                    dve.wait_ge(p1_ready, 1)
                    keep(0, first, rps[:, 1, 0:NT * E0].rearrange("p (g e) -> p g e", g=NT))
                    dve.wait_ge(p2_ready, 1)
                    keep(1, second, rps[:, 2, 0:NT * E0].rearrange("p (g e) -> p g e", g=NT))
                    for k, dst in enumerate((comb, disp)):
                        for g in range(NT):
                            ins = v.tensor_tensor(dst[:, g], amount[k][:, g].unsqueeze(2).broadcast_to([P, E0, CAP]),
                                                  spot[k][:, g].unsqueeze(1).broadcast_to([P, E0, CAP]), ALU.mult)
                    link(ins)
                    v.tensor_tensor(comb[:], comb[:], disp[:], ALU.add).then_inc(disp_done, 1)
                    dve.wait_ge(disp_done, 1)
                    v.tensor_scalar(disp[:], comb[:], 0.0, None, ALU.not_equal).then_inc(disp_done, 1)
                    for j in range(NT // 2):
                        dve.wait_ge(ct_ready, j + 1)
                        v.tensor_copy(combT[:, :, 2 * j * P:2 * (j + 1) * P],
                                      tps[:, j % 2].rearrange("p (h n) -> p h n", h=2)).then_inc(ct_done, 1)
                    dve.wait_ge(ct_done, NT // 2)

        hid = pr.sb(c, "hid", [P, NJ, NT * CAP], F32)
        act_out = pr.sb(c, "gelu_out", [P, 4, NT * CAP], F32)
        eout = pr.sb(c, "expert_out", [P, E0, 2, D], F32)
        ec = pr.sb(c, "expert_places", [P, NT, 2, D], F32)
        h_ps = pr.banks(c, "h_ps", 4)
        e_ps = pr.banks(c, "e_ps", 2)
        y_ps = pr.banks(c, "moe_y_ps", 2)
        h_ready, gelu_done, hid_done, e_ready = (pr.sem(x) for x in ("h_ready", "gelu_done", "hid_done", "e_ready"))
        e_copied, e_out, ec_in, y_ready, y_done = (pr.sem(x) for x in ("e_copied", "e_out", "ec_in", "my_ready", "my_done"))

        with nc.Block() as block:

            @block.sync
            def _(sp):
                def results_out(e):
                    sp.wait_ge(e_copied, e + 3)
                    sp.dma_start(t["e_scr"][e].rearrange("(r p) m -> p r m", p=P), eout[:, e]).then_inc(e_out, 16)

                with sp.Fori(1, E0 // 2) as i:
                    for s in range(2):
                        sp.wait_ge(e_ready, i * 2 + s - 1)
                        load_weights(sp, i * 2 + s, s)
                for e in range(E0):
                    results_out(e)
                sp.wait_ge(e_out, 16 * E0)
                for e in range(E0):
                    sp.dma_start(ec[CAP * (e % 4):CAP * (e % 4 + 1), :, e // 4],
                                 t["e_scr"][e].rearrange("(g c) m -> c g m", c=CAP)).then_inc(ec_in, 16)

            @block.tensor
            def _(pe):
                with pe.Fori(0, E0 // 2) as i:
                    for s in range(2):
                        e = i * 2 + s
                        pe.wait_ge(w_in[s], i * 64 + 64)
                        for j, (h0, hn) in enumerate(HJ):
                            if j >= 4:
                                pe.wait_ge(hid_done, e * NJ + j - 3)
                            for w, off in ((w0[s], 0), (w1[s], 256)):
                                for k in range(DT):
                                    mm = pe.matmul(h_ps[0:hn, j % 4, off:off + 256], w[:, k, h0:h0 + hn],
                                                   ein[:, k, bass.ds(e, 1)],
                                                   start=(k == 0), stop=(k == DT - 1))
                            mm.then_inc(h_ready, 1)
                        pe.wait_ge(e_copied, e + 1)
                        for r in range(2):
                            for j, (h0, hn) in enumerate(HJ):
                                if r == 0:
                                    pe.wait_ge(hid_done, e * NJ + j + 1)
                                mm = pe.matmul(e_ps[:, s, r * 256:(r + 1) * 256], hid[0:hn, j, r * P:(r + 1) * P],
                                               w2[s][0:hn, j], start=(j == 0), stop=(j == NJ - 1))
                        mm.then_inc(e_ready, 1)
                pe.wait_ge(ec_in, 16 * E0)
                for g in range(NT):
                    if g >= 2:
                        pe.wait_ge(y_done, g - 1)
                    for h in range(2):
                        mm = pe.matmul(y_ps[:, g % 2, 0:D], combT[:, h, g * P:(g + 1) * P], ec[:, g, h],
                                       start=(h == 0), stop=(h == 1))
                    mm.then_inc(y_ready, 1)

            @block.scalar
            def _(act):
                with act.Fori(0, E0 // 2) as i:
                    for s in range(2):
                        e = i * 2 + s
                        for j, (h0, hn) in enumerate(HJ):
                            act.wait_ge(h_ready, e * NJ + j + 1)
                            if j >= 4:
                                act.wait_ge(hid_done, e * NJ + j - 3)
                            nc.scalar.activation(act_out[0:hn, j % 4], h_ps[0:hn, j % 4, 0:256],
                                                 ACT.Gelu_apprx_tanh).then_inc(gelu_done, 1)

            @block.vector
            def _(dve):
                nc.vector.memset(eout[:, :, :, 0:1], 0.0).then_inc(e_copied, 2)
                with dve.Fori(0, E0 // 2) as i:
                    for s in range(2):
                        e = i * 2 + s
                        for j, (h0, hn) in enumerate(HJ):
                            dve.wait_ge(gelu_done, e * NJ + j + 1)
                            nc.vector.tensor_tensor(hid[0:hn, j], act_out[0:hn, j % 4], h_ps[0:hn, j % 4, 256:512],
                                                    ALU.mult).then_inc(hid_done, 1)
                        dve.wait_ge(e_ready, e + 1)
                        nc.vector.tensor_copy(eout[:, bass.ds(e, 1)].rearrange("p o r m -> p (o r m)"),
                                              e_ps[:, s]).then_inc(e_copied, 1)
                for g in range(NT):
                    dve.wait_ge(y_ready, g + 1)
                    nc.vector.tensor_tensor(pr.x[:, g], pr.x[:, g], y_ps[:, g % 2, 0:D], ALU.add).then_inc(y_done, 1)
                dve.wait_ge(y_done, NT)


def moe_top2(pr):
    nc, t = pr.nc, pr.t
    with pr.stage() as c:
        wg = pr.sb(c, "wg", [P, 2, DT, I1], F32)
        wu = pr.sb(c, "wu", [P, 2, DT, I1], F32)
        wd = pr.sb(c, "wd", [P, 2, I1 // P, D], F32)
        rows = pr.sb(c, "row_token", [P, TILES], U32)
        slots = pr.sb(c, "token_row", [P, 2, NT], U32)
        share = [pr.sb(c, f"share{k}", [P, NT], F32) for k in range(2)]
        table = pr.sb(c, "tile_table", [P, 2 * TILES + E1], I32)
        w_in = [pr.sem(f"w1_in{s}") for s in range(2)]

        def load_weights(sp, e, s):
            sp.dma_start(wg[:, s], t["gateT"][e].rearrange("(t p) i -> p t i", p=P)).then_inc(w_in[s], 16)
            sp.dma_start(wu[:, s], t["upT"][e].rearrange("(t p) i -> p t i", p=P)).then_inc(w_in[s], 16)
            sp.dma_start(wd[:, s], t["downT"][e].rearrange("(t p) d -> p t d", p=P)).then_inc(w_in[s], 16)

        with pr.stage() as c1:
            norm = NormSteps(pr, c1, "fn1")
            cw = pr.sb(c1, "conf_w", [P, DT, E1], F32)
            cb = pr.sb(c1, "conf_b", [P, E1], F32)
            wealth = pr.sb(c1, "wealth", [P, E1], F32)
            g3 = lambda name: pr.sb(c1, name, [P, NT, E1], F32)
            g2 = lambda name: pr.sb(c1, name, [P, NT], F32)
            g1 = lambda name: pr.sb(c1, name, [P, E1], F32)
            bids, tmp, chosen, rank, rest = g3("bids"), g3("bid_tmp"), g3("chosen"), g3("rank"), g3("bid_rest")
            one = [g3("one_hot0"), g3("one_hot1")]
            top, low = [g2("bid0"), g2("bid1")], g2("bid_low")
            place, full, tile_no, slot_f = g2("place_in"), g2("full_tiles"), g2("tile_no"), g2("slot_f")
            place_k = [g2("place0"), g2("place1")]
            count, tiles, end, start = g1("count"), g1("tiles"), g1("end"), g1("start")
            steps = pr.sb(c1, "steps", [P, 8], F32)
            big = pr.sb(c1, "compare", [P, TILES, 8], F32)
            line = pr.sb(c1, "line", [P, P], F32)
            token = pr.sb(c1, "token_no", [P, NT], F32)
            expert = pr.sb(c1, "expert_of", [P, TILES], F32)
            odd = pr.sb(c1, "odd", [P, TILES], F32)
            hot_row = pr.sb(c1, "hot_row", [P, 2 * NT, P], F32)
            hot_tile = pr.sb(c1, "hot_tile", [P, 2 * NT, TILES], F32)
            tps = pr.banks(c1, "gtr_ps", 2)
            rps = pr.banks(c1, "bid_ps", 3)
            ips = pr.banks(c1, "row_ps", 1)
            c_in, y_out, iota_done, l_ready, z_done, sig_done = (
                pr.sem(x) for x in ("c_in", "y_out", "iota_done", "bl_ready", "z_done", "sig_done"))
            b_step, c_done, r_ready, diff_done, exp_done, hot_done, i_ready = (
                pr.sem(x) for x in ("b_step", "c_done", "r_ready", "diff_done", "bexp_done", "hot_done", "i_ready"))

            with nc.Block() as block:

                @block.sync
                def _(sp):
                    sp.dma_start(cw[:], t["confT"].rearrange("(t p) e -> p t e", p=P)).then_inc(c_in, 16)
                    sp.dma_start(cb[:], t["conf_b"].partition_broadcast(P)).then_inc(c_in, 16)
                    sp.dma_start(wealth[:], t["wealth"].partition_broadcast(P)).then_inc(c_in, 16)
                    load_weights(sp, 0, 0)
                    load_weights(sp, 1, 1)
                    sp.wait_ge(norm.s_y, NT)
                    sp.dma_start(t["y_scr"].rearrange("(t p) d -> p t d", p=P), pr.y[:]).then_inc(y_out, 16)
                    sp.wait_ge(y_out, 16)

                @block.gpsimd
                def _(pool):
                    g = nc.gpsimd
                    loose = dict(allow_small_or_imprecise_dtypes=True)
                    g.iota(steps[:], pattern=[[P, 8]], base=0, channel_multiplier=0, **loose).then_inc(iota_done, 1)
                    g.iota(line[:], pattern=[[1, P]], base=0, channel_multiplier=0, **loose).then_inc(iota_done, 1)
                    g.iota(token[:], pattern=[[P, NT]], base=0, channel_multiplier=1, **loose).then_inc(iota_done, 1)
                    norm.pool(pool)

                @block.tensor
                def _(pe):
                    norm.tensor(pe, tps)
                    pe.wait_ge(c_in, 48)
                    pe.wait_ge(norm.s_yT, NT // 2)
                    for g in range(NT):
                        for k in range(DT):
                            mm = pe.matmul(rps[:, 0, g * E1:(g + 1) * E1], pr.yT[:, k, g * P:(g + 1) * P], cw[:, k],
                                           start=(k == 0), stop=(k == DT - 1))
                    mm.then_inc(l_ready, 1)
                    pe.wait_ge(c_done, 1)
                    flat = chosen[:].rearrange("p g e -> p (g e)")
                    pe.matmul(rps[:, 1, 0:NT * E1], pr.lower[:], flat, start=True, stop=True)
                    pe.matmul(rps[:, 2, 0:NT * E1], pr.ones[:], flat, start=True, stop=True).then_inc(r_ready, 1)
                    pe.wait_ge(hot_done, 1)
                    for n in range(2 * NT):
                        mm = pe.matmul(ips[:, 0, 0:TILES], hot_row[:, n], hot_tile[:, n],
                                       start=(n == 0), stop=(n == 2 * NT - 1))
                    mm.then_inc(i_ready, 1)

                @block.scalar
                def _(act):
                    norm.scalar(act, tps)
                    act.wait_ge(z_done, 1)
                    nc.scalar.activation(bids[:], bids[:], ACT.Sigmoid).then_inc(sig_done, 1)
                    act.wait_ge(diff_done, 1)
                    nc.scalar.activation(low[:], low[:], ACT.Exp).then_inc(exp_done, 1)

                @block.vector
                def _(dve):
                    v = nc.vector
                    n_links = [0]

                    def link(ins):
                        n_links[0] += 1
                        ins.then_inc(b_step, 1)
                        dve.wait_ge(b_step, n_links[0])

                    wide = lambda a: a.unsqueeze(2).broadcast_to([P, NT, E1])
                    by_e = lambda a: a.unsqueeze(1).broadcast_to([P, NT, E1])

                    def best(src, value, one_hot):
                        link(v.tensor_reduce(value[:], src[:], AX.X, ALU.max))
                        link(v.tensor_tensor(tmp[:], src[:], wide(value[:]), ALU.is_equal))
                        link(v.tensor_tensor(tmp[:], tmp[:], by_e(pr.desc[:]), ALU.mult))
                        link(v.tensor_reduce(low[:], tmp[:], AX.X, ALU.max))
                        link(v.tensor_tensor(one_hot[:], by_e(pr.desc[:]), wide(low[:]), ALU.is_equal))

                    norm.vector(dve)
                    dve.wait_ge(l_ready, 1)
                    v.tensor_tensor(bids[:], rps[:, 0, 0:NT * E1].rearrange("p (g e) -> p g e", g=NT), by_e(cb[:]),
                                    ALU.add).then_inc(z_done, 1)
                    dve.wait_ge(sig_done, 1)
                    link(v.tensor_tensor(bids[:], bids[:], by_e(wealth[:]), ALU.mult))
                    best(bids, top[0], one[0])
                    link(v.tensor_scalar(tmp[:], one[0][:], -1.0, 1.0, ALU.mult, ALU.add))
                    link(v.tensor_tensor(rest[:], bids[:], tmp[:], ALU.mult))
                    link(v.scalar_tensor_tensor(out=rest[:], in0=one[0][:], scalar=-BIG, in1=rest[:],
                                                op0=ALU.mult, op1=ALU.add))
                    best(rest, top[1], one[1])
                    v.tensor_tensor(chosen[:], one[0][:], one[1][:], ALU.add).then_inc(c_done, 1)
                    v.tensor_tensor(low[:], top[1][:], top[0][:], ALU.subtract).then_inc(diff_done, 1)
                    dve.wait_ge(exp_done, 1)
                    link(v.tensor_scalar(slot_f[:], low[:], 1.0, None, ALU.add))
                    link(v.reciprocal(share[0][:], slot_f[:]))
                    link(v.tensor_tensor(share[1][:], low[:], share[0][:], ALU.mult))
                    dve.wait_ge(r_ready, 1)
                    link(v.memset(count[:], 0.0))
                    for g in range(NT):
                        link(v.tensor_tensor(rank[:, g], rps[:, 1, g * E1:(g + 1) * E1], count[:], ALU.add))
                        link(v.tensor_tensor(count[:], count[:], rps[:, 2, g * E1:(g + 1) * E1], ALU.add))
                    dve.wait_ge(iota_done, 3)
                    grid = big[:, 0:E1]
                    link(v.tensor_tensor(grid, count[:].unsqueeze(2).broadcast_to([P, E1, 8]),
                                         steps[:].unsqueeze(1).broadcast_to([P, E1, 8]), ALU.is_gt))
                    link(v.tensor_reduce(tiles[:], grid, AX.X, ALU.add))
                    link(v.tensor_copy(end[:, 0:1], tiles[:, 0:1]))
                    for e in range(1, E1):
                        link(v.tensor_tensor(end[:, e:e + 1], end[:, e - 1:e], tiles[:, e:e + 1], ALU.add))
                    link(v.tensor_tensor(start[:], end[:], tiles[:], ALU.subtract))
                    link(v.tensor_tensor(big[:, :, 0:7], end[:, 0:7].unsqueeze(1).broadcast_to([P, TILES, 7]),
                                         line[:, 0:TILES].unsqueeze(2).broadcast_to([P, TILES, 7]), ALU.is_le))
                    link(v.tensor_reduce(expert[:], big[:, :, 0:7], AX.X, ALU.add))
                    link(v.tensor_tensor(big[:, :, 0:4], expert[:].unsqueeze(2).broadcast_to([P, TILES, 4]),
                                         line[:, 1:8:2].unsqueeze(1).broadcast_to([P, TILES, 4]), ALU.is_equal))
                    link(v.tensor_reduce(odd[:], big[:, :, 0:4], AX.X, ALU.add))
                    link(v.tensor_copy(table[:, 0:TILES], odd[:]))
                    link(v.tensor_scalar(table[:, TILES:2 * TILES], expert[:], 1.0, None, ALU.add))
                    link(v.tensor_scalar(table[:, 2 * TILES:], end[:], 1.0, None, ALU.add))
                    for k in range(2):
                        link(v.tensor_tensor(tmp[:], one[k][:], rank[:], ALU.mult))
                        link(v.tensor_reduce(place[:], tmp[:], AX.X, ALU.add))
                        link(v.tensor_tensor(tmp[:, :, 0:7], place[:].unsqueeze(2).broadcast_to([P, NT, 7]),
                                             steps[:, 1:8].unsqueeze(1).broadcast_to([P, NT, 7]), ALU.is_ge))
                        link(v.tensor_reduce(full[:], tmp[:, :, 0:7], AX.X, ALU.add))
                        link(v.tensor_tensor(tmp[:], one[k][:], by_e(start[:]), ALU.mult))
                        link(v.tensor_reduce(tile_no[:], tmp[:], AX.X, ALU.add))
                        link(v.scalar_tensor_tensor(out=slot_f[:], in0=tile_no[:], scalar=float(P), in1=place[:],
                                                    op0=ALU.mult, op1=ALU.add))
                        link(v.tensor_copy(slots[:, k], slot_f[:]))
                        link(v.tensor_tensor(tile_no[:], tile_no[:], full[:], ALU.add))
                        link(v.scalar_tensor_tensor(out=place_k[k][:], in0=full[:], scalar=-float(P), in1=place[:],
                                                    op0=ALU.mult, op1=ALU.add))
                        link(v.tensor_tensor(hot_row[:, k * NT:(k + 1) * NT],
                                             place_k[k][:].unsqueeze(2).broadcast_to([P, NT, P]),
                                             line[:].unsqueeze(1).broadcast_to([P, NT, P]), ALU.is_equal))
                        mine = hot_tile[:, k * NT:(k + 1) * NT]
                        link(v.tensor_tensor(mine, tile_no[:].unsqueeze(2).broadcast_to([P, NT, TILES]),
                                             line[:, 0:TILES].unsqueeze(1).broadcast_to([P, NT, TILES]), ALU.is_equal))
                        ins = v.tensor_tensor(mine, mine, token[:].unsqueeze(2).broadcast_to([P, NT, TILES]), ALU.mult)
                        if k == 0:
                            link(ins)
                    ins.then_inc(hot_done, 1)
                    dve.wait_ge(i_ready, 1)
                    link(v.tensor_copy(rows[:], ips[:, 0, 0:TILES]))

        now = pr.sb(c, "rows_now", [P, 2], U32)
        xg = pr.sb(c, "xg", [P, 2, D], F32)
        xgT = pr.sb(c, "xg_T", [P, DT, P], F32)
        silu = pr.sb(c, "silu", [P, 2, 512], F32)
        prod = pr.sb(c, "silu_up", [P, 2, 512], F32)
        prodT = pr.sb(c, "silu_up_T", [P, 8, P], F32)
        y_all = pr.sb(c, "y_all", [P, TILES, D], F32)
        back = pr.sb(c, "y_back", [P, NT, 2, D], F32)
        gu_ps = pr.banks(c, "gu_ps", 4)
        tr_ps = pr.banks(c, "pt_ps", 2)
        xt_ps = pr.banks(c, "xt_ps", 1)
        y_ps = pr.banks(c, "y2_ps", 1)
        xg_in = [pr.sem(f"xg_in{s}") for s in range(2)]
        ready, pool_step, now_done, xt_ready, xT_done = (
            pr.sem(x) for x in ("weights_ready", "pool_step", "now_done", "xt_ready", "xT_done"))
        g_ready, u_ready, silu_done, prod_done, tr_ready = (
            pr.sem(x) for x in ("g_ready", "u_ready", "silu_done", "prod_done", "tr_ready"))
        pT_done = [pr.sem("pT_done0"), pr.sem("pT_done1")]
        y_ready, y_copied, y_sent, x_done = (pr.sem(x) for x in ("y2_ready", "y2_copied", "y2_sent", "x2_done"))
        back_in = [pr.sem(f"back_in{g}") for g in range(NT)]

        def tiles_of(eng, tile):
            with eng.Fori(0, TILES // 2) as i:
                for s in range(2):
                    tile(i * 2 + s, i, s, True)
            tile(TILES - 1, TILES // 2, 0, False)

        with nc.Block() as block:

            @block.sync
            def _(sp):
                def arrived(n, s):
                    sp.wait_ge(w_in[s], n * 48 + 48)
                    sp.sem_inc(ready, 1)

                arrived(0, 0)
                with sp.Fori(1, E1 // 2) as i:
                    for s in range(2):
                        last = sp.value_load(table[0:1, bass.ds(i * 2 + s - 2 + 2 * TILES, 1)], min_val=1, max_val=TILES + 1)
                        sp.wait_ge(y_ready, last)
                        load_weights(sp, i * 2 + s, s)
                        arrived(i - 1 + s, 1 - s)
                arrived(E1 // 2 - 1, 1)

            @block.gpsimd
            def _(pool):
                def fetch(T, s):
                    pool.wait_ge(xt_ready, T + 1)
                    pool.sem_inc(pool_step, 1)
                    nc.gpsimd.tensor_copy(now[:, s:s + 1], rows[:, bass.ds(T, 1)]).then_inc(now_done, 1)
                    pool.wait_ge(now_done, T + 1)
                    pool.sem_inc(pool_step, 1)
                    pool.indirect_dma_start(out=xg[:, s], out_offset=None, in_=t["y_scr"],
                                            in_offset=bass.IndirectOffsetOnAxis(ap=now[:, s:s + 1], axis=0),
                                            bounds_check=TOK - 1).then_inc(xg_in[s], 16)

                tiles_of(pool, lambda T, i, s, has_next: fetch(T, s))
                pool.wait_ge(y_sent, 16 * TILES)
                for g in range(NT):
                    for k in range(2):
                        pool.indirect_dma_start(out=back[:, g, k], out_offset=None, in_=t["row_scr"],
                                                in_offset=bass.IndirectOffsetOnAxis(ap=slots[:, k, g:g + 1], axis=0),
                                                bounds_check=TILES * P - 1).then_inc(back_in[g], 16)

            @block.tensor
            def _(pe):
                pe.sem_inc(xt_ready, 2)
                pe.sem_inc(y_ready, 1)

                def turn_x(T, i, s):
                    pe.wait_ge(xg_in[s], i * 16 + 16)
                    for k in range(DT):
                        mm = pe.transpose(xt_ps[:, 0, k * P:(k + 1) * P], xg[:, s, k * P:(k + 1) * P], pr.ident[:])
                    mm.then_inc(xt_ready, 1)

                def up(w, slot, bank, h, done):
                    for k in range(DT):
                        mm = pe.matmul(gu_ps[:, bank], xgT[:, k], w[:, bass.ds(slot, 1), k, h * 512:(h + 1) * 512],
                                       start=(k == 0), stop=(k == DT - 1))
                    mm.then_inc(done, 1)

                def turn_prod(T, h):
                    pe.wait_ge(prod_done, T * 2 + h + 3)
                    for j in range(4):
                        mm = pe.transpose(tr_ps[:, h, j * P:(j + 1) * P], prod[:, h, j * P:(j + 1) * P], pr.ident[:])
                    mm.then_inc(tr_ready, 1)

                def down(T, slot, h):
                    pe.wait_ge(pT_done[h], T + 1)
                    if h == 0:
                        pe.wait_ge(y_copied, T + 1)
                    for j in range(4 * h, 4 * h + 4):
                        mm = pe.matmul(y_ps[:, 0, 0:D], prodT[:, j], wd[:, bass.ds(slot, 1), j],
                                       start=(j == 0), stop=(j == 7))
                    if h == 1:
                        mm.then_inc(y_ready, 1)

                def tile(T, i, s, has_next):
                    slot = pe.value_load(table[0:1, bass.ds(T, 1)], min_val=0, max_val=1)
                    need = pe.value_load(table[0:1, bass.ds(T + TILES, 1)], min_val=1, max_val=E1)
                    pe.wait_ge(ready, need)
                    pe.wait_ge(xT_done, T + 1)
                    pe.wait_ge(prod_done, T * 2 + 1)
                    up(wg, slot, 0, 0, g_ready)
                    up(wu, slot, 1, 0, u_ready)
                    pe.wait_ge(prod_done, T * 2 + 2)
                    up(wg, slot, 2, 1, g_ready)
                    turn_prod(T, 0)
                    up(wu, slot, 3, 1, u_ready)
                    down(T, slot, 0)
                    turn_prod(T, 1)
                    if has_next:
                        turn_x(T + 1, i + s, 1 - s)
                    down(T, slot, 1)

                turn_x(0, 0, 0)
                tiles_of(pe, tile)

            @block.scalar
            def _(act):
                def tile(T, i, s, has_next):
                    for h in range(2):
                        act.wait_ge(g_ready, T * 2 + h + 1)
                        nc.scalar.activation(silu[:, h], gu_ps[:, 2 * h], ACT.Silu).then_inc(silu_done, 1)
                    act.wait_ge(tr_ready, T * 2 + 2)
                    nc.scalar.activation(prodT[:, 4:8], tr_ps[:, 1].rearrange("p (j n) -> p j n", j=4),
                                         ACT.Copy).then_inc(pT_done[1], 1)
                    act.wait_ge(y_ready, T + 2)
                    nc.scalar.activation(y_all[:, bass.ds(T, 1)], y_ps[:, 0, 0:D], ACT.Copy).then_inc(y_copied, 1)
                    act.wait_ge(y_copied, T + 2)
                    act.dma_start(t["row_scr"][bass.ds(T * P, P)], y_all[:, bass.ds(T, 1)]
                                  .rearrange("p o d -> p (o d)")).then_inc(y_sent, 16)

                act.sem_inc(y_copied, 1)
                tiles_of(act, tile)

            @block.vector
            def _(dve):
                def turn_x_out(T):
                    dve.wait_ge(xt_ready, T + 3)
                    nc.vector.tensor_copy(xgT[:], xt_ps[:, 0, 0:D].rearrange("p (k n) -> p k n", k=DT)).then_inc(xT_done, 1)

                def multiply(T, h):
                    dve.wait_ge(silu_done, T * 2 + h + 1)
                    dve.wait_ge(u_ready, T * 2 + h + 1)
                    nc.vector.tensor_tensor(prod[:, h], silu[:, h], gu_ps[:, 2 * h + 1], ALU.mult).then_inc(prod_done, 1)

                def tile(T, i, s, has_next):
                    multiply(T, 0)
                    dve.wait_ge(tr_ready, T * 2 + 1)
                    nc.vector.tensor_copy(prodT[:, 0:4], tr_ps[:, 0].rearrange("p (j n) -> p j n", j=4)).then_inc(pT_done[0], 1)
                    multiply(T, 1)
                    if has_next:
                        turn_x_out(T + 1)

                nc.vector.memset(prod[:, :, 0:1], 0.0).then_inc(prod_done, 2)
                turn_x_out(0)
                tiles_of(dve, tile)
                for g in range(NT):
                    dve.wait_ge(back_in[g], 32)
                    for k in range(2):
                        nc.vector.scalar_tensor_tensor(out=pr.x[:, g], in0=back[:, g, k], scalar=share[k][:, g:g + 1],
                                                       in1=pr.x[:, g], op0=ALU.mult, op1=ALU.add).then_inc(x_done, 1)
                        dve.wait_ge(x_done, 2 * g + k + 1)


def main_program(nc, t, stages=99):
    with ExitStack() as ctx:
        pr = Prog(nc, t)
        pr.x = pr.sb(ctx, "x_tok", [P, NT, D], F32)
        pr.y = pr.sb(ctx, "y_tok", [P, NT, D], F32)
        pr.yT = pr.sb(ctx, "y_T", [P, DT, TOK], F32)
        pr.ident = pr.sb(ctx, "ident", [P, P], F32)
        pr.ident_bf = pr.sb(ctx, "ident_bf", [P, P], BF16)
        pr.ident_r = pr.sb(ctx, "ident_r", [P, P], F32R)
        pr.lower = pr.sb(ctx, "lower", [P, P], F32)
        pr.ones = pr.sb(ctx, "ones", [P, P], F32)
        pr.desc = pr.sb(ctx, "desc", [P, 8], F32)
        pr.place = pr.sb(ctx, "place", [P, CAP], F32)
        attention_layer(pr, 0)
        if stages >= 2:
            moe_capacity(pr)
        if stages >= 3:
            attention_layer(pr, 1)
        if stages >= 4:
            moe_top2(pr)
        x_out = pr.sem("x_out")
        with nc.Block() as block:

            @block.sync
            def _(sp):
                sp.dma_start(t["out"].rearrange("(t p) d -> p t d", p=P), pr.x[:]).then_inc(x_out, 16)
                sp.wait_ge(x_out, 16)


def laid_out(v):
    import numpy as np

    a = {k: np.asarray(x) for k, x in v.items()}
    T = lambda x: np.ascontiguousarray(np.swapaxes(x, -1, -2))
    flag = lambda x: np.ascontiguousarray(x).view(np.uint32)
    t = {
        "x": a["x"].reshape(TOK, D),
        "ctxT": T(a["ctx_1024"].reshape(B * SK, D)),
        "mask": flag(a["mask_1x1xSxS2_bk1"].reshape(SQ, SK)),
        "maskT": flag(T(a["mask_1x1xSxS2_bk1"].reshape(SQ, SK))),
        "amask": a["fside_SxS2_0"],
        "amaskT": T(a["fside_SxS2_0"]),
        "pad": flag(a["mask_BxS2_bf0"]),
        "router": a["L0_ffn_router_w"],
        "w0": a["L0_ffn_w0_kernel"], "w1": a["L0_ffn_w1_kernel"], "w2": a["L0_ffn_wo_kernel"],
        "confT": T(a["L1_ffn_conf_w"]),
        "conf_b": a["L1_ffn_conf_b"], "wealth": a["L1_ffn_wealth"],
        "gateT": T(a["L1_ffn_gate_w"]), "upT": T(a["L1_ffn_up_w"]), "downT": T(a["L1_ffn_down_w"]),
    }
    for l in range(2):
        for n in "qkvo":
            t[f"w{n}T{l}"] = T(a[f"L{l}_xattn_W{n}"])
        for n in "qk":
            t[f"b{n}{l}"] = T(a[f"L{l}_xattn_b{n}"].reshape(DT, P))
        for n in "vo":
            t[f"b{n}{l}"] = a[f"L{l}_xattn_b{n}"]
    return {k: np.ascontiguousarray(x) for k, x in t.items()}


SCRATCH = {
    "k_scr": ([2, 3, D, B * SK], BF16),
    "q_scr": ([2, 3, D, TOK], BF16),
    "v_scr": ([P, B * KT, D], F32),
    "y_scr": ([TOK, D], F32),
    "row_scr": ([TILES * P, D], F32),
    "e_scr": ([E0, NT * CAP, D], F32),
}


def kernel(**inputs):
    import concourse.bacc as bacc
    from concourse.bass_utils import run_bass_kernel_spmd

    nc = bacc.Bacc("TRN2", target_bir_lowering=False, num_devices=1)
    arrays = laid_out(inputs)
    t = {k: nc.dram_tensor(f"in_{k}", a.shape, mybir.dt.from_np(a.dtype), kind="ExternalInput").ap()
         for k, a in arrays.items()}
    t["out"] = nc.dram_tensor("out", [TOK, D], F32, kind="ExternalOutput").ap()
    for k, (shape, dt) in SCRATCH.items():
        t[k] = nc.dram_tensor(k, shape, dt, kind="Internal").ap()
    main_program(nc, t)
    r = run_bass_kernel_spmd(nc, [{f"in_{k}": a for k, a in arrays.items()}], core_ids=[0])
    return r.results[0]["out"].reshape(B, SQ, D)
```

```python
from contextlib import ExitStack, contextmanager

import concourse.bass as bass
from concourse import mybir

F32 = mybir.dt.float32
BF16 = mybir.dt.bfloat16
U8 = mybir.dt.uint8
U32 = mybir.dt.uint32
I32 = mybir.dt.int32
ALU = mybir.AluOpType
ACT = mybir.ActivationFunctionType
AX = mybir.AxisListType

P = 128
B, SQ, SK, D = 2, 512, 1024, 256
NH, DH = 16, 16
TOK = B * SQ
NT = TOK // P
DT = D // P
QT = SQ // P
KT = SK // P
HG = 4
NG = NH // HG
E0, H0, CAP = 8, 1368, 32
E1, I1 = 8, 1024
TILES = 2 * TOK // P + E1 - 1
BIG = float(2.0 ** 100)
EPS = 1e-5
K_PARTS = (0, 1, 0, 2, 0, 1)
Q_PARTS = (0, 0, 1, 0, 2, 1)
STACK = 6 * DH
N_DMA = 12
PADROW = STACK
MROW = STACK + 1
ROWS = STACK + 4
A_SPLIT = (3, 5, 5, 6, 5, 5, 3, 0)
TURN_AT = 5


class Prog:

    def __init__(self, nc, t):
        self.nc, self.t, self.sems = nc, t, []

    def sem(self, name):
        s = self.nc.alloc_semaphore(name=name)
        self.sems.append(s)
        return s

    @contextmanager
    def stage(self):
        outer, self.sems = self.sems, []
        with ExitStack() as inner:
            yield inner
        if self.sems:
            self.nc.clear_and_free_semaphores(self.sems)
            self.nc.all_engine_barrier()
        self.sems = outer

    def sb(self, ctx, name, shape, dt):
        return ctx.enter_context(self.nc.sbuf_tensor(name, shape, dt))

    def banks(self, ctx, name, n):
        return ctx.enter_context(self.nc.psum_tensor(name, [P, n, 512], F32))


class FirstLoads:

    def __init__(self, pr, c):
        self.pr = pr
        self.ctxT = pr.sb(c, "ctxT", [P, DT, B * SK], F32)
        self.wk = pr.sb(c, "wk", [P, 2, DT, D], F32)
        self.wv = pr.sb(c, "wv", [P, 2, DT, D], F32)
        self.bk = pr.sb(c, "bk", [P, 2, DT], F32)
        self.bv = pr.sb(c, "bv", [P, 2, D], F32)
        self.x_in = [pr.sem(f"x_in{i}") for i in range(2)]
        self.w_in = [pr.sem(f"wkv_in{l}") for l in range(2)]
        self.ctx_in = [pr.sem(f"ctx_in{i}") for i in range(4)]
        self.id_zero, self.id_done = pr.sem("id_zero"), pr.sem("id_done")

    def tokens(self, sp):
        for i in range(2):
            half = slice(i * NT // 2, (i + 1) * NT // 2)
            sp.dma_start(self.pr.x[:, half], self.pr.t["x"].rearrange("(t p) d -> p t d", p=P)[:, half]
                         ).then_inc(self.x_in[i], 16)

    def context(self, sp):
        t = self.pr.t
        for l in range(2):
            sp.dma_start(self.wk[:, l], t[f"wkT{l}"].rearrange("(t p) n -> p t n", p=P)).then_inc(self.w_in[l], 16)
            sp.dma_start(self.bk[:, l], t[f"bk{l}"]).then_inc(self.w_in[l], 16)
            if l == 0:
                for i in range(4):
                    cols = slice(i * 512, (i + 1) * 512)
                    sp.dma_start(self.ctxT[:, :, cols],
                                 t["ctxT"][:, cols].rearrange("(t p) n -> p t n", p=P)).then_inc(self.ctx_in[i], 16)
            sp.dma_start(self.wv[:, l], t[f"wvT{l}"].rearrange("(t p) n -> p t n", p=P)).then_inc(self.w_in[l], 16)
            sp.dma_start(self.bv[:, l], t[f"bv{l}"].partition_broadcast(P)).then_inc(self.w_in[l], 16)

    def identities(self, pool):
        pr, nc = self.pr, self.pr.nc
        nc.gpsimd.memset(pr.ident[:], 0.0).then_inc(self.id_zero, 1)
        nc.gpsimd.memset(pr.lower[:], 1.0).then_inc(self.id_zero, 1)
        nc.gpsimd.memset(pr.ones[:], 1.0).then_inc(self.id_zero, 1)
        pool.wait_ge(self.id_zero, 3)
        nc.gpsimd.affine_select(out=pr.ident[:], in_=pr.ident[:], compare_op=ALU.not_equal, fill=1.0,
                                base=0, pattern=[[-1, P]], channel_multiplier=1).then_inc(self.id_done, 1)
        nc.gpsimd.affine_select(out=pr.lower[:], in_=pr.lower[:], compare_op=ALU.is_gt, fill=0.0,
                                base=0, pattern=[[1, P]], channel_multiplier=-1).then_inc(self.id_done, 1)
        pool.wait_ge(self.id_done, 2)
        nc.gpsimd.tensor_copy(pr.ident_bf[:], pr.ident[:]).then_inc(self.id_done, 1)
        for p in range(3):
            blk = slice(32 * p, 32 * p + 32)
            pool.wait_ge(self.id_done, 3 + p)
            nc.gpsimd.tensor_copy(pr.ident3[blk], pr.ident[blk, blk]).then_inc(self.id_done, 1)
        pool.wait_ge(self.id_done, 6)


def passed(eng, step):
    eng.sem_inc(step, 1)


class RowPass:

    def __init__(self, pr, c, l, m, tag):
        self.pr, self.l, self.m = pr, l, m
        self.junk = pr.sb(c, f"junk{tag}", [P, 2, 512], F32)
        self.ps = pr.banks(c, f"s_ps{tag}", 2)
        self.ready, self.done = pr.sem(f"s_ready{tag}"), pr.sem(f"mx_done{tag}")
        self.step = pr.sem(f"row_step{tag}")

    def scores(self, pe, u, i, b, jobs):
        for j in jobs:
            h, half, qt = j // 8, j % 8 // 4, j % 4
            pe.wait_ge(self.done, u * 32 + j + 1)
            pe.matmul(self.ps[:, j % 2], stack(self.pr.Q[b], MROW, i % 2, h, slice(qt * P, (qt + 1) * P)),
                      stack(self.pr.K[b], MROW, i % 2, h, slice(half * 512, (half + 1) * 512)),
                      start=True, stop=True).then_inc(self.ready, 1)

    def maxima(self, dve, u, b, jobs):
        mx = self.m.mx
        for j in jobs:
            h, half, qt = j // 8, j % 8 // 4, j % 4
            dve.wait_ge(self.ready, u * 32 + j + 1)
            first = -4 * BIG
            if half:
                dve.wait_ge(self.done, u * 32 + j + 1 - 4 + 2)
                first = mx[:, b, h, qt, 0:1]
            passed(dve, self.step)
            self.pr.nc.vector.tensor_tensor_reduce(out=self.junk[:, j % 2], in0=self.ps[:, j % 2],
                                                   in1=self.m.bias_rows[:, qt, half * 512:(half + 1) * 512],
                                                   scale=1.0, scalar=first, op0=ALU.add, op1=ALU.max,
                                                   accum_out=mx[:, b, h, qt, half:half + 1]).then_inc(self.done, 1)


def stack(X, rows, k, h, cols):
    return X[0:rows, bass.ds(k, 1), h, cols].rearrange("r o c -> r (o c)")


def context_products(pr, m, f):
    nc, t = pr.nc, pr.t
    with pr.stage() as c:
        ctxT, wk, wv, bk, bv, w_in, ctx_in = f.ctxT, f.wk, f.wv, f.bk, f.bv, f.w_in, f.ctx_in
        full = pr.sb(c, "k_full", [P, 2, 512], F32)
        rest = pr.sb(c, "k_rest", [P, 2, 512], F32)
        parts = pr.sb(c, "k_parts", [P, 3, DT, B * SK], BF16)
        vals1 = pr.sb(c, "vals1", [P, B * KT, D], F32)
        vals = [m.vals, vals1]
        kps = pr.banks(c, "k_ps", 4)
        vps = pr.banks(c, "v_ps", 2)
        row = RowPass(pr, c, 0, m, "_first")
        init, const_done = pr.sem("stack_init"), pr.sem("const_done")
        k_ready, k_full, k_hi = pr.sem("k_ready"), pr.sem("k_full_done"), pr.sem("k_hi_done")
        k_rest, k_mid, k_lo = pr.sem("k_rest_done"), pr.sem("k_mid_done"), pr.sem("k_lo_done")
        v_ready, v_done, v_out = (pr.sem(x) for x in ("v_ready", "v_done", "v_out"))
        k_out = [pr.sem(f"k_out{u}") for u in range(2 * DT)]
        CH = B * SK // 512
        NK = DT * CH
        NV = B * KT

        def tile_of(n):
            l, r = divmod(n, NK)
            return l, r // CH, r % CH

        with nc.Block() as block:

            @block.sync
            def _(sp):
                def keys_out(u):
                    l, dt = divmod(u, DT)
                    sp.wait_ge(k_hi, CH * (u + 1))
                    sp.wait_ge(k_mid, CH * (u + 1))
                    sp.wait_ge(k_lo, CH * (u + 1))
                    for part in range(3):
                        sp.dma_start(t["k_scr"][l, part, dt * P:(dt + 1) * P, :],
                                     parts[:, part, dt]).then_inc(k_out[u], 16)

                keys_out(0)
                keys_out(1)
                sp.wait_ge(k_out[0], 48)
                for b in range(B):
                    sp.wait_ge(m.q_out[b], 48)
                    k_stack(pr, sp, 0, 0, b)
                    q_stack(pr, sp, 0, 0, b)
                keys_out(2)
                keys_out(3)
                for n in range(0, NV, 4):
                    sp.wait_ge(v_done, NV + n + 4)
                    sp.dma_start(t["v_scr"][:, n:n + 4], vals1[:, n:n + 4]).then_inc(v_out, 16)
                for u in range(2 * DT):
                    sp.wait_ge(k_out[u], 48)
                sp.wait_ge(v_out, 16 * NV // 4)
                for n in range(B, DT * B):
                    sp.wait_ge(m.q_out[n], 48)

            @block.gpsimd
            def _(pool):
                nc.gpsimd.iota(pr.desc[:], pattern=[[-1, 8]], base=8, channel_multiplier=0,
                               allow_small_or_imprecise_dtypes=True).then_inc(const_done, 1)
                nc.gpsimd.iota(pr.place[:], pattern=[[1, CAP]], base=0, channel_multiplier=0,
                               allow_small_or_imprecise_dtypes=True).then_inc(const_done, 1)
                pool.wait_ge(const_done, 2)
                stack_ones(pr, pool, init)
                nc.gpsimd.memset(pr.V[0][:], 1.0)
                nc.gpsimd.memset(pr.V[1][:], 1.0)

            @block.tensor
            def _(pe):
                def keys(l):
                    for r in range(NK):
                        n = l * NK + r
                        _, dt, ch = tile_of(n)
                        if n < CH:
                            pe.wait_ge(ctx_in[ch], 16)
                        if n >= 4:
                            pe.wait_ge(k_hi, n - 3)
                        for k in range(DT):
                            mm = pe.matmul(kps[:, n % 4], wk[:, l, k, dt * P:(dt + 1) * P],
                                           ctxT[:, k, ch * 512:(ch + 1) * 512], start=(k == 0), stop=(k == DT - 1))
                        mm.then_inc(k_ready, 1)

                def values(l):
                    for r in range(NV):
                        n = l * NV + r
                        if n >= 2:
                            pe.wait_ge(v_done, n - 1)
                        for k in range(DT):
                            mm = pe.matmul(vps[:, n % 2, 0:D], ctxT[:, k, r * P:(r + 1) * P],
                                           wv[:, l, k], start=(k == 0), stop=(k == DT - 1))
                        mm.then_inc(v_ready, 1)
                        row.scores(pe, 0, 0, 0, [n])

                pe.wait_ge(w_in[0], 64)
                keys(0)
                pe.wait_ge(w_in[1], 64)
                keys(1)
                pe.wait_ge(pr.load[0][0], 16 * N_DMA)
                pe.wait_ge(init, 3)
                values(0)
                values(1)

            @block.scalar
            def _(act):
                def middle(n):
                    l, dt, ch = tile_of(n)
                    act.wait_ge(k_rest, n + 1)
                    nc.scalar.activation(parts[:, 1, dt, ch * 512:(ch + 1) * 512], rest[:, n % 2],
                                         ACT.Copy).then_inc(k_mid, 1)

                act.wait_ge(w_in[0], 64)
                act.wait_ge(w_in[1], 64)
                for n in range(2 * NK):
                    l, dt, ch = tile_of(n)
                    act.wait_ge(k_ready, n + 1)
                    if n >= 2:
                        act.wait_ge(k_rest, n - 1)
                    nc.scalar.activation(full[:, n % 2], kps[:, n % 4], ACT.Identity,
                                         bias=bk[:, l, dt:dt + 1]).then_inc(k_full, 1)
                    if l == 1 and ch == 0:
                        act.wait_ge(k_out[dt], 48)
                    nc.scalar.activation(parts[:, 0, dt, ch * 512:(ch + 1) * 512], kps[:, n % 4],
                                         ACT.Identity, bias=bk[:, l, dt:dt + 1]).then_inc(k_hi, 1)
                    if n % NK:
                        middle(n - 1)
                    if n % NK == NK - 1:
                        middle(n)

            @block.vector
            def _(dve):
                def low(n):
                    l, dt, ch = tile_of(n)
                    dve.wait_ge(k_mid, n + 1)
                    nc.vector.tensor_tensor(parts[:, 2, dt, ch * 512:(ch + 1) * 512], rest[:, n % 2],
                                            parts[:, 1, dt, ch * 512:(ch + 1) * 512],
                                            ALU.subtract).then_inc(k_lo, 1)

                def keys(l):
                    for r in range(NK):
                        n = l * NK + r
                        _, dt, ch = tile_of(n)
                        dve.wait_ge(k_full, n + 1)
                        dve.wait_ge(k_hi, n + 1)
                        if n >= 2:
                            dve.wait_ge(k_lo, n - 1)
                        nc.vector.tensor_tensor(rest[:, n % 2], full[:, n % 2],
                                                parts[:, 0, dt, ch * 512:(ch + 1) * 512],
                                                ALU.subtract).then_inc(k_rest, 1)
                        if r >= 1:
                            low(n - 1)
                    low(l * NK + NK - 1)

                def values(l):
                    dve.wait_ge(w_in[l], 64)
                    for r in range(NV):
                        n = l * NV + r
                        dve.wait_ge(v_ready, n + 1)
                        nc.vector.tensor_tensor(vals[l][:, r], vps[:, n % 2, 0:D], bv[:, l],
                                                ALU.add).then_inc(v_done, 1)
                        row.maxima(dve, 0, 0, [n])

                nc.vector.memset(m.mx[:], 0.0).then_inc(row.done, 2)
                keys(0)
                keys(1)
                values(0)
                values(1)


class NormSteps:

    def __init__(self, pr, c, tag, first=False):
        self.pr, self.tag, self.first = pr, tag, first
        self.mv = pr.sb(c, f"{tag}_mv", [P, NT, 2], F32)
        self.rstd = pr.sb(c, f"{tag}_rstd", [P, NT], F32)
        self.var = pr.sb(c, f"{tag}_var", [P, NT], F32)
        self.root = pr.sb(c, f"{tag}_root", [P, NT], F32)
        self.s_var, self.s_root = pr.sem(f"{tag}_var_done"), pr.sem(f"{tag}_root_done")
        self.s_stats, self.s_mv, self.s_rstd = (pr.sem(f"{tag}_{x}") for x in ("stats", "mv", "rstd"))
        self.s_y, self.s_tr, self.s_yT = (pr.sem(f"{tag}_{x}") for x in ("y", "tr", "yT"))

    def vector(self, dve):
        nc, pr = self.pr.nc, self.pr
        if self.first:
            for i in range(NT):
                nc.vector.bn_stats(pr.stats[:, i], pr.x[:, i]).then_inc(self.s_stats, 1)
        for i in range(NT):
            if self.first:
                dve.wait_ge(self.s_stats, i + 1)
            nc.vector.bn_aggr(self.mv[:, i], pr.stats[:, i]).then_inc(self.s_mv, 1)
        dve.wait_ge(self.s_root, 1)
        nc.vector.reciprocal(self.rstd[:], self.root[:]).then_inc(self.s_rstd, 1)
        dve.wait_ge(self.s_rstd, 1)
        nc.vector.tensor_tensor(self.root[:], self.rstd[:], self.rstd[:], ALU.mult).then_inc(self.s_rstd, 1)
        dve.wait_ge(self.s_rstd, 2)
        nc.vector.tensor_tensor(self.root[:], self.root[:], self.var[:], ALU.mult).then_inc(self.s_rstd, 1)
        dve.wait_ge(self.s_rstd, 3)
        nc.vector.tensor_scalar(self.root[:], self.root[:], -0.5, 1.5, ALU.mult, ALU.add).then_inc(self.s_rstd, 1)
        dve.wait_ge(self.s_rstd, 4)
        nc.vector.tensor_tensor(self.rstd[:], self.rstd[:], self.root[:], ALU.mult).then_inc(self.s_rstd, 1)
        dve.wait_ge(self.s_rstd, 5)
        for i in range(NT):
            nc.vector.tensor_scalar(pr.y[:, i], pr.x[:, i], self.mv[:, i, 0:1], self.rstd[:, i:i + 1],
                                    ALU.subtract, ALU.mult).then_inc(self.s_y, 1)

    def pool(self, pool):
        pool.wait_ge(self.s_mv, NT)
        self.pr.nc.gpsimd.tensor_scalar(self.var[:], self.mv[:, :, 1], EPS, None, ALU.add).then_inc(self.s_var, 1)

    def tensor(self, pe, ps, use=None):
        for j in range(NT // 2):
            pe.wait_ge(self.s_y, 2 * j + 2)
            if j >= 2:
                pe.wait_ge(self.s_yT, j - 1)
            for i in range(2):
                for k in range(DT):
                    mm = pe.transpose(ps[:, j % 2, (k * 2 + i) * P:(k * 2 + i + 1) * P],
                                      self.pr.y[:, 2 * j + i, k * P:(k + 1) * P], self.pr.ident[:])
            mm.then_inc(self.s_tr, 1)
            if use and j >= 1:
                use(j - 1)
        if use:
            use(NT // 2 - 1)

    def scalar(self, act, ps):
        act.wait_ge(self.s_var, 1)
        self.pr.nc.scalar.activation(self.root[:], self.var[:], ACT.Sqrt).then_inc(self.s_root, 1)
        for j in range(NT // 2):
            act.wait_ge(self.s_tr, j + 1)
            self.pr.nc.scalar.activation(self.pr.yT[:, :, 2 * j * P:2 * (j + 1) * P],
                                         ps[:, j % 2].rearrange("p (k n) -> p k n", k=DT),
                                         ACT.Copy).then_inc(self.s_yT, 1)


def k_stack(pr, sp, l, i, b):
    for r in range(6):
        sp.dma_start(pr.K[b][r * DH:(r + 1) * DH, bass.ds(i % 2, 1)].rearrange("d o h k -> d (o h) k"),
                     pr.t["k_scr"][l, K_PARTS[r], bass.ds(i * (HG * DH), HG * DH), b * SK:(b + 1) * SK]
                     .rearrange("(h d) k -> d h k", h=HG)).then_inc(pr.load[l][b], 16)


def q_stack(pr, sp, l, i, b):
    for r in range(6):
        sp.dma_start(pr.Q[b][r * DH:(r + 1) * DH, bass.ds(i % 2, 1)].rearrange("d o h k -> d (o h) k"),
                     pr.t["q_scr"][l, Q_PARTS[r], bass.ds(i * (HG * DH), HG * DH), b * SQ:(b + 1) * SQ]
                     .rearrange("(h d) k -> d h k", h=HG)).then_inc(pr.load[l][b], 16)


def stack_ones(pr, pool, done):
    n = 0
    for b in range(B):
        for X, rows, value in ((pr.K, slice(STACK, ROWS), 1.0), (pr.Q, slice(STACK, ROWS), 1.0),
                               (pr.K, slice(PADROW, PADROW + 1), 0.0)):
            n += 1
            pr.nc.gpsimd.memset(X[b][rows], value).then_inc(done, 1)
            pool.wait_ge(done, n)


def queries_out(pr, sp, l, m, dt, b):
    cols = slice(b * SQ, (b + 1) * SQ)
    for part in range(3):
        sp.dma_start(pr.t["q_scr"][l, part, dt * P:(dt + 1) * P, cols],
                     m.q_parts[:, part, dt, cols]).then_inc(m.q_out[dt * B + b], 16)


def prepare_attention(pr, l, m, first=None):
    nc, t = pr.nc, pr.t
    with pr.stage() as c:
        norm = NormSteps(pr, c, f"an{l}", first=(l == 0))
        wq = pr.sb(c, f"wq{l}", [P, DT, D], F32)
        bq = pr.sb(c, f"bq{l}", [P, DT], F32)
        bq4 = pr.sb(c, f"bq4{l}", [P, DT], F32)
        full = pr.sb(c, f"q_full{l}", [P, 2, 512], F32)
        rest = pr.sb(c, f"q_rest{l}", [P, 2, 512], F32)
        parts = m.q_parts
        tps = pr.banks(c, f"tr_ps{l}", 2)
        qps = pr.banks(c, f"q_ps{l}", 4)
        if l == 0:
            mrow = pr.sb(c, "mask_rows", [P, QT, SK // 4], U32)
            mcol = pr.sb(c, "mask_cols", [P, KT, SQ // 4], U32)
        else:
            padin = pr.sb(c, "pad_in", [1, B * SK // 4], U32)
            padbf = pr.sb(c, "pad_bf", [1, B, SK], BF16)
        w_in, m_in = pr.sem(f"wq_in{l}"), pr.sem(f"m_in{l}")
        b4, q_ready, q_full, q_hi = (pr.sem(f"{x}{l}") for x in ("bq4_", "q_ready", "q_full_", "q_hi"))
        q_rest, q_mid, q_lo, s_pad = (pr.sem(f"{x}{l}") for x in ("q_rest_", "q_mid", "q_lo", "s_pad"))
        CH = TOK // 512
        NQ = DT * CH

        with nc.Block() as block:

            @block.sync
            def _(sp):
                if l == 0:
                    first.tokens(sp)
                sp.dma_start(wq[:], t[f"wqT{l}"].rearrange("(t p) n -> p t n", p=P)).then_inc(w_in, 16)
                sp.dma_start(bq[:], t[f"bq{l}"]).then_inc(w_in, 16)
                if l == 1:
                    sp.dma_start(padin[:], t["pad"].rearrange("b k -> (b k)").unsqueeze(0)).then_inc(m_in, 16)
                if l == 0:
                    sp.dma_start(mrow[:], t["mask"].rearrange("(t p) k -> p t k", p=P)).then_inc(m_in, 16)
                    sp.dma_start(mcol[:], t["maskT"].rearrange("(t p) k -> p t k", p=P)).then_inc(m_in, 16)
                    first.context(sp)
                else:
                    sp.dma_start(m.bias_rows[:], t["amask"].rearrange("(t p) k -> p t k", p=P)).then_inc(m.rows_in, 16)
                    sp.wait_ge(s_pad, 1)
                    for b in range(B):
                        sp.dma_start(pr.K[b][PADROW:PADROW + 1].rearrange("p s h k -> p (s h) k"),
                                     padbf[:, b].unsqueeze(1).broadcast_to([1, 2 * HG, SK])).then_inc(m.pad_in, 16)
                for n in range(NQ if l == 0 else 1):
                    sp.wait_ge(q_hi, n + 1)
                    sp.wait_ge(q_mid, n + 1)
                    sp.wait_ge(q_lo, n + 1)
                    queries_out(pr, sp, l, m, *divmod(n, B))
                if l == 1:
                    sp.wait_ge(m.q_out[0], 48)
                    q_stack(pr, sp, l, 0, 0)

            @block.gpsimd
            def _(pool):
                if l == 0:
                    first.identities(pool)
                norm.pool(pool)
                if l == 1:
                    pool.wait_ge(m_in, 16)
                    nc.gpsimd.tensor_scalar(padbf[:].rearrange("p b k -> p (b k)"), padin[:].bitcast(U8), -BIG, None,
                                            ALU.mult).then_inc(s_pad, 1)
                    pool.wait_ge(s_pad, 1)

            @block.tensor
            def _(pe):
                if l == 0:
                    pe.wait_ge(first.id_done, 2)
                norm.tensor(pe, tps)
                pe.wait_ge(w_in, 32)
                for n in range(NQ):
                    dt, ch = divmod(n, CH)
                    pe.wait_ge(norm.s_yT, NT // 4 * (ch + 1))
                    for k in range(DT):
                        mm = pe.matmul(qps[:, n % 4], wq[:, k, dt * P:(dt + 1) * P],
                                       pr.yT[:, k, ch * 512:(ch + 1) * 512], start=(k == 0), stop=(k == DT - 1))
                    mm.then_inc(q_ready, 1)

            @block.scalar
            def _(act):
                def middle(n):
                    dt, ch = divmod(n, CH)
                    act.wait_ge(q_rest, n + 1)
                    nc.scalar.activation(parts[:, 1, dt, ch * 512:(ch + 1) * 512], rest[:, n % 2],
                                         ACT.Copy).then_inc(q_mid, 1)

                norm.scalar(act, tps)
                act.wait_ge(w_in, 32)
                nc.scalar.activation(bq4[:], bq[:], ACT.Copy, scale=0.25).then_inc(b4, 1)
                act.wait_ge(b4, 1)
                for n in range(NQ):
                    dt, ch = divmod(n, CH)
                    act.wait_ge(q_ready, n + 1)
                    if n >= 2:
                        act.wait_ge(q_rest, n - 1)
                    nc.scalar.activation(full[:, n % 2], qps[:, n % 4], ACT.Identity, bias=bq4[:, dt:dt + 1],
                                         scale=0.25).then_inc(q_full, 1)
                    nc.scalar.activation(parts[:, 0, dt, ch * 512:(ch + 1) * 512], qps[:, n % 4], ACT.Identity,
                                         bias=bq4[:, dt:dt + 1], scale=0.25).then_inc(q_hi, 1)
                    if n >= 1:
                        middle(n - 1)
                middle(NQ - 1)
                if l == 0:
                    act.wait_ge(m_in, 32)
                    nc.scalar.activation(m.bias_hi[:], mcol[:].bitcast(U8), ACT.Copy, scale=-BIG)

            @block.vector
            def _(dve):
                def low(n):
                    dt, ch = divmod(n, CH)
                    dve.wait_ge(q_mid, n + 1)
                    nc.vector.tensor_tensor(parts[:, 2, dt, ch * 512:(ch + 1) * 512], rest[:, n % 2],
                                            parts[:, 1, dt, ch * 512:(ch + 1) * 512], ALU.subtract).then_inc(q_lo, 1)

                if l == 0:
                    dve.wait_ge(first.x_in[0], 16)
                    dve.wait_ge(first.x_in[1], 16)
                norm.vector(dve)
                for n in range(NQ):
                    dt, ch = divmod(n, CH)
                    dve.wait_ge(q_full, n + 1)
                    dve.wait_ge(q_hi, n + 1)
                    if n >= 2:
                        dve.wait_ge(q_lo, n - 1)
                    nc.vector.tensor_tensor(rest[:, n % 2], full[:, n % 2],
                                            parts[:, 0, dt, ch * 512:(ch + 1) * 512], ALU.subtract).then_inc(q_rest, 1)
                    if n >= 1:
                        low(n - 1)
                low(NQ - 1)
                if l == 0:
                    dve.wait_ge(m_in, 32)
                    nc.vector.tensor_scalar(m.bias_rows[:], mrow[:].bitcast(U8), -BIG, None, ALU.mult)


class Mem:
    pass


def attend(pr, l, m):
    nc, t = pr.nc, pr.t
    with pr.stage() as c:
        K, Q, V, load = pr.K, pr.Q, pr.V, pr.load[l]
        prob = pr.sb(c, f"prob{l}", [P, 2, HG, SQ], F32)
        mx = m.mx
        mneg = pr.sb(c, f"mneg{l}", [P, 2, 2 * QT], F32)
        mrest = pr.sb(c, f"mrest{l}", [P, 2, 2 * QT], F32)
        mpart = pr.sb(c, f"mpart{l}", [P, 2, 2 * QT, 4], BF16)
        row = RowPass(pr, c, l, m, l)
        st_ps = pr.banks(c, f"st_ps{l}", 4)
        o_ps = pr.banks(c, f"o_ps{l}", 1)
        m_ps = c.enter_context(nc.psum_tensor(f"m_ps{l}", [P, 1024], BF16))
        init, x_bias = pr.sem(f"mpart_init{l}"), pr.sem(f"x_bias{l}")
        chain, mp_done, mt_done, mrow_done = (pr.sem(f"{x}{l}") for x in ("chain", "mp_done", "mt_done", "mrow_done"))
        st_ready, exp_done, pv_done = (pr.sem(f"{x}{l}") for x in ("st_ready", "exp_done", "pv_done"))
        pool_step, sp_step = (pr.sem(f"{x}_step{l}") for x in ("pool", "sp"))
        evac_done, v_copied = (pr.sem(f"{x}{l}") for x in ("evac_done", "v_copied"))
        if l == 0:
            cols = pr.sb(c, "mask1_cols", [P, KT, SQ], F32)
            cparts = pr.sb(c, "mask1_parts", [P, 3, KT, SQ], BF16)
            cols_in, cut_step, cut_done, cut_out = (pr.sem(x) for x in ("cols_in", "cut_step", "cut_done", "cut_out"))

        def units(eng, unit):
            with eng.Fori(0, NG - 1) as i:
                for b in range(B):
                    unit(i, b, True)
            for b in range(B):
                unit(NG - 1, b, b == 0)

        def nxt(i, b):
            return i * 2 + b + 1, 1 - b

        def a_jobs(kt):
            first = sum(A_SPLIT[:kt])
            return range(first, first + A_SPLIT[kt])

        with nc.Block() as block:

            @block.sync
            def _(sp):
                if l == 1:
                    sp.dma_start(m.vals[:], t["v_scr"]).then_inc(m.vals_in, 16)
                    for n in range(1, DT * B):
                        queries_out(pr, sp, l, m, *divmod(n, B))
                    sp.wait_ge(m.q_out[1], 48)
                    q_stack(pr, sp, l, 0, 1)
                    for part in range(3):
                        sp.dma_start(m.bias3[32 * part:32 * part + 32], t["mask_scr"][part]
                                     .rearrange("(j r) k q -> r j (k q)", r=32)).then_inc(m.bias3_in, 16)
                sp.dma_start(m.wo[:], t[f"woT{l}"].rearrange("(t p) n -> p t n", p=P)).then_inc(m.wo_in, 16)
                sp.dma_start(m.bo[:], t[f"bo{l}"].partition_broadcast(P)).then_inc(m.wo_in, 16)

                def stacks(i, b):
                    sp.wait_ge(load[b], i * (16 * N_DMA))
                    passed(sp, sp_step)
                    k_stack(pr, sp, l, i, b)
                    q_stack(pr, sp, l, i, b)

                for b in range(B):
                    stacks(1, b)
                if l == 0:
                    sp.dma_start(cols[:], t["amaskT"].rearrange("(t p) k -> p t k", p=P)).then_inc(cols_in, 16)
                if l == 1:
                    sp.wait_ge(m.q_out[2], 48)
                    sp.wait_ge(m.q_out[3], 48)
                with sp.Fori(2, NG) as i:
                    for b in range(B):
                        sp.wait_ge(st_ready, (i * 2 + b - 3) * 16)
                        passed(sp, sp_step)
                        stacks(i, b)
                if l == 0:
                    sp.wait_ge(cut_done, KT)
                    for part in range(3):
                        sp.dma_start(t["mask_scr"][part], cparts[:, part]).then_inc(cut_out, 16)
                    sp.wait_ge(cut_out, 48)

            @block.gpsimd
            def _(pool):
                nc.gpsimd.memset(mpart[:], 1.0).then_inc(init, 1)

                def values(u, i, b):
                    pool.wait_ge(evac_done, u + 1)
                    passed(pool, pool_step)
                    nc.gpsimd.tensor_copy(V[b][:, :, :, 0:DH],
                                          m.vals[:, b * KT:(b + 1) * KT, bass.ds(i * (HG * DH), HG * DH)]
                                          .rearrange("p k (h d) -> p k h d", h=HG)).then_inc(v_copied, 1)

                def half(u, b, c2):
                    hs = slice(2 * c2, 2 * c2 + 2)
                    n = (u * 2 + c2) * 4
                    pool.wait_ge(row.done, u * 32 + 2 + 16 * (c2 + 1))
                    pool.wait_ge(mrow_done, u * 2 + c2 + 1)
                    passed(pool, pool_step)
                    nc.gpsimd.tensor_scalar(mneg[:, c2].rearrange("p (h q) -> p h q", h=2), mx[:, b, hs, :, 1],
                                            -BIG / 2, -1.0, ALU.max, ALU.mult).then_inc(chain, 1)
                    pool.wait_ge(chain, n + 1)
                    passed(pool, pool_step)
                    nc.gpsimd.tensor_copy(mpart[:, c2, :, 1], mneg[:, c2]).then_inc(chain, 1)
                    pool.wait_ge(chain, n + 2)
                    passed(pool, pool_step)
                    nc.gpsimd.tensor_tensor(mrest[:, c2], mneg[:, c2], mpart[:, c2, :, 1], ALU.subtract).then_inc(chain, 1)
                    pool.wait_ge(chain, n + 3)
                    passed(pool, pool_step)
                    nc.gpsimd.tensor_copy(mpart[:, c2, :, 2], mrest[:, c2]).then_inc(chain, 1)
                    pool.wait_ge(chain, n + 4)
                    passed(pool, pool_step)
                    nc.gpsimd.tensor_tensor(mpart[:, c2, :, 3], mrest[:, c2], mpart[:, c2, :, 2],
                                            ALU.subtract).then_inc(mp_done, 1)

                def cut_mask(kt):
                    x = cols[:, bass.ds(kt, 1)].rearrange("p o q -> p (o q)")
                    part = [cparts[:, k, bass.ds(kt, 1)].rearrange("p o q -> p (o q)") for k in range(3)]
                    nc.gpsimd.tensor_copy(part[0], x).then_inc(cut_step, 1)
                    pool.wait_ge(cut_step, kt * 3 + 1)
                    passed(pool, pool_step)
                    nc.gpsimd.tensor_tensor(x, x, part[0], ALU.subtract).then_inc(cut_step, 1)
                    pool.wait_ge(cut_step, kt * 3 + 2)
                    passed(pool, pool_step)
                    nc.gpsimd.tensor_copy(part[1], x).then_inc(cut_step, 1)
                    pool.wait_ge(cut_step, kt * 3 + 3)
                    passed(pool, pool_step)
                    nc.gpsimd.tensor_tensor(part[2], x, part[1], ALU.subtract).then_inc(cut_done, 1)

                if l == 1:
                    pool.wait_ge(m.vals_in, 16)
                    values(0, 0, 0)
                pool.wait_ge(init, 1)
                half(0, 0, 0)
                half(0, 0, 1)
                if l == 0:
                    values(0, 0, 0)

                def unit(i, b, has_next):
                    if has_next:
                        u, nb = nxt(i, b)
                        values(u, i + b, nb)
                        half(u, nb, 0)
                        half(u, nb, 1)
                    if l == 0:
                        cut_mask(i * 2 + b)

                if l == 0:
                    pool.wait_ge(cols_in, 16)
                    nc.gpsimd.tensor_scalar(cols[:], cols[:], -BIG, None, ALU.max).then_inc(init, 1)
                    pool.wait_ge(init, 2)
                units(pool, unit)
                pool.wait_ge(m.wo_in, 32)
                nc.gpsimd.tensor_tensor(pr.x[:], pr.x[:], m.bo[:].unsqueeze(1).broadcast_to([P, NT, D]),
                                        ALU.add).then_inc(x_bias, 1)
                pool.wait_ge(x_bias, 1)

            @block.tensor
            def _(pe):
                pe.sem_inc(pv_done, 2)

                def turn_max(u, b, c2):
                    pe.wait_ge(mp_done, u * 2 + c2 + 1)
                    pe.wait_ge(mrow_done, u * 2 + c2 + 2)
                    for k in range(2 * QT):
                        mm = pe.transpose(m_ps[STACK:ROWS, k * P:(k + 1) * P], mpart[:, c2, k], pr.ident_bf[:])
                    mm.then_inc(mt_done, 1)

                def col_scores(u, i, b, kt, hp):
                    n = u * 16 + kt * 2 + hp
                    pe.wait_ge(exp_done, n + 1)
                    for e in range(2):
                        h = 2 * hp + e
                        mm = pe.matmul(st_ps[:, 2 * hp + e], stack(K[b], ROWS, i % 2, h, slice(kt * P, (kt + 1) * P)),
                                       stack(Q[b], ROWS, i % 2, h, slice(0, SQ)),
                                       start=True, stop=False)
                        if l == 0:
                            mm = pe.matmul(st_ps[:, 2 * hp + e], pr.ident_bf[:], m.bias_hi[:, kt], start=False, stop=True)
                        else:
                            for j in range(4):
                                mm = pe.matmul(st_ps[32 * j:32 * j + 32, 2 * hp + e], pr.ident3[:],
                                               m.bias3[:, j, kt], start=False, stop=True)
                    mm.then_inc(st_ready, 1)

                def weigh(u, b, kt):
                    pe.wait_ge(exp_done, u * 16 + 2 * kt + 4)
                    if kt == 0:
                        pe.wait_ge(evac_done, u + 2)
                        pe.wait_ge(v_copied, u + 1)
                    for h in range(HG):
                        mm = pe.matmul(o_ps[32 * h:32 * h + 32, 0], V[b][:, kt, h], prob[:, kt % 2, h],
                                       start=(kt == 0), stop=(kt == KT - 1))
                    mm.then_inc(pv_done, 1)

                pe.wait_ge(load[0], 16 * N_DMA)
                if l == 0:
                    pe.sem_inc(row.ready, 32)
                else:
                    pe.wait_ge(m.pad_in, 16 * B)
                    row.scores(pe, 0, 0, 0, range(32))
                turn_max(0, 0, 0)
                turn_max(0, 0, 1)

                def unit(i, b, has_next):
                    u = i * 2 + b
                    un, nb = nxt(i, b)
                    for kt in range(KT):
                        jobs = list(a_jobs(kt)) if has_next else []
                        if kt == 0 and has_next:
                            pe.wait_ge(load[nb], (i + b) * (16 * N_DMA) + 16 * N_DMA)
                        if kt == 0:
                            pe.wait_ge(mrow_done, u * 2 + 3)
                        col_scores(u, i, b, kt, 0)
                        row.scores(pe, un, i + b, nb, jobs[:2])
                        if kt == 0:
                            pe.wait_ge(mrow_done, u * 2 + 4)
                        col_scores(u, i, b, kt, 1)
                        row.scores(pe, un, i + b, nb, jobs[2:4])
                        if kt >= 1:
                            weigh(u, b, kt - 1)
                        row.scores(pe, un, i + b, nb, jobs[4:])
                        if kt == TURN_AT and has_next:
                            turn_max(un, nb, 0)
                    if has_next:
                        turn_max(un, nb, 1)
                    weigh(u, b, KT - 1)

                if l == 1:
                    pe.wait_ge(m.bias3_in, 48)
                units(pe, unit)

            @block.scalar
            def _(act):
                nc.scalar.activation(prob[:, 0, 0, 0:8], pr.ones[:, 0:8], ACT.Copy).then_inc(exp_done, 2)
                nc.scalar.activation(prob[:, 0, 0, 8:16], pr.ones[:, 0:8], ACT.Copy).then_inc(evac_done, 2)
                nc.scalar.activation(prob[:, 0, 0, 16:24], pr.ones[:, 0:8], ACT.Copy).then_inc(mrow_done, 2)

                def max_row(u, i, b, c2):
                    act.wait_ge(mt_done, u * 2 + c2 + 1)
                    rows = Q[b][STACK:ROWS, bass.ds(i % 2, 1), 2 * c2:2 * c2 + 2]
                    nc.scalar.activation(rows.rearrange("p o h q -> p (o h q)"),
                                         m_ps[STACK:ROWS, :], ACT.Copy).then_inc(mrow_done, 1)

                max_row(0, 0, 0, 0)
                max_row(0, 0, 0, 1)

                def unit(i, b, has_next):
                    u = i * 2 + b
                    un, nb = nxt(i, b)
                    for kt in range(KT):
                        for hp in range(2):
                            if hp == 0:
                                act.wait_ge(pv_done, u * 8 + kt + 1)
                            act.wait_ge(st_ready, u * 16 + kt * 2 + hp + 1)
                            nc.scalar.activation(prob[:, kt % 2, 2 * hp:2 * hp + 2], st_ps[:, 2 * hp:2 * hp + 2],
                                                 ACT.Exp).then_inc(exp_done, 1)
                        if kt == TURN_AT and has_next:
                            max_row(un, i + b, nb, 0)
                    if has_next:
                        max_row(un, i + b, nb, 1)
                    act.wait_ge(pv_done, u * 8 + KT + 2)
                    nc.scalar.activation(m.out[:, bass.ds(i, 1), b], o_ps[:, 0], ACT.Copy).then_inc(evac_done, 1)

                units(act, unit)

            @block.vector
            def _(dve):
                if l == 0:
                    dve.sem_inc(row.done, 2 + 32)
                else:
                    nc.vector.memset(mx[:], 0.0).then_inc(row.done, 2)
                    dve.wait_ge(m.rows_in, 16)
                    row.maxima(dve, 0, 0, range(32))

                def unit(i, b, has_next):
                    u = i * 2 + b
                    un, nb = nxt(i, b)
                    for kt in range(KT):
                        if has_next:
                            row.maxima(dve, un, nb, a_jobs(kt))

                units(dve, unit)


def project(pr, c, l, m):
    nc = pr.nc
    sums = pr.sb(c, f"sums{l}", [P, 2, NH], F32)
    rec = pr.sb(c, f"rec{l}", [P, 2, NH], F32)
    o = pr.sb(c, f"o_tok{l}", [P, 2, D], F32)
    oT = pr.sb(c, f"o_T{l}", [P, 2, DT, P], F32)
    o_ps = pr.banks(c, f"o_tok_ps{l}", 3)
    t_ps = pr.banks(c, f"o_T_ps{l}", 2)
    y_ps = pr.banks(c, f"y_ps{l}", 2)
    o_ready, sum_done, rec_done, o_done = (pr.sem(f"{x}{l}") for x in ("o_ready", "sum_done", "rec_done", "o_done"))
    t_ready, t_done, y_ready, x_done = (pr.sem(f"{x}{l}") for x in ("t_ready", "t_done", "y_ready", "x_done"))

    with nc.Block() as block:

        @block.tensor
        def _(pe):
            def to_tokens(i):
                b, q = divmod(i, QT)
                if i >= 3:
                    pe.wait_ge(o_done, i - 2)
                for g in range(NG):
                    mm = pe.transpose(o_ps[:, i % 3, g * P:(g + 1) * P], m.out[:, g, b, q * P:(q + 1) * P], pr.ident[:])
                mm.then_inc(o_ready, 1)

            def back(i):
                pe.wait_ge(o_done, i + 1)
                if i >= 2:
                    pe.wait_ge(t_done, i - 1)
                for k in range(DT):
                    mm = pe.transpose(t_ps[:, i % 2, k * P:(k + 1) * P], o[:, i % 2, k * P:(k + 1) * P], pr.ident[:])
                mm.then_inc(t_ready, 1)

            def output(i):
                pe.wait_ge(t_done, i + 1)
                if i >= 2:
                    pe.wait_ge(x_done, i - 1)
                for k in range(DT):
                    mm = pe.matmul(y_ps[:, i % 2, 0:D], oT[:, i % 2, k], m.wo[:, k], start=(k == 0), stop=(k == DT - 1))
                mm.then_inc(y_ready, 1)

            to_tokens(0)
            to_tokens(1)
            pe.wait_ge(m.wo_in, 32)
            for i in range(NT):
                if i + 2 < NT:
                    to_tokens(i + 2)
                back(i)
                if i >= 1:
                    output(i - 1)
            output(NT - 1)

        @block.scalar
        def _(act):
            for i in range(NT):
                act.wait_ge(t_ready, i + 1)
                if i >= 2:
                    act.wait_ge(y_ready, i - 1)
                nc.scalar.activation(oT[:, i % 2], t_ps[:, i % 2, 0:D].rearrange("p (k n) -> p k n", k=DT),
                                     ACT.Copy).then_inc(t_done, 1)

        @block.vector
        def _(dve):
            def add(i):
                dve.wait_ge(y_ready, i + 1)
                nc.vector.tensor_tensor(pr.x[:, i], pr.x[:, i], y_ps[:, i % 2, 0:D], ALU.add).then_inc(x_done, 1)
                if i >= 1:
                    statistics(i - 1)

            def statistics(i):
                dve.wait_ge(x_done, i + 1)
                nc.vector.bn_stats(pr.stats[:, i], pr.x[:, i])

            for i in range(NT):
                heads = o_ps[:, i % 3].rearrange("p (h r) -> p h r", h=NH)
                dve.wait_ge(o_ready, i + 1)
                nc.vector.tensor_scalar(sums[:, i % 2], heads[:, :, DH], 1e-30 if l == 0 else 0.0, None,
                                        ALU.max).then_inc(sum_done, 1)
                dve.wait_ge(sum_done, i + 1)
                nc.vector.reciprocal(rec[:, i % 2], sums[:, i % 2]).then_inc(rec_done, 1)
                dve.wait_ge(rec_done, i + 1)
                if i >= 2:
                    dve.wait_ge(t_ready, i - 1)
                nc.vector.tensor_tensor(o[:, i % 2].rearrange("p (h d) -> p h d", h=NH), heads[:, :, 0:DH],
                                        rec[:, i % 2].unsqueeze(2).broadcast_to([P, NH, DH]),
                                        ALU.mult).then_inc(o_done, 1)
                if i >= 2:
                    add(i - 2)
            add(NT - 2)
            add(NT - 1)
            statistics(NT - 1)


def attention_memory(pr, c, l):
    m = Mem()
    m.vals = pr.sb(c, f"vals_all{l}", [P, B * KT, D], F32)
    m.bias_rows = pr.sb(c, f"bias_rows{l}", [P, QT, SK], F32 if l else BF16)
    m.mx = pr.sb(c, f"mx{l}", [P, 2, HG, QT, 2], F32)
    m.q_out = [pr.sem(f"q_out{l}{n}") for n in range(DT * B)]
    if l == 0:
        m.bias_hi = pr.sb(c, "bias_hi", [P, KT, SQ], BF16)
    else:
        m.bias3 = pr.sb(c, "bias3", [3 * 32, 4, KT, SQ], BF16)
    m.wo = pr.sb(c, f"wo{l}", [P, DT, D], F32)
    m.bo = pr.sb(c, f"bo{l}", [P, D], F32)
    m.wo_in = pr.sem(f"wo_in{l}")
    if l == 1:
        m.pad_in, m.vals_in, m.rows_in, m.bias3_in = (pr.sem(x) for x in ("pad_row_in", "vals_in", "rows_in", "bias3_in"))
    return m


def attention_layer(pr, l):
    with pr.stage() as c:
        m = attention_memory(pr, c, l)
        if l == 0:
            with pr.stage() as c0:
                first = FirstLoads(pr, c0)
                m.q_parts = pr.sb(c0, "q_parts0", [P, 3, DT, TOK], BF16)
                prepare_attention(pr, 0, m, first)
                context_products(pr, m, first)
        else:
            m.q_parts = pr.sb(c, "q_parts1", [P, 3, DT, TOK], BF16)
            prepare_attention(pr, 1, m)
        m.out = pr.sb(c, f"o_all{l}", [P, NG, B, SQ], F32)
        attend(pr, l, m)
        project(pr, c, l, m)


def moe_capacity(pr):
    nc, t = pr.nc, pr.t
    HJ = [(j * P, min(P, H0 - j * P)) for j in range((H0 + P - 1) // P)]
    NJ = len(HJ)
    with pr.stage() as c:
        w0 = [pr.sb(c, f"w0_{s}", [P, DT, H0], F32) for s in range(2)]
        w1 = [pr.sb(c, f"w1_{s}", [P, DT, H0], F32) for s in range(2)]
        w2 = [pr.sb(c, f"w2_{s}", [P, NJ, D], F32) for s in range(2)]
        ein = pr.sb(c, "expert_in", [P, DT, E0, NT * CAP], F32)
        combT = pr.sb(c, "comb_T", [P, 2, TOK], F32)
        w_in = [pr.sem(f"w_in{s}") for s in range(2)]

        def load_weights(sp, e, s):
            sp.dma_start(w0[s][:], t["w0"][e].rearrange("(t p) h -> p t h", p=P)).then_inc(w_in[s], 16)
            sp.dma_start(w1[s][:], t["w1"][e].rearrange("(t p) h -> p t h", p=P)).then_inc(w_in[s], 16)
            full = (NJ - 1) * P
            sp.dma_start(w2[s][:, 0:NJ - 1], t["w2"][e, 0:full].rearrange("(j p) m -> p j m", p=P)).then_inc(w_in[s], 16)
            sp.dma_start(w2[s][0:H0 - full, NJ - 1], t["w2"][e, full:H0]).then_inc(w_in[s], 16)

        with pr.stage() as c1:
            norm = NormSteps(pr, c1, "fn0")
            rw = pr.sb(c1, "router", [P, DT, E0], F32)
            g3 = lambda name: pr.sb(c1, name, [P, NT, E0], F32)
            g2 = lambda name: pr.sb(c1, name, [P, NT], F32)
            raw, tmp, only, rest = g3("raw"), g3("gate_tmp"), g3("gate_only"), g3("gate_rest")
            first, second, amount = g3("first"), g3("second"), [g3("amount0"), g3("amount1")]
            top, low, gate, where = g2("top"), g2("low"), [g2("gate0"), g2("gate1")], g2("where")
            spot = [pr.sb(c1, f"spot{k}", [P, NT, CAP], F32) for k in range(2)]
            comb = pr.sb(c1, "comb", [P, NT, E0, CAP], F32)
            disp = pr.sb(c1, "disp", [P, NT, E0, CAP], F32)
            tps = pr.banks(c1, "ftr_ps", 2)
            rps = pr.banks(c1, "router_ps", 3)
            dps = pr.banks(c1, "disp_ps", 2)
            r_in, l_ready, x_sub, x_exp = pr.sem("r_in"), pr.sem("l_ready"), pr.sem("x_sub"), pr.sem("x_exp")
            g_step, m1_done, p1_ready, m1k_done, p2_ready = (
                pr.sem(x) for x in ("g_step", "m1_done", "p1_ready", "m1k_done", "p2_ready"))
            prod_done, comb_done, disp_done, ct_ready, ct_done, d_ready, d_done = (
                pr.sem(x) for x in ("amount_done", "comb_done", "disp_done", "ct_ready", "ct_done", "d_ready", "d_done"))

            with nc.Block() as block:

                @block.sync
                def _(sp):
                    sp.dma_start(rw[:], t["router"].rearrange("(t p) e -> p t e", p=P)).then_inc(r_in, 16)
                    load_weights(sp, 0, 0)
                    load_weights(sp, 1, 1)

                @block.gpsimd
                def _(pool):
                    norm.pool(pool)

                @block.tensor
                def _(pe):
                    def logits(j):
                        pe.wait_ge(r_in, 16)
                        pe.wait_ge(norm.s_yT, j + 1)
                        for g in (2 * j, 2 * j + 1):
                            for k in range(DT):
                                mm = pe.matmul(rps[:, 0, g * E0:(g + 1) * E0], pr.yT[:, k, g * P:(g + 1) * P], rw[:, k],
                                               start=(k == 0), stop=(k == DT - 1))
                        mm.then_inc(l_ready, 1)

                    norm.tensor(pe, tps, logits)
                    pe.wait_ge(m1_done, 1)
                    pe.matmul(rps[:, 1, 0:NT * E0], pr.lower[:], first[:].rearrange("p g e -> p (g e)"),
                              start=True, stop=True).then_inc(p1_ready, 1)
                    pe.wait_ge(m1k_done, 1)
                    pe.matmul(rps[:, 2, 0:NT * E0], pr.lower[:], second[:].rearrange("p g e -> p (g e)"),
                              start=True, stop=False)
                    pe.matmul(rps[:, 2, 0:NT * E0], pr.ones[:], first[:].rearrange("p g e -> p (g e)"),
                              start=False, stop=True).then_inc(p2_ready, 1)
                    for g in range(NT):
                        pe.wait_ge(disp_done, g + 1)
                        if g >= 2:
                            pe.wait_ge(d_done, g - 1)
                        for k in range(DT):
                            mm = pe.matmul(dps[:, g % 2, k * 256:(k + 1) * 256], pr.y[:, g, k * P:(k + 1) * P],
                                           disp[:, g].rearrange("p e c -> p (e c)"), start=True, stop=True)
                        mm.then_inc(d_ready, 1)
                    for j in range(NT // 2):
                        if j >= 2:
                            pe.wait_ge(ct_done, j - 1)
                        for i in range(2):
                            for h in range(2):
                                mm = pe.transpose(tps[:, j % 2, (h * 2 + i) * P:(h * 2 + i + 1) * P],
                                                  comb[:, 2 * j + i, 4 * h:4 * h + 4].rearrange("p e c -> p (e c)"),
                                                  pr.ident[:])
                        mm.then_inc(ct_ready, 1)

                @block.scalar
                def _(act):
                    norm.scalar(act, tps)
                    act.wait_ge(x_sub, 1)
                    nc.scalar.activation(raw[:], raw[:], ACT.Exp).then_inc(x_exp, 1)
                    for g in range(NT):
                        act.wait_ge(d_ready, g + 1)
                        nc.scalar.activation(ein[:, :, :, g * CAP:(g + 1) * CAP],
                                             dps[:, g % 2].rearrange("p (k e c) -> p k e c", k=DT, e=E0),
                                             ACT.Copy).then_inc(d_done, 1)
                    act.wait_ge(d_done, NT)

                @block.vector
                def _(dve):
                    v = nc.vector
                    count = [0]

                    def link(ins):
                        count[0] += 1
                        ins.then_inc(g_step, 1)
                        dve.wait_ge(g_step, count[0])

                    over_e = lambda a: a.unsqueeze(2).broadcast_to([P, NT, E0])
                    order = pr.desc[:].unsqueeze(1).broadcast_to([P, NT, E0])

                    def best(src, one_hot):
                        link(v.tensor_reduce(top[:], src[:], AX.X, ALU.max))
                        link(v.tensor_tensor(tmp[:], src[:], over_e(top[:]), ALU.is_equal))
                        link(v.tensor_tensor(tmp[:], tmp[:], order, ALU.mult))
                        link(v.tensor_reduce(low[:], tmp[:], AX.X, ALU.max))
                        link(v.tensor_tensor(one_hot[:], order, over_e(low[:]), ALU.is_equal))

                    def keep(k, one_hot, counted):
                        link(v.tensor_scalar(tmp[:], counted, float(CAP), None, ALU.is_lt))
                        link(v.tensor_tensor(one_hot[:], one_hot[:], tmp[:], ALU.mult))
                        if k == 0:
                            v.tensor_copy(where[:], top[:]).then_inc(m1k_done, 1)
                        link(v.tensor_tensor(tmp[:], one_hot[:], counted, ALU.mult))
                        link(v.tensor_reduce(where[:], tmp[:], AX.X, ALU.add))
                        link(v.tensor_tensor(amount[k][:], one_hot[:], over_e(gate[k][:]), ALU.mult))
                        link(v.tensor_tensor(spot[k][:], pr.place[:].unsqueeze(1).broadcast_to([P, NT, CAP]),
                                             where[:].unsqueeze(2).broadcast_to([P, NT, CAP]), ALU.is_equal))

                    norm.vector(dve)
                    dve.wait_ge(l_ready, NT // 2)
                    logits = rps[:, 0, 0:NT * E0].rearrange("p (g e) -> p g e", g=NT)
                    link(v.tensor_reduce(top[:], logits, AX.X, ALU.max))
                    v.tensor_tensor(raw[:], logits, over_e(top[:]), ALU.subtract).then_inc(x_sub, 1)
                    dve.wait_ge(x_exp, 1)
                    link(v.tensor_reduce(low[:], raw[:], AX.X, ALU.add))
                    link(v.reciprocal(low[:], low[:]))
                    link(v.tensor_tensor(raw[:], raw[:], over_e(low[:]), ALU.mult))
                    best(raw, first)
                    link(v.tensor_copy(gate[0][:], top[:]))
                    v.tensor_scalar(only[:], first[:], -1.0, 1.0, ALU.mult, ALU.add).then_inc(m1_done, 1)
                    dve.wait_ge(m1_done, 1)
                    link(v.tensor_tensor(rest[:], raw[:], only[:], ALU.mult))
                    best(rest, second)
                    link(v.tensor_copy(gate[1][:], top[:]))
                    dve.wait_ge(p1_ready, 1)
                    keep(0, first, rps[:, 1, 0:NT * E0].rearrange("p (g e) -> p g e", g=NT))
                    dve.wait_ge(p2_ready, 1)
                    keep(1, second, rps[:, 2, 0:NT * E0].rearrange("p (g e) -> p g e", g=NT))
                    for g in range(NT + 2):
                        if g < NT:
                            for k, dst in enumerate((comb, disp)):
                                v.tensor_tensor(dst[:, g], amount[k][:, g].unsqueeze(2).broadcast_to([P, E0, CAP]),
                                                spot[k][:, g].unsqueeze(1).broadcast_to([P, E0, CAP]),
                                                ALU.mult).then_inc(prod_done, 1)
                        if 1 <= g <= NT:
                            dve.wait_ge(prod_done, 2 * g)
                            v.tensor_tensor(comb[:, g - 1], comb[:, g - 1], disp[:, g - 1], ALU.add).then_inc(comb_done, 1)
                        if g >= 2:
                            dve.wait_ge(comb_done, g - 1)
                            v.tensor_scalar(disp[:, g - 2], comb[:, g - 2], 0.0, None, ALU.not_equal).then_inc(disp_done, 1)
                    for j in range(NT // 2):
                        dve.wait_ge(ct_ready, j + 1)
                        v.tensor_copy(combT[:, :, 2 * j * P:2 * (j + 1) * P],
                                      tps[:, j % 2].rearrange("p (h n) -> p h n", h=2)).then_inc(ct_done, 1)
                    dve.wait_ge(ct_done, NT // 2)

        hid = pr.sb(c, "hid", [P, NJ, NT * CAP], F32)
        act_out = pr.sb(c, "gelu_out", [P, 4, NT * CAP], F32)
        eout = pr.sb(c, "expert_out", [P, E0, 2, D], F32)
        ec = [pr.y, pr.yT[:].rearrange("p t n -> p (t n)").rearrange("p (g m) -> p g m", g=NT)]
        h_ps = pr.banks(c, "h_ps", 4)
        e_ps = pr.banks(c, "e_ps", 2)
        y_ps = pr.banks(c, "moe_y_ps", 2)
        h_ready, gelu_done, hid_done, e_ready = (pr.sem(x) for x in ("h_ready", "gelu_done", "hid_done", "e_ready"))
        e_copied, ec_in, y_ready, y_done = (pr.sem(x) for x in ("e_copied", "ec_in", "my_ready", "my_done"))
        e_out = [pr.sem("e_out_first"), pr.sem("e_out_last")]

        with nc.Block() as block:

            @block.sync
            def _(sp):
                def results_out(e):
                    sp.wait_ge(e_copied, e + 3)
                    sp.dma_start(t["e_scr"][e].rearrange("(r p) m -> p r m", p=P),
                                 eout[:, e]).then_inc(e_out[e // (E0 - 1)], 16)

                def results_in(e):
                    sp.dma_start(ec[e // 4][CAP * (e % 4):CAP * (e % 4 + 1)],
                                 t["e_scr"][e].rearrange("(g c) m -> c g m", c=CAP)).then_inc(ec_in, 16)

                for b in range(B):
                    k_stack(pr, sp, 1, 0, b)
                with sp.Fori(1, E0 // 2) as i:
                    for s in range(2):
                        sp.wait_ge(e_ready, i * 2 + s - 1)
                        load_weights(sp, i * 2 + s, s)
                for e in range(E0 - 1):
                    results_out(e)
                sp.wait_ge(e_out[0], 16 * (E0 - 1))
                for e in range(E0 - 1):
                    results_in(e)
                results_out(E0 - 1)
                sp.wait_ge(e_out[1], 16)
                results_in(E0 - 1)

            @block.tensor
            def _(pe):
                with pe.Fori(0, E0 // 2) as i:
                    for s in range(2):
                        e = i * 2 + s
                        pe.wait_ge(w_in[s], i * 64 + 64)
                        for j, (h0, hn) in enumerate(HJ):
                            if j >= 4:
                                pe.wait_ge(hid_done, e * NJ + j - 3)
                            for w, off in ((w0[s], 0), (w1[s], 256)):
                                for k in range(DT):
                                    mm = pe.matmul(h_ps[0:hn, j % 4, off:off + 256], w[:, k, h0:h0 + hn],
                                                   ein[:, k, bass.ds(e, 1)],
                                                   start=(k == 0), stop=(k == DT - 1))
                            mm.then_inc(h_ready, 1)
                        pe.wait_ge(e_copied, e + 1)
                        for r in range(2):
                            for j, (h0, hn) in enumerate(HJ):
                                if r == 0:
                                    pe.wait_ge(hid_done, e * NJ + j + 1)
                                mm = pe.matmul(e_ps[:, s, r * 256:(r + 1) * 256], hid[0:hn, j, r * P:(r + 1) * P],
                                               w2[s][0:hn, j], start=(j == 0), stop=(j == NJ - 1))
                        mm.then_inc(e_ready, 1)
                pe.wait_ge(ec_in, 16 * E0)
                for g in range(NT):
                    if g >= 2:
                        pe.wait_ge(y_done, g - 1)
                    for h in range(2):
                        mm = pe.matmul(y_ps[:, g % 2, 0:D], combT[:, h, g * P:(g + 1) * P], ec[h][:, g],
                                       start=(h == 0), stop=(h == 1))
                    mm.then_inc(y_ready, 1)

            @block.scalar
            def _(act):
                with act.Fori(0, E0 // 2) as i:
                    for s in range(2):
                        e = i * 2 + s
                        for j, (h0, hn) in enumerate(HJ):
                            act.wait_ge(h_ready, e * NJ + j + 1)
                            if j >= 4:
                                act.wait_ge(hid_done, e * NJ + j - 3)
                            nc.scalar.activation(act_out[0:hn, j % 4], h_ps[0:hn, j % 4, 0:256],
                                                 ACT.Gelu_apprx_tanh).then_inc(gelu_done, 1)

            @block.vector
            def _(dve):
                nc.vector.memset(eout[:, :, :, 0:1], 0.0).then_inc(e_copied, 2)
                with dve.Fori(0, E0 // 2) as i:
                    for s in range(2):
                        e = i * 2 + s
                        for j, (h0, hn) in enumerate(HJ):
                            dve.wait_ge(gelu_done, e * NJ + j + 1)
                            nc.vector.tensor_tensor(hid[0:hn, j], act_out[0:hn, j % 4], h_ps[0:hn, j % 4, 256:512],
                                                    ALU.mult).then_inc(hid_done, 1)
                        dve.wait_ge(e_ready, e + 1)
                        nc.vector.tensor_copy(eout[:, bass.ds(e, 1)].rearrange("p o r m -> p (o r m)"),
                                              e_ps[:, s]).then_inc(e_copied, 1)
                for g in range(NT):
                    dve.wait_ge(y_ready, g + 1)
                    nc.vector.tensor_tensor(pr.x[:, g], pr.x[:, g], y_ps[:, g % 2, 0:D], ALU.add).then_inc(y_done, 1)
                    dve.wait_ge(y_done, g + 1)
                    nc.vector.bn_stats(pr.stats[:, g], pr.x[:, g])


def moe_top2(pr):
    nc, t = pr.nc, pr.t
    with pr.stage() as c:
        wg = pr.sb(c, "wg", [P, 2, DT, I1], F32)
        wu = pr.sb(c, "wu", [P, 2, DT, I1], F32)
        wd = pr.sb(c, "wd", [P, 2, I1 // P, D], F32)
        rows = pr.sb(c, "row_token", [P, TILES], U32)
        slots = pr.sb(c, "token_row", [P, 2, NT], U32)
        share = [pr.sb(c, f"share{k}", [P, NT], F32) for k in range(2)]
        table = pr.sb(c, "tile_table", [P, 2 * TILES + E1], I32)
        w_in = [pr.sem(f"w1_in{s}") for s in range(2)]

        def load_weights(sp, e, s):
            sp.dma_start(wg[:, s], t["gateT"][e].rearrange("(t p) i -> p t i", p=P)).then_inc(w_in[s], 16)
            sp.dma_start(wu[:, s], t["upT"][e].rearrange("(t p) i -> p t i", p=P)).then_inc(w_in[s], 16)
            sp.dma_start(wd[:, s], t["downT"][e].rearrange("(t p) d -> p t d", p=P)).then_inc(w_in[s], 16)

        with pr.stage() as c1:
            norm = NormSteps(pr, c1, "fn1")
            cw = pr.sb(c1, "conf_w", [P, DT, E1], F32)
            cb = pr.sb(c1, "conf_b", [P, E1], F32)
            wealth = pr.sb(c1, "wealth", [P, E1], F32)
            g3 = lambda name: pr.sb(c1, name, [P, NT, E1], F32)
            g2 = lambda name: pr.sb(c1, name, [P, NT], F32)
            g1 = lambda name: pr.sb(c1, name, [P, E1], F32)
            bids, tmp, chosen, rank, rest = g3("bids"), g3("bid_tmp"), g3("chosen"), g3("rank"), g3("bid_rest")
            both = lambda name: pr.sb(c1, name, [P, 2, NT, E1], F32)
            one, pick = both("one_hot"), both("pick")
            top, low = [g2("bid0"), g2("bid1")], g2("bid_low")
            k2 = lambda name: pr.sb(c1, name, [P, 2, NT], F32)
            place, full, tile_no, slot_f, spot = (k2(x) for x in ("place_in", "full_tiles", "tile_no", "slot_f", "spot_in"))
            total, run = g3("tile_total"), [g3("run0"), g3("run1")]
            tiles, start = g1("tiles"), g1("start")
            ends = [g1("end0"), g1("end1"), g1("end2")]
            high, low_t = g2("token_high"), g2("token_low")
            steps = pr.sb(c1, "steps", [P, 8], F32)
            big = pr.sb(c1, "compare", [P, TILES, 8], F32)
            line = pr.sb(c1, "line", [P, P], F32)
            expert = pr.sb(c1, "expert_of", [P, TILES], F32)
            odd = pr.sb(c1, "odd", [P, TILES], F32)
            hot_row = pr.sb(c1, "hot_row", [P, 2 * NT, P], BF16)
            hot_tile = pr.sb(c1, "hot_tile", [P, 2 * NT, TILES], F32)
            hot_token = pr.sb(c1, "hot_token", [P, 2 * NT, 2, TILES], BF16)
            tps = pr.banks(c1, "gtr_ps", 2)
            rps = pr.banks(c1, "bid_ps", 3)
            ips = pr.banks(c1, "row_ps", 1)
            c_in, y_out, iota_done, l_ready, z_done, sig_done = (
                pr.sem(x) for x in ("c_in", "y_out", "iota_done", "bl_ready", "z_done", "sig_done"))
            b_step, run_done, c_done, r_ready, diff_done, exp_done, hot_done, i_ready = (
                pr.sem(x) for x in ("b_step", "run_done", "c_done", "r_ready", "diff_done", "bexp_done", "hot_done", "i_ready"))

            with nc.Block() as block:

                @block.sync
                def _(sp):
                    sp.dma_start(cw[:], t["confT"].rearrange("(t p) e -> p t e", p=P)).then_inc(c_in, 16)
                    sp.dma_start(cb[:], t["conf_b"].partition_broadcast(P)).then_inc(c_in, 16)
                    sp.dma_start(wealth[:], t["wealth"].partition_broadcast(P)).then_inc(c_in, 16)
                    load_weights(sp, 0, 0)
                    load_weights(sp, 1, 1)
                    sp.wait_ge(norm.s_y, NT)
                    sp.dma_start(t["y_scr"].rearrange("(t p) d -> p t d", p=P), pr.y[:]).then_inc(y_out, 16)
                    sp.wait_ge(y_out, 16)

                @block.gpsimd
                def _(pool):
                    g = nc.gpsimd
                    loose = dict(allow_small_or_imprecise_dtypes=True)
                    g.iota(steps[:], pattern=[[P, 8]], base=0, channel_multiplier=0, **loose).then_inc(iota_done, 1)
                    g.iota(line[:], pattern=[[1, P]], base=0, channel_multiplier=0, **loose).then_inc(iota_done, 1)
                    g.iota(high[:], pattern=[[1, NT]], base=0, channel_multiplier=0, **loose).then_inc(iota_done, 1)
                    g.iota(low_t[:], pattern=[[0, NT]], base=0, channel_multiplier=1, **loose).then_inc(iota_done, 1)
                    norm.pool(pool)

                @block.tensor
                def _(pe):
                    def logits(j):
                        pe.wait_ge(c_in, 48)
                        pe.wait_ge(norm.s_yT, j + 1)
                        for g in (2 * j, 2 * j + 1):
                            for k in range(DT):
                                mm = pe.matmul(rps[:, 0, g * E1:(g + 1) * E1], pr.yT[:, k, g * P:(g + 1) * P], cw[:, k],
                                               start=(k == 0), stop=(k == DT - 1))
                        mm.then_inc(l_ready, 1)

                    norm.tensor(pe, tps, logits)
                    pe.wait_ge(c_done, 1)
                    flat = chosen[:].rearrange("p g e -> p (g e)")
                    pe.matmul(rps[:, 1, 0:NT * E1], pr.lower[:], flat, start=True, stop=True)
                    pe.matmul(rps[:, 2, 0:NT * E1], pr.ones[:], flat, start=True, stop=True).then_inc(r_ready, 1)
                    for n in range(2 * NT):
                        if n % NT == 0:
                            pe.wait_ge(hot_done, 3 * (n // NT + 1))
                        mm = pe.matmul(ips[:, 0, 0:2 * TILES], hot_row[:, n],
                                       hot_token[:, n].rearrange("p o t -> p (o t)"),
                                       start=(n == 0), stop=(n == 2 * NT - 1))
                    mm.then_inc(i_ready, 1)

                @block.scalar
                def _(act):
                    norm.scalar(act, tps)
                    act.wait_ge(z_done, 1)
                    nc.scalar.activation(bids[:], bids[:], ACT.Sigmoid).then_inc(sig_done, 1)
                    act.wait_ge(diff_done, 1)
                    nc.scalar.activation(low[:], low[:], ACT.Exp).then_inc(exp_done, 1)

                @block.vector
                def _(dve):
                    v = nc.vector
                    n_links = [0]

                    def link(ins):
                        n_links[0] += 1
                        ins.then_inc(b_step, 1)
                        dve.wait_ge(b_step, n_links[0])

                    wide = lambda a: a.unsqueeze(2).broadcast_to([P, NT, E1])
                    by_e = lambda a: a.unsqueeze(1).broadcast_to([P, NT, E1])

                    def best(src, value, one_hot):
                        link(v.tensor_reduce(value[:], src[:], AX.X, ALU.max))
                        link(v.tensor_tensor(tmp[:], src[:], wide(value[:]), ALU.is_equal))
                        link(v.tensor_tensor(tmp[:], tmp[:], by_e(pr.desc[:]), ALU.mult))
                        link(v.tensor_reduce(low[:], tmp[:], AX.X, ALU.max))
                        link(v.tensor_tensor(one_hot, by_e(pr.desc[:]), wide(low[:]), ALU.is_equal))

                    norm.vector(dve)
                    dve.wait_ge(l_ready, NT // 2)
                    v.tensor_tensor(bids[:], rps[:, 0, 0:NT * E1].rearrange("p (g e) -> p g e", g=NT), by_e(cb[:]),
                                    ALU.add).then_inc(z_done, 1)
                    dve.wait_ge(sig_done, 1)
                    link(v.tensor_tensor(bids[:], bids[:], by_e(wealth[:]), ALU.mult))
                    best(bids, top[0], one[:, 0])
                    link(v.tensor_scalar(tmp[:], one[:, 0], -1.0, 1.0, ALU.mult, ALU.add))
                    link(v.tensor_tensor(rest[:], bids[:], tmp[:], ALU.mult))
                    link(v.scalar_tensor_tensor(out=rest[:], in0=one[:, 0], scalar=-BIG, in1=rest[:],
                                                op0=ALU.mult, op1=ALU.add))
                    best(rest, top[1], one[:, 1])
                    v.tensor_tensor(chosen[:], one[:, 0], one[:, 1], ALU.add).then_inc(c_done, 1)
                    v.tensor_tensor(low[:], top[1][:], top[0][:], ALU.subtract).then_inc(diff_done, 1)
                    dve.wait_ge(exp_done, 1)
                    link(v.tensor_scalar(top[0][:], low[:], 1.0, None, ALU.add))
                    link(v.reciprocal(share[0][:], top[0][:]))
                    link(v.tensor_tensor(share[1][:], low[:], share[0][:], ALU.mult))
                    dve.wait_ge(r_ready, 1)
                    flat = lambda bank: rps[:, bank, 0:NT * E1].rearrange("p (g e) -> p g e", g=NT)
                    link(v.tensor_copy(total[:], flat(2)))
                    src = total
                    for i, step in enumerate((1, 2, 4)):
                        dst = run[i % 2]
                        v.tensor_copy(dst[:, 0:step], src[:, 0:step]).then_inc(run_done, 1)
                        v.tensor_tensor(dst[:, step:], src[:, step:], src[:, 0:NT - step], ALU.add).then_inc(run_done, 1)
                        dve.wait_ge(run_done, 2 * i + 2)
                        src = dst
                    count = src[:, NT - 1]
                    link(v.tensor_tensor(rank[:], flat(1), src[:], ALU.add))
                    link(v.tensor_tensor(rank[:], rank[:], total[:], ALU.subtract))
                    dve.wait_ge(iota_done, 4)
                    grid = big[:, 0:E1]
                    link(v.tensor_tensor(grid, count.unsqueeze(2).broadcast_to([P, E1, 8]),
                                         steps[:].unsqueeze(1).broadcast_to([P, E1, 8]), ALU.is_gt))
                    link(v.tensor_reduce(tiles[:], grid, AX.X, ALU.add))
                    link(v.tensor_scalar(tiles[:], tiles[:], 1.0, None, ALU.max))
                    src = tiles
                    for i, step in enumerate((1, 2, 4)):
                        end = ends[i]
                        v.tensor_copy(end[:, 0:step], src[:, 0:step]).then_inc(run_done, 1)
                        v.tensor_tensor(end[:, step:], src[:, step:], src[:, 0:E1 - step], ALU.add).then_inc(run_done, 1)
                        dve.wait_ge(run_done, 2 * i + 8)
                        src = end
                    link(v.tensor_tensor(start[:], end[:], tiles[:], ALU.subtract))
                    link(v.tensor_tensor(big[:, :, 0:7], end[:, 0:7].unsqueeze(1).broadcast_to([P, TILES, 7]),
                                         line[:, 0:TILES].unsqueeze(2).broadcast_to([P, TILES, 7]), ALU.is_le))
                    link(v.tensor_reduce(expert[:], big[:, :, 0:7], AX.X, ALU.add))
                    link(v.tensor_tensor(big[:, :, 0:4], expert[:].unsqueeze(2).broadcast_to([P, TILES, 4]),
                                         line[:, 1:8:2].unsqueeze(1).broadcast_to([P, TILES, 4]), ALU.is_equal))
                    link(v.tensor_reduce(odd[:], big[:, :, 0:4], AX.X, ALU.add))
                    link(v.tensor_copy(table[:, 0:TILES], odd[:]))
                    link(v.tensor_scalar(table[:, TILES:2 * TILES], expert[:], 1.0, None, ALU.add))
                    link(v.tensor_scalar(table[:, 2 * TILES:], end[:], 1.0, None, ALU.add))
                    twice = lambda a: a.unsqueeze(1).broadcast_to([P, 2, NT, E1])
                    link(v.tensor_tensor(pick[:], one[:], twice(rank[:]), ALU.mult))
                    link(v.tensor_reduce(place[:], pick[:], AX.X, ALU.add))
                    link(v.tensor_tensor(pick[:, :, :, 0:7], place[:].unsqueeze(3).broadcast_to([P, 2, NT, 7]),
                                         steps[:, 1:8].unsqueeze(1).unsqueeze(1).broadcast_to([P, 2, NT, 7]), ALU.is_ge))
                    link(v.tensor_reduce(full[:], pick[:, :, :, 0:7], AX.X, ALU.add))
                    link(v.tensor_tensor(pick[:], one[:], start[:].unsqueeze(1).unsqueeze(1).broadcast_to([P, 2, NT, E1]),
                                         ALU.mult))
                    link(v.tensor_reduce(tile_no[:], pick[:], AX.X, ALU.add))
                    link(v.scalar_tensor_tensor(out=slot_f[:], in0=tile_no[:], scalar=float(P), in1=place[:],
                                                op0=ALU.mult, op1=ALU.add))
                    v.tensor_scalar(slots[:], slot_f[:], float(P), None, ALU.add)
                    link(v.tensor_tensor(tile_no[:], tile_no[:], full[:], ALU.add))
                    link(v.scalar_tensor_tensor(out=spot[:], in0=full[:], scalar=-float(P), in1=place[:],
                                                op0=ALU.mult, op1=ALU.add))
                    for k in range(2):
                        mine = slice(k * NT, (k + 1) * NT)
                        link(v.tensor_tensor(hot_tile[:, mine], tile_no[:, k].unsqueeze(2).broadcast_to([P, NT, TILES]),
                                             line[:, 0:TILES].unsqueeze(1).broadcast_to([P, NT, TILES]), ALU.is_equal))
                        for o, x in enumerate((high, low_t)):
                            v.tensor_tensor(hot_token[:, mine, o], hot_tile[:, mine],
                                            x[:].unsqueeze(2).broadcast_to([P, NT, TILES]), ALU.mult).then_inc(hot_done, 1)
                        v.tensor_tensor(hot_row[:, mine], spot[:, k].unsqueeze(2).broadcast_to([P, NT, P]),
                                        line[:].unsqueeze(1).broadcast_to([P, NT, P]), ALU.is_equal).then_inc(hot_done, 1)
                    dve.wait_ge(i_ready, 1)
                    link(v.tensor_copy(odd[:], ips[:, 0, TILES:2 * TILES]))
                    link(v.scalar_tensor_tensor(out=rows[:], in0=ips[:, 0, 0:TILES], scalar=float(P), in1=odd[:],
                                                op0=ALU.mult, op1=ALU.add))

        now = pr.sb(c, "rows_now", [P, 2], U32)
        xg = pr.sb(c, "xg", [P, 2, D], F32)
        xgT = pr.sb(c, "xg_T", [P, DT, P], F32)
        silu = pr.sb(c, "silu", [P, 2, 512], F32)
        prod = pr.sb(c, "silu_up", [P, 2, 512], F32)
        prodT = pr.sb(c, "silu_up_T", [P, 8, P], F32)
        y_all = pr.sb(c, "y_all", [P, TILES + 1, D], F32)
        back = pr.sb(c, "y_back", [P, NT, 2, D], F32)
        gu_ps = pr.banks(c, "gu_ps", 4)
        tr_ps = pr.banks(c, "pt_ps", 2)
        xt_ps = pr.banks(c, "xt_ps", 1)
        y_ps = pr.banks(c, "y2_ps", 1)
        xg_in = [pr.sem(f"xg_in{s}") for s in range(2)]
        ready, pool_step, now_done, xt_ready, xT_done = (
            pr.sem(x) for x in ("weights_ready", "pool_step", "now_done", "xt_ready", "xT_done"))
        g_ready, u_ready, silu_done, prod_done, tr_ready = (
            pr.sem(x) for x in ("g_ready", "u_ready", "silu_done", "prod_done", "tr_ready"))
        pT_done = [pr.sem("pT_done0"), pr.sem("pT_done1")]
        y_ready, y_copied, y_sent, x_done = (pr.sem(x) for x in ("y2_ready", "y2_copied", "y2_sent", "x2_done"))
        x_out, back_in = pr.sem("x_out"), [pr.sem(f"back_in{g}") for g in range(NT)]

        def tiles_of(eng, tile):
            with eng.Fori(0, TILES // 2) as i:
                for s in range(2):
                    tile(i * 2 + s, i, s, True)
            tile(TILES - 1, TILES // 2, 0, False)

        with nc.Block() as block:

            @block.sync
            def _(sp):
                def arrived(n, s):
                    sp.wait_ge(w_in[s], n * 48 + 48)
                    sp.sem_inc(ready, 1)

                arrived(0, 0)
                arrived(0, 1)
                with sp.Fori(1, E1 // 2) as i:
                    for s in range(2):
                        last = sp.value_load(table[0:1, bass.ds(i * 2 + s - 2 + 2 * TILES, 1)], min_val=1, max_val=TILES + 1)
                        sp.wait_ge(y_ready, last)
                        load_weights(sp, i * 2 + s, s)
                        arrived(i, s)
                for g in range(NT):
                    sp.wait_ge(x_done, 2 * g + 2)
                    sp.dma_start(t["out"][g * P:(g + 1) * P], pr.x[:, g]).then_inc(x_out, 16)
                sp.wait_ge(x_out, 16 * NT)

            @block.gpsimd
            def _(pool):
                def fetch(T, s):
                    pool.wait_ge(xt_ready, T + 1)
                    pool.sem_inc(pool_step, 1)
                    nc.gpsimd.tensor_copy(now[:, s:s + 1], rows[:, bass.ds(T, 1)]).then_inc(now_done, 1)
                    pool.wait_ge(now_done, T + 1)
                    pool.sem_inc(pool_step, 1)
                    pool.indirect_dma_start(out=xg[:, s], out_offset=None, in_=t["y_scr"],
                                            in_offset=bass.IndirectOffsetOnAxis(ap=now[:, s:s + 1], axis=0),
                                            bounds_check=TOK - 1).then_inc(xg_in[s], 16)

                tiles_of(pool, lambda T, i, s, has_next: fetch(T, s))
                pool.wait_ge(y_sent, 16 * (TILES + 1))
                for g in range(NT):
                    for k in range(2):
                        pool.indirect_dma_start(out=back[:, g, k], out_offset=None, in_=t["row_scr"],
                                                in_offset=bass.IndirectOffsetOnAxis(ap=slots[:, k, g:g + 1], axis=0),
                                                bounds_check=(TILES + 1) * P - 1).then_inc(back_in[g], 16)

            @block.tensor
            def _(pe):
                pe.sem_inc(xt_ready, 2)
                pe.sem_inc(y_ready, 1)

                def turn_x(T, i, s):
                    pe.wait_ge(xg_in[s], i * 16 + 16)
                    for k in range(DT):
                        mm = pe.transpose(xt_ps[:, 0, k * P:(k + 1) * P], xg[:, s, k * P:(k + 1) * P], pr.ident[:])
                    mm.then_inc(xt_ready, 1)

                def up(w, slot, bank, h, done):
                    for k in range(DT):
                        mm = pe.matmul(gu_ps[:, bank], xgT[:, k], w[:, bass.ds(slot, 1), k, h * 512:(h + 1) * 512],
                                       start=(k == 0), stop=(k == DT - 1))
                    mm.then_inc(done, 1)

                def turn_prod(T, h):
                    pe.wait_ge(prod_done, T * 2 + h + 3)
                    for j in range(4):
                        mm = pe.transpose(tr_ps[:, h, j * P:(j + 1) * P], prod[:, h, j * P:(j + 1) * P], pr.ident[:])
                    mm.then_inc(tr_ready, 1)

                def down(T, slot, h):
                    pe.wait_ge(pT_done[h], T + 1)
                    if h == 0:
                        pe.wait_ge(y_copied, T + 1)
                    for j in range(4 * h, 4 * h + 4):
                        mm = pe.matmul(y_ps[:, 0, 0:D], prodT[:, j], wd[:, bass.ds(slot, 1), j],
                                       start=(j == 0), stop=(j == 7))
                    if h == 1:
                        mm.then_inc(y_ready, 1)

                slot_reg = [pe.alloc_register(f"weight_slot{s}") for s in range(2)]

                def start(T, s):
                    pe.reg_load(slot_reg[s], table[0:1, bass.ds(T, 1)])
                    need = pe.value_load(table[0:1, bass.ds(T + TILES, 1)], min_val=1, max_val=E1)
                    pe.wait_ge(ready, need)
                    pe.wait_ge(xT_done, T + 1)
                    pe.wait_ge(prod_done, T * 2 + 1)
                    up(wg, slot_of(s), 0, 0, g_ready)

                def slot_of(s):
                    return pe.snap(slot_reg[s], min_val=0, max_val=1)

                def tile(T, i, s, has_next):
                    slot = slot_of(s)
                    up(wu, slot, 1, 0, u_ready)
                    pe.wait_ge(prod_done, T * 2 + 2)
                    up(wg, slot, 2, 1, g_ready)
                    turn_prod(T, 0)
                    up(wu, slot, 3, 1, u_ready)
                    if has_next:
                        turn_x(T + 1, i + s, 1 - s)
                    down(T, slot, 0)
                    turn_prod(T, 1)
                    if has_next:
                        start(T + 1, 1 - s)
                    down(T, slot, 1)

                turn_x(0, 0, 0)
                start(0, 0)
                tiles_of(pe, tile)

            @block.scalar
            def _(act):
                def send(n):
                    act.wait_ge(y_copied, n + 1)
                    act.dma_start(t["row_scr"][bass.ds(n * P, P)], y_all[:, bass.ds(n, 1)]
                                  .rearrange("p o d -> p (o d)")).then_inc(y_sent, 16)

                def tile(T, i, s, has_next):
                    for h in range(2):
                        act.wait_ge(g_ready, T * 2 + h + 1)
                        nc.scalar.activation(silu[:, h], gu_ps[:, 2 * h], ACT.Silu).then_inc(silu_done, 1)
                        if h == 0:
                            send(T)

                tiles_of(act, tile)
                send(TILES)

            @block.vector
            def _(dve):
                def turn_x_out(T):
                    dve.wait_ge(xt_ready, T + 3)
                    nc.vector.tensor_copy(xgT[:], xt_ps[:, 0, 0:D].rearrange("p (k n) -> p k n", k=DT)).then_inc(xT_done, 1)

                def multiply(T, h):
                    dve.wait_ge(silu_done, T * 2 + h + 1)
                    dve.wait_ge(u_ready, T * 2 + h + 1)
                    nc.vector.tensor_tensor(prod[:, h], silu[:, h], gu_ps[:, 2 * h + 1], ALU.mult).then_inc(prod_done, 1)

                def tile(T, i, s, has_next):
                    multiply(T, 0)
                    turn_prod_out(T, 0)
                    multiply(T, 1)
                    if has_next:
                        turn_x_out(T + 1)
                    turn_prod_out(T, 1)
                    dve.wait_ge(y_ready, T + 2)
                    nc.vector.tensor_copy(y_all[:, bass.ds(T + 1, 1)].rearrange("p o d -> p (o d)"),
                                          y_ps[:, 0, 0:D]).then_inc(y_copied, 1)

                def turn_prod_out(T, h):
                    dve.wait_ge(tr_ready, T * 2 + h + 1)
                    nc.vector.tensor_copy(prodT[:, 4 * h:4 * h + 4],
                                          tr_ps[:, h].rearrange("p (j n) -> p j n", j=4)).then_inc(pT_done[h], 1)

                nc.vector.memset(y_all[:, 0], 0.0).then_inc(y_copied, 1)
                nc.vector.memset(prod[:, :, 0:1], 0.0).then_inc(prod_done, 2)
                turn_x_out(0)
                tiles_of(dve, tile)
                for g in range(NT):
                    dve.wait_ge(back_in[g], 32)
                    for k in range(2):
                        nc.vector.scalar_tensor_tensor(out=pr.x[:, g], in0=back[:, g, k], scalar=share[k][:, g:g + 1],
                                                       in1=pr.x[:, g], op0=ALU.mult, op1=ALU.add).then_inc(x_done, 1)
                        dve.wait_ge(x_done, 2 * g + k + 1)


def main_program(nc, t):
    with ExitStack() as ctx:
        pr = Prog(nc, t)
        pr.x = pr.sb(ctx, "x_tok", [P, NT, D], F32)
        pr.y = pr.sb(ctx, "y_tok", [P, NT, D], F32)
        pr.stats = pr.sb(ctx, "x_stats", [P, NT, 6], F32)
        pr.yT = pr.sb(ctx, "y_T", [P, DT, TOK], F32)
        pr.ident = pr.sb(ctx, "ident", [P, P], F32)
        pr.ident_bf = pr.sb(ctx, "ident_bf", [P, P], BF16)
        pr.ident3 = pr.sb(ctx, "ident3", [3 * 32, 32], BF16)
        pr.K = [pr.sb(ctx, f"k_stack{b}", [P, 2, HG, SK], BF16) for b in range(B)]
        pr.Q = [pr.sb(ctx, f"q_stack{b}", [P, 2, HG, SQ], BF16) for b in range(B)]
        pr.load = [[pr.sem(f"kq_in{l}{b}") for b in range(B)] for l in range(2)]
        pr.V = [pr.sb(ctx, f"v_unit{b}", [P, KT, HG, 32], F32) for b in range(B)]
        pr.lower = pr.sb(ctx, "lower", [P, P], F32)
        pr.ones = pr.sb(ctx, "ones", [P, P], F32)
        pr.desc = pr.sb(ctx, "desc", [P, 8], F32)
        pr.place = pr.sb(ctx, "place", [P, CAP], F32)
        attention_layer(pr, 0)
        moe_capacity(pr)
        attention_layer(pr, 1)
        moe_top2(pr)


def laid_out(v):
    import numpy as np

    a = {k: np.asarray(x) for k, x in v.items()}
    T = lambda x: np.ascontiguousarray(np.swapaxes(x, -1, -2))
    flag = lambda x: np.ascontiguousarray(x).view(np.uint32)
    t = {
        "x": a["x"].reshape(TOK, D),
        "ctxT": T(a["ctx_1024"].reshape(B * SK, D)),
        "mask": flag(a["mask_1x1xSxS2_bk1"].reshape(SQ, SK)),
        "maskT": flag(T(a["mask_1x1xSxS2_bk1"].reshape(SQ, SK))),
        "amask": a["fside_SxS2_0"],
        "amaskT": T(a["fside_SxS2_0"]),
        "pad": flag(a["mask_BxS2_bf0"]),
        "router": a["L0_ffn_router_w"],
        "w0": a["L0_ffn_w0_kernel"], "w1": a["L0_ffn_w1_kernel"], "w2": a["L0_ffn_wo_kernel"],
        "confT": T(a["L1_ffn_conf_w"]),
        "conf_b": a["L1_ffn_conf_b"], "wealth": a["L1_ffn_wealth"],
        "gateT": T(a["L1_ffn_gate_w"]), "upT": T(a["L1_ffn_up_w"]), "downT": T(a["L1_ffn_down_w"]),
    }
    for l in range(2):
        for n in "qkvo":
            t[f"w{n}T{l}"] = T(a[f"L{l}_xattn_W{n}"])
        for n in "qk":
            t[f"b{n}{l}"] = T(a[f"L{l}_xattn_b{n}"].reshape(DT, P))
        for n in "vo":
            t[f"b{n}{l}"] = a[f"L{l}_xattn_b{n}"]
    return {k: np.ascontiguousarray(x) for k, x in t.items()}


SCRATCH = {
    "k_scr": ([2, 3, D, B * SK], BF16),
    "q_scr": ([2, 3, D, TOK], BF16),
    "mask_scr": ([3, P, KT, SQ], BF16),
    "v_scr": ([P, B * KT, D], F32),
    "y_scr": ([TOK, D], F32),
    "row_scr": ([(TILES + 1) * P, D], F32),
    "e_scr": ([E0, NT * CAP, D], F32),
}


def kernel(**inputs):
    import concourse.bacc as bacc
    from concourse.bass_utils import run_bass_kernel_spmd

    nc = bacc.Bacc("TRN2", target_bir_lowering=False, num_devices=1)
    arrays = laid_out(inputs)
    t = {k: nc.dram_tensor(f"in_{k}", a.shape, mybir.dt.from_np(a.dtype), kind="ExternalInput").ap()
         for k, a in arrays.items()}
    t["out"] = nc.dram_tensor("out", [TOK, D], F32, kind="ExternalOutput").ap()
    for k, (shape, dt) in SCRATCH.items():
        t[k] = nc.dram_tensor(k, shape, dt, kind="Internal").ap()
    main_program(nc, t)
    r = run_bass_kernel_spmd(nc, [{f"in_{k}": a for k, a in arrays.items()}], core_ids=[0])
    return r.results[0]["out"].reshape(B, SQ, D)
```
